# Optimizing a Trainium2 kernel written in Bass

```python
import numpy as np
import jax
import jax.numpy as jnp

def _softmax(x, axis=-1):
    return jax.nn.softmax(x, axis=axis)

def _gelu(x):
    return jax.nn.gelu(x, approximate=True)

def _silu(x):
    return jax.nn.silu(x)

def _sigmoid(x):
    return jax.nn.sigmoid(x)

def _layernorm(x, axis=-1, eps=1e-05):
    m = jnp.mean(x, axis=axis, keepdims=True)
    v = jnp.var(x, axis=axis, keepdims=True)
    return (x - m) / jnp.sqrt(v + eps)

def _scatter_add(tgt, idx, src, axis=0):
    return tgt.at[idx].add(src)

def _segment_sum(src, seg, n):
    return jax.ops.segment_sum(src, seg, n)
kernel_name = 'mk_decoder_preln_d1_seqx_r4_6464ac'

def setup_inputs(seed: int=0):
    np.random.seed(seed)
    _w = jnp.asarray

    def _rec_inputs():
        import jax
        import jax.numpy as jnp
        _rk = jax.random.key(seed)
        x = -0.0002928 + 1 * jax.random.normal(jax.random.fold_in(_rk, 1), (32, 256, 256), jnp.float32)
        _lenS = 256 - jax.random.randint(jax.random.fold_in(_rk, 7), (32,), 0, max(1, 256 // 4) + 1, jnp.int32)
        _lenS2 = 120 - jax.random.randint(jax.random.fold_in(_rk, 8), (32,), 0, max(1, 120 // 4) + 1, jnp.int32)
        _ctx_1024P = jax.random.normal(jax.random.fold_in(_rk, 11), (32, 16, 256), jnp.float32)
        _ctx_1024c = jax.random.dirichlet(jax.random.fold_in(_rk, 511), 0.3 * jnp.ones((16,), jnp.float32), (32, 120))
        _ctx_1024t = jnp.einsum('bsk,bkd->bsd', _ctx_1024c, _ctx_1024P)
        _ctx_1024t = _ctx_1024t * jax.lax.rsqrt(jnp.mean(jnp.square(_ctx_1024t)) + 1e-12) * 0.953939
        ctx_1024 = -1.39393e-06 + 0.999914 * (_ctx_1024t + 0.3 * jax.random.normal(jax.random.fold_in(_rk, 611), (32, 120, 256), jnp.float32))
        fside_BxSxS2_0 = jax.random.uniform(jax.random.fold_in(_rk, 12), (32, 256, 120), jnp.float32, 0.0, 1)
        _validS = jnp.arange(256)[None, :] < _lenS[:, None]
        _validS2 = jnp.arange(120)[None, :] < _lenS2[:, None]
        _causal = jnp.tril(jnp.ones((256, 256), dtype=bool))
        mask_BxSxS2_ik1 = jnp.where(jnp.broadcast_to(_validS2[:, None, :], (32, 256, 120)), 1, 0).astype(jnp.int32)
        return (x, ctx_1024, fside_BxSxS2_0, mask_BxSxS2_ik1)
    x, ctx_1024, fside_BxSxS2_0, mask_BxSxS2_ik1 = _rec_inputs()

    def _L0_attn_setup():
        import jax, jax.numpy as jnp
        import numpy as np
        B, L, C = (1, 512, 256)
        H, H_KV, D = (16, 4, 64)
        N_REP = H // H_KV
        K_SEL = 64
        H_I, D_I = (4, 64)
        ROPE_BASE = 10000.0
        SCALE = D ** (-0.5)

        def _rope_tables(seq_len, dim, dtype):
            inv_freq = 1.0 / ROPE_BASE ** (jnp.arange(0, dim, 2, dtype=jnp.float32) / dim)
            t = jnp.arange(seq_len, dtype=jnp.float32)
            freqs = jnp.einsum('i,j->ij', t, inv_freq)
            emb = jnp.concatenate([freqs, freqs], axis=-1)
            return (jnp.cos(emb).astype(dtype), jnp.sin(emb).astype(dtype))

        def _rotate_half(x):
            x1, x2 = jnp.split(x, 2, axis=-1)
            return jnp.concatenate([-x2, x1], axis=-1)

        def _apply_rope(x, cos, sin):
            c = cos[None, :, None, :]
            s = sin[None, :, None, :]
            return x * c + _rotate_half(x) * s
        key = jax.random.key(seed)
        ks = jax.random.split(key, 12)

        def xavier(k, shape):
            fan_in, fan_out = (shape[0], shape[1])
            lim = np.sqrt(6.0 / (fan_in + fan_out))
            return jax.random.uniform(k, shape, jnp.float32, -lim, lim)
        return {'hidden_states': jax.random.normal(ks[0], (B, L, C), jnp.float32), 'Wq': xavier(ks[1], (C, H * D)), 'Wk': xavier(ks[2], (C, H_KV * D)), 'Wv': xavier(ks[3], (C, H_KV * D)), 'Wo': xavier(ks[4], (H * D, C)), 'Wvg': xavier(ks[5], (C, H_KV * D)), 'bvg': jnp.full((H_KV * D,), 0.5, jnp.float32), 'Wog': xavier(ks[6], (C, H * D)), 'bog': jnp.full((H * D,), 0.5, jnp.float32), 'Wqi': xavier(ks[7], (C, H_I * D_I)), 'Wki': xavier(ks[8], (C, D_I)), 'Wwi': xavier(ks[9], (C, H_I)), 'bi': jnp.zeros((H_I,), jnp.float32)}
    _L0_attn_all = _L0_attn_setup()
    _L0_attn_in = {k: v for k, v in _L0_attn_all.items() if k in ('Wq', 'Wk', 'Wv', 'Wo', 'Wvg', 'bvg', 'Wog', 'bog', 'Wqi', 'Wki', 'Wwi', 'bi')}
    del _L0_attn_all

    def _L0_xattn_setup():
        import jax, jax.numpy as jnp
        import numpy as np
        NUM_HEADS = 16
        HIDDEN = 256
        B, S = (2, 512)

        def _split_heads(x, H):
            b, s, d = x.shape
            return x.reshape(b, s, H, d // H).transpose(0, 2, 1, 3)
        key = jax.random.key(seed)
        ks = jax.random.split(key, 14)
        D = HIDDEN
        scale = 1.0 / np.sqrt(D)
        inp = {'query': jax.random.normal(ks[0], (B, S, D), jnp.float32), 'key_in': jax.random.normal(ks[1], (B, S, D), jnp.float32), 'value': jax.random.normal(ks[2], (B, S, D), jnp.float32), 'group_prob': jax.random.uniform(ks[3], (B, S, S), jnp.float32), 'mask': jax.random.randint(ks[4], (B, S, S), 0, 2, jnp.int32), 'wq_k': jax.random.normal(ks[5], (D, D), jnp.float32) * scale, 'wq_b': jnp.zeros((D,), jnp.float32), 'wk_k': jax.random.normal(ks[6], (D, D), jnp.float32) * scale, 'wk_b': jnp.zeros((D,), jnp.float32), 'wv_k': jax.random.normal(ks[7], (D, D), jnp.float32) * scale, 'wv_b': jnp.zeros((D,), jnp.float32), 'wo_k': jax.random.normal(ks[8], (D, D), jnp.float32) * scale, 'wo_b': jnp.zeros((D,), jnp.float32)}
        return inp
    _L0_xattn_all = _L0_xattn_setup()
    _L0_xattn_in = {k: v for k, v in _L0_xattn_all.items() if k in ('wq_k', 'wq_b', 'wk_k', 'wk_b', 'wv_k', 'wv_b', 'wo_k', 'wo_b')}
    del _L0_xattn_all

    def _L0_ffn_setup():
        import jax, jax.numpy as jnp
        import numpy as np
        H = 256
        I = 128
        E = 8
        TOPK = 2
        NGROUP = 4
        TOPKG = 2
        SCALE = 1.0
        B, S = (4, 256)

        def _gate(xf, gate_weight, bias):
            T = xf.shape[0]
            logits = xf @ gate_weight.T
            scores = jax.nn.sigmoid(logits)
            scores_for_choice = scores + bias[None, :]
            gsz = E // NGROUP
            grp = scores_for_choice.reshape(T, NGROUP, gsz)
            group_scores = jax.lax.top_k(grp, 2)[0].sum(-1)
            _, group_idx = jax.lax.top_k(group_scores, TOPKG)
            rows = jnp.arange(T)[:, None]
            group_mask = jnp.zeros((T, NGROUP), xf.dtype).at[rows, group_idx].set(1.0)
            score_mask = jnp.broadcast_to(group_mask[:, :, None], (T, NGROUP, gsz)).reshape(T, E)
            tmp_scores = jnp.where(score_mask > 0, scores_for_choice, 0.0)
            _, topk_idx = jax.lax.top_k(tmp_scores, TOPK)
            topk_weight = jnp.take_along_axis(scores, topk_idx, axis=1)
            if TOPK > 1:
                topk_weight = topk_weight / (topk_weight.sum(-1, keepdims=True) + 1e-20)
            topk_weight = topk_weight * SCALE
            return (topk_idx, topk_weight)
        key = jax.random.key(seed)
        k0, k1, k2, k3, k4 = jax.random.split(key, 5)
        return {'hidden_states': jax.random.normal(k0, (B, S, H), jnp.float32), 'gate_weight': jax.random.normal(k1, (E, H), jnp.float32) * (1.0 / np.sqrt(H)), 'e_score_correction_bias': jnp.zeros((E,), jnp.float32), 'gate_proj': jax.random.normal(k2, (E, I, H), jnp.float32) * 0.02, 'up_proj': jax.random.normal(k3, (E, I, H), jnp.float32) * 0.02, 'down_proj': jax.random.normal(k4, (E, H, I), jnp.float32) * 0.02}
    _L0_ffn_all = _L0_ffn_setup()
    _L0_ffn_in = {k: v for k, v in _L0_ffn_all.items() if k in ('gate_weight', 'e_score_correction_bias', 'gate_proj', 'up_proj', 'down_proj')}
    del _L0_ffn_all
    return {'x': x, 'ctx_1024': ctx_1024, 'fside_BxSxS2_0': fside_BxSxS2_0, 'mask_BxSxS2_ik1': mask_BxSxS2_ik1, 'L0_attn_Wq': _L0_attn_in['Wq'], 'L0_attn_Wk': _L0_attn_in['Wk'], 'L0_attn_Wv': _L0_attn_in['Wv'], 'L0_attn_Wo': _L0_attn_in['Wo'], 'L0_attn_Wvg': _L0_attn_in['Wvg'], 'L0_attn_bvg': _L0_attn_in['bvg'], 'L0_attn_Wog': _L0_attn_in['Wog'], 'L0_attn_bog': _L0_attn_in['bog'], 'L0_attn_Wqi': _L0_attn_in['Wqi'], 'L0_attn_Wki': _L0_attn_in['Wki'], 'L0_attn_Wwi': _L0_attn_in['Wwi'], 'L0_attn_bi': _L0_attn_in['bi'], 'L0_xattn_wq_k': _L0_xattn_in['wq_k'], 'L0_xattn_wq_b': _L0_xattn_in['wq_b'], 'L0_xattn_wk_k': _L0_xattn_in['wk_k'], 'L0_xattn_wk_b': _L0_xattn_in['wk_b'], 'L0_xattn_wv_k': _L0_xattn_in['wv_k'], 'L0_xattn_wv_b': _L0_xattn_in['wv_b'], 'L0_xattn_wo_k': _L0_xattn_in['wo_k'], 'L0_xattn_wo_b': _L0_xattn_in['wo_b'], 'L0_ffn_gate_weight': _L0_ffn_in['gate_weight'], 'L0_ffn_e_score_correction_bias': _L0_ffn_in['e_score_correction_bias'], 'L0_ffn_gate_proj': _L0_ffn_in['gate_proj'], 'L0_ffn_up_proj': _L0_ffn_in['up_proj'], 'L0_ffn_down_proj': _L0_ffn_in['down_proj']}

def reference(x, ctx_1024, fside_BxSxS2_0, mask_BxSxS2_ik1, L0_attn_Wq, L0_attn_Wk, L0_attn_Wv, L0_attn_Wo, L0_attn_Wvg, L0_attn_bvg, L0_attn_Wog, L0_attn_bog, L0_attn_Wqi, L0_attn_Wki, L0_attn_Wwi, L0_attn_bi, L0_xattn_wq_k, L0_xattn_wq_b, L0_xattn_wk_k, L0_xattn_wk_b, L0_xattn_wv_k, L0_xattn_wv_b, L0_xattn_wo_k, L0_xattn_wo_b, L0_ffn_gate_weight, L0_ffn_e_score_correction_bias, L0_ffn_gate_proj, L0_ffn_up_proj, L0_ffn_down_proj):
    import jax
    import jax.numpy as jnp

    def _L0_attn_ref(hidden_states, Wq, Wk, Wv, Wo, Wvg, bvg, Wog, bog, Wqi, Wki, Wwi, bi):
        import jax, jax.numpy as jnp
        import numpy as np
        B, L, C = (1, 512, 256)
        H, H_KV, D = (16, 4, 64)
        N_REP = H // H_KV
        K_SEL = 64
        H_I, D_I = (4, 64)
        ROPE_BASE = 10000.0
        SCALE = D ** (-0.5)

        def _rope_tables(seq_len, dim, dtype):
            inv_freq = 1.0 / ROPE_BASE ** (jnp.arange(0, dim, 2, dtype=jnp.float32) / dim)
            t = jnp.arange(seq_len, dtype=jnp.float32)
            freqs = jnp.einsum('i,j->ij', t, inv_freq)
            emb = jnp.concatenate([freqs, freqs], axis=-1)
            return (jnp.cos(emb).astype(dtype), jnp.sin(emb).astype(dtype))

        def _rotate_half(x):
            x1, x2 = jnp.split(x, 2, axis=-1)
            return jnp.concatenate([-x2, x1], axis=-1)

        def _apply_rope(x, cos, sin):
            c = cos[None, :, None, :]
            s = sin[None, :, None, :]
            return x * c + _rotate_half(x) * s
        x = hidden_states
        b, l, c = x.shape
        q = (x @ Wq).reshape(b, l, H, D)
        k = (x @ Wk).reshape(b, l, H_KV, D)
        v = (x @ Wv).reshape(b, l, H_KV, D)
        cos, sin = _rope_tables(l, D, x.dtype)
        q = _apply_rope(q, cos, sin)
        k = _apply_rope(k, cos, sin)
        g2 = jax.nn.sigmoid(x @ Wvg + bvg).reshape(b, l, H_KV, D)
        v = v * g2
        qI = (x @ Wqi).reshape(b, l, H_I, D_I)
        kI = x @ Wki
        wI = jax.nn.sigmoid(x @ Wwi)
        s = jnp.einsum('blhd,bsd->blhs', qI, kI) + bi[None, None, :, None]
        I = jnp.einsum('blh,blhs->bls', wI, jax.nn.sigmoid(s))
        _, idx = jax.lax.top_k(I, K_SEL)
        gather = jax.vmap(lambda arr, ii: arr[ii])
        k_sel = gather(k, idx)
        v_sel = gather(v, idx)
        qg = q.reshape(b, l, H_KV, N_REP, D)
        att = jnp.einsum('blgrd,blkgd->blgrk', qg, k_sel) * SCALE
        p = jax.nn.softmax(att, axis=-1)
        out = jnp.einsum('blgrk,blkgd->blgrd', p, v_sel).reshape(b, l, H * D)
        g1 = jax.nn.sigmoid(x @ Wog + bog)
        out = out * g1
        return out @ Wo

    def _L0_xattn_ref(query, key_in, value, group_prob, mask, wq_k, wq_b, wk_k, wk_b, wv_k, wv_b, wo_k, wo_b):
        import jax, jax.numpy as jnp
        import numpy as np
        NUM_HEADS = 16
        HIDDEN = 256
        B, S = (2, 512)

        def _split_heads(x, H):
            b, s, d = x.shape
            return x.reshape(b, s, H, d // H).transpose(0, 2, 1, 3)
        H = NUM_HEADS
        dh = query.shape[-1] // H
        q = _split_heads(query @ wq_k + wq_b, H)
        k = _split_heads(key_in @ wk_k + wk_b, H)
        v = _split_heads(value @ wv_k + wv_b, H)
        logits = jnp.einsum('bhqd,bhkd->bhqk', q, k) / jnp.sqrt(jnp.asarray(dh, q.dtype))
        neg = (1.0 - mask.astype(q.dtype)) * -1000000000.0
        logits = logits + neg[:, None, :, :]
        attn = jax.nn.softmax(logits, axis=-1)
        attn = attn * group_prob[:, None, :, :]
        out = jnp.einsum('bhqk,bhkd->bhqd', attn, v)
        out = out.transpose(0, 2, 1, 3).reshape(query.shape[0], -1, H * dh)
        return out @ wo_k + wo_b

    def _L0_ffn_ref(hidden_states, gate_weight, e_score_correction_bias, gate_proj, up_proj, down_proj):
        import jax, jax.numpy as jnp
        import numpy as np
        H = 256
        I = 128
        E = 8
        TOPK = 2
        NGROUP = 4
        TOPKG = 2
        SCALE = 1.0
        B, S = (4, 256)

        def _gate(xf, gate_weight, bias):
            T = xf.shape[0]
            logits = xf @ gate_weight.T
            scores = jax.nn.sigmoid(logits)
            scores_for_choice = scores + bias[None, :]
            gsz = E // NGROUP
            grp = scores_for_choice.reshape(T, NGROUP, gsz)
            group_scores = jax.lax.top_k(grp, 2)[0].sum(-1)
            _, group_idx = jax.lax.top_k(group_scores, TOPKG)
            rows = jnp.arange(T)[:, None]
            group_mask = jnp.zeros((T, NGROUP), xf.dtype).at[rows, group_idx].set(1.0)
            score_mask = jnp.broadcast_to(group_mask[:, :, None], (T, NGROUP, gsz)).reshape(T, E)
            tmp_scores = jnp.where(score_mask > 0, scores_for_choice, 0.0)
            _, topk_idx = jax.lax.top_k(tmp_scores, TOPK)
            topk_weight = jnp.take_along_axis(scores, topk_idx, axis=1)
            if TOPK > 1:
                topk_weight = topk_weight / (topk_weight.sum(-1, keepdims=True) + 1e-20)
            topk_weight = topk_weight * SCALE
            return (topk_idx, topk_weight)
        Bv, Sv, Hv = hidden_states.shape
        xf = hidden_states.reshape(-1, Hv).astype(jnp.float32)
        topk_idx, topk_weight = _gate(xf, gate_weight.astype(jnp.float32), e_score_correction_bias.astype(jnp.float32))
        y = jnp.zeros_like(xf)
        for e in range(E):
            combine_w = jnp.where(topk_idx == e, topk_weight, 0.0).sum(-1)
            g = xf @ gate_proj[e].T
            u = xf @ up_proj[e].T
            o = jax.nn.silu(g) * u @ down_proj[e].T
            y = y + combine_w[:, None] * o
        return y.reshape(Bv, Sv, Hv)
    x = x + _L0_attn_ref(_layernorm(x, axis=-1), L0_attn_Wq, L0_attn_Wk, L0_attn_Wv, L0_attn_Wo, L0_attn_Wvg, L0_attn_bvg, L0_attn_Wog, L0_attn_bog, L0_attn_Wqi, L0_attn_Wki, L0_attn_Wwi, L0_attn_bi)
    x = x + _L0_xattn_ref(_layernorm(x, axis=-1), ctx_1024, ctx_1024, fside_BxSxS2_0, mask_BxSxS2_ik1, L0_xattn_wq_k, L0_xattn_wq_b, L0_xattn_wk_k, L0_xattn_wk_b, L0_xattn_wv_k, L0_xattn_wv_b, L0_xattn_wo_k, L0_xattn_wo_b)
    x = x + _L0_ffn_ref(_layernorm(x, axis=-1), L0_ffn_gate_weight, L0_ffn_e_score_correction_bias, L0_ffn_gate_proj, L0_ffn_up_proj, L0_ffn_down_proj)
    return x

_drawn_inputs = setup_inputs


def setup_inputs(seed=0):
    import zlib

    import numpy as np

    out = dict(_drawn_inputs(seed))
    spreads = {'L0_attn_bvg': (0.5, 0.6),
     'L0_attn_bog': (0.5, 0.6),
     'L0_attn_bi': (0.0, 0.8),
     'L0_xattn_wq_b': (0.0, 0.694),
     'L0_xattn_wk_b': (0.0, 0.8),
     'L0_xattn_wv_b': (0.0, 0.1),
     'L0_xattn_wo_b': (0.0, 0.1),
     'L0_ffn_e_score_correction_bias': (0.0, 0.8)}
    factors = {'L0_attn_Wog': 3.138,
     'L0_ffn_gate_weight': 8.0,
     'L0_ffn_gate_proj': 7.031,
     'L0_ffn_up_proj': 6.941,
     'L0_ffn_down_proj': 6.981}
    for name, (base, spread) in spreads.items():
        noise = np.random.default_rng([zlib.crc32(name.encode()), seed]).standard_normal(out[name].shape)
        drawn = base * np.exp(spread * noise) if base else spread * noise
        out[name] = jnp.asarray(drawn.astype(out[name].dtype))
    for name, factor in factors.items():
        out[name] = (out[name] * factor).astype(out[name].dtype)
    return out
```

```python
from contextlib import ExitStack

import numpy as np

import concourse.bass as bass
from concourse import mybir

F = mybir.dt.float32
R = mybir.dt.float32r
I32 = mybir.dt.int32
ALU = mybir.AluOpType
ACT = mybir.ActivationFunctionType

B, L, C = 32, 256, 256
P = 128
T = L // P
CT = C // P
H, G, D = 16, 4, 64
RG = H // G
HI = 4
KSEL = 64
SCALE = D ** -0.5
EPS = 1e-5
MASKED = -1e30
LOWEST = -3.0e38
TAKEN = -64.0
MAGIC = 0x5F3759DF

NIDX = HI * D + D + HI
NPJ = RG * D + 2 * D
ROT = RG * D + D
ST = RG * 2 * D + 3 * D
HT = H * D // P

O_IDX = 0
O_PJ = O_IDX + CT * NIDX
O_VG = O_PJ + CT * G * NPJ
O_OG = O_VG + CT * G * D
O_WO = O_OG + CT * H * D
N_W1 = O_WO + HT * C

K_BVG = 0
K_BI = K_BVG + G * D
K_BOG = K_BI + HI
N_K1 = K_BOG + HT

PRODUCTS = (("h", "h"), ("h", "l"), ("l", "h"))


class Fills:

    def __init__(self, banks, full, free, names):
        self.banks, self.full, self.free = banks, full, free
        self.at = {name: (n % len(banks), n // len(banks)) for n, name in enumerate(names)}

    def bank(self, name):
        return self.banks[self.at[name][0]]

    def wait_free(self, eng, name):
        b, n = self.at[name]
        if n:
            eng.wait_ge(self.free[b], n)

    def wait_full(self, eng, name):
        b, n = self.at[name]
        eng.wait_ge(self.full[b], n + 1)

    def wait_drained(self, eng, name):
        b, n = self.at[name]
        eng.wait_ge(self.free[b], n + 1)

    def filled(self, ins, name):
        ins.then_inc(self.full[self.at[name][0]], 1)

    def drained(self, ins, name):
        ins.then_inc(self.free[self.at[name][0]], 1)


NTK = KSEL // 8
NTA = 4
AHEAD = 2


def self_stages(attend, prepare, fetch):
    units = G * T
    norm = [("a_norm", 1)] if fetch else []
    ahead = []
    if prepare:
        ahead = [[("a_xn",)], [("a_xt",)], [("a_ix", 0), ("a_ix", 1)],
                 [("a_iqx", 0), ("a_iqx", 1), ("a_ikx",)], [("a_si", 0, 0), ("a_si", 0, 1)],
                 [("a_si", 1, 0), ("a_si", 1, 1)]] + [[("a_tk", r)] for r in range(NTA)]
        scores = {4: [("a_sc", 0, 0), ("a_sc", 0, 1)], 5: [("a_sc", 1, 0), ("a_sc", 1, 1)]}
    if not attend:
        return [("a_norm", 0)] + [s for n, slot in enumerate(ahead) for s in slot + scores.get(n, [])] + norm
    if not prepare:
        ahead, scores = [[], [], []], {}

    def logits(u):
        return [("b_s", u, 0), ("b_s", u, 1)]

    def projected(g):
        return [("b_pj", g, 0), ("b_pj", g, 1)]

    def rounded(g):
        return [("b_r", g, 0), ("b_r", g, 1)]

    def values(g):
        return [("b_v", g, 0), ("b_v", g, 1)]

    def stacks(g):
        return [("b_kx", g), ("b_qx", g, 0), ("b_qx", g, 1)]

    late = [("b_tk", r) for r in range(NTA, NTK)]
    out = ahead[0] + [("b_vg",)] + projected(0) + [("b_cp",), ("b_og", 0)] + rounded(0) + late[:2]
    out += ahead[1] + [("b_og", 1), ("b_og", 2), ("b_og", 3)]
    out += late[2:] + [("b_mk",)] + stacks(0) + projected(1) + rounded(1) + logits(0) + [("b_e", 0)]
    out += logits(1) + ahead[2] + [("b_n", 0), ("b_e", 1)] + values(0) + stacks(1) + values(1)
    for u in range(units):
        g = u // T + 2
        if u % T == 1 and g < G:
            out += rounded(g)
        if u + 1 < units:
            out += [("b_n", u + 1)]
        out += [("b_t", u, 0), ("b_t", u, 1)]
        if u + AHEAD < units:
            out += logits(u + AHEAD) + [("b_e", u + AHEAD)]
        out += [("b_l", u, 0), ("b_l", u, 1)]
        if u >= 2:
            out += [("b_h", u - 2)]
        if u >= 1:
            out += [("b_o", u - 1)]
        if u == units - 1:
            out += [("b_o", u)]
        more = u + 3 < len(ahead) and u < units - 1
        if more:
            out += ahead[u + 3]
        if u >= 1:
            out += [("b_g", u - 1)]
        if u % T == 0 and g < G:
            out += projected(g)
        if more:
            out += scores.get(u + 3, [])
        if u % T == 1 and g < G:
            out += stacks(g) + values(g)
        if u == units - 2:
            out += norm
    u = units - 1
    out += [("b_h", u - 1), ("b_g", u), ("b_h", u), ("b_w1a",), ("b_w0",), ("b_w1b",)]
    return out + [s for slot in ahead[u + 3:] for s in slot]


def self_attention(nc, keep, x, x1, w1, k1, rope, ident, batches=B):
    with ExitStack() as ctx:
        def sb(name, shape, dt=F):
            return ctx.enter_context(nc.sbuf_tensor("s_" + name, shape, dt))

        sems = []

        def sem(name):
            sems.append(keep.enter_context(nc.semaphore("s_" + name)))
            return sems[-1]

        wh, wl = sb("wh", [P, N_W1], R), sb("wl", [P, N_W1], R)
        w = {"h": wh, "l": wl}
        cst = sb("cst", [P, N_K1])
        half = sb("half", [P, N_K1])
        cs = sb("cs", [P, T, 2, D])
        idn = sb("idn", [P, P])
        xin = sb("xin", [P, T, C])
        stats, mv = sb("stats", [P, T, 6]), sb("mv", [P, T, 2])
        var, rstd, nt = sb("var", [P, T]), sb("rstd", [P, T]), sb("nt", [P, T])
        xn = sb("xn", [P, T, C])
        xnt = {k: sb("xnt" + k, [P, CT, L], R) for k in "hl"}
        ist = sb("ist", [P, T, ST], R)
        wth, wt1 = sb("wth", [P, T, HI]), sb("wt1", [P, T, HI])
        iqt = sb("iqt", [P, HI, L], R)
        ikt = sb("ikt", [P, 2, L], R)
        sig = sb("sig", [P, 2, 2, L])
        score = sb("score", [P, T, L])
        top8 = sb("top8", [P, T, 8])
        xct = {k: sb("xct" + k, [P, CT, L], R) for k in "hl"}
        mb = sb("mb", [P, T, L])
        vg = sb("vg", [P, T, G * D])
        g1t = sb("g1t", [P, HT, L])
        t1, t2, rs = sb("t1", [P, T, ROT]), sb("t2", [P, T, ROT]), sb("rs", [P, T, ROT])
        st = sb("st", [P, T, ST], R)
        kt = sb("kt", [P, 2, 2, L], R)
        qt = sb("qt", [P, 2, RG, L], R)
        vf = sb("vf", [P, 2, T, D])
        va = {k: sb("va" + k, [P, T, G, 2, D], R) for k in "hl"}
        sm = sb("sm", [P, 2, RG, L])
        mx, nm = sb("mx", [P, 2, RG]), sb("nm", [P, 2, RG])
        pr = sb("pr", [P, 2, RG, L])
        rsum, rinv = sb("rsum", [P, 2, RG]), sb("rinv", [P, 2, RG])
        pt = {k: sb("pt" + k, [P, 2, T, RG * P], R) for k in "hl"}
        on = sb("on", [P, 2, 2, P])
        ot = {k: sb("ot" + k, [P, HT, L], R) for k in "hl"}
        xres = sb("xres", [P, T, C])
        x1b = sb("x1b", [P, T, C])

        psb = [ctx.enter_context(nc.psum_tensor(f"s_ps{i}", [P, 512], F)) for i in range(8)]
        full, free = [sem(f"full{i}") for i in range(8)], [sem(f"free{i}") for i in range(8)]
        s_own = {e: sem("own_" + e) for e in ("dve", "pool")}
        arrive, fetched = sem("arrive"), sem("fetched")
        guess, rstd_ready, xn_ready = sem("guess"), sem("rstd_ready"), sem("xn_ready")
        xnt_hi = sem("xnt_hi")
        ist_hi = sem("ist_hi")
        sig_ready, sig_used = sem("sig_ready"), sem("sig_used")
        wt_ready = sem("wt_ready")
        xct_ready, vg_ready = sem("xct_ready"), sem("vg_ready")
        turned, summed, rounded, stacked = sem("turned"), sem("summed"), sem("rounded"), sem("stacked")
        va_hi, va_ready = sem("va_hi"), sem("va_ready")
        nm_ready, exp_done = sem("nm_ready"), sem("exp_done")
        rinv_ready, pt_hi = sem("rinv_ready"), sem("pt_hi")
        pr_ready = [sem("pr_ready0"), sem("pr_ready1")]
        on_ready, ot_hi, ot_ready = sem("on_ready"), sem("ot_hi"), sem("ot_ready")
        last_add = sem("last_add")
        in_iteration = list(sems)
        go, passed = sem("go"), sem("passed")
        const_in, split = sem("const_in"), sem("split")
        stage_in = [sem("stage_in0"), sem("stage_in1")]
        xin_in, xres_in, stored = sem("xin_in"), sem("xres_in"), sem("stored")
        w_hi = sem("w_hi")
        first, last = in_iteration[0].num, in_iteration[-1].num
        assert last - first == len(in_iteration) - 1

        def fills(attend, prepare, fetch):
            b, a = [], []
            for s in self_stages(attend, prepare, fetch):
                if s[0] in ("a_xt", "a_ix", "a_iqx", "a_ikx", "a_si"):
                    a.append(s)
                elif s[0] in ("b_vg", "b_og", "b_pj", "b_kx", "b_qx", "b_s", "b_t", "b_o", "b_w0",
                              "b_w1a"):
                    b.append(s)
            return (Fills(psb[0:5], full[0:5], free[0:5], b),
                    Fills(psb[5:8], full[5:8], free[5:8], a))

        def iterations(eng, body):
            def meet(n):
                eng.drain().then_inc(arrive, 1)
                eng.wait_ge(go, n)
                eng.sem_inc(passed, 1)
            body(-1, False, True, True)
            meet(1)
            if batches > 2:
                with eng.Fori(0, batches - 2) as b:
                    body(b, True, True, True)
                    meet(b + 2)
            body(batches - 2, True, True, False)
            meet(batches)
            body(batches - 1, True, False, False)
            meet(batches + 1)

        CH = 1024
        stage = [sm[:, :, :, :].rearrange("p a b c -> p (a b c)"),
                 pr[:, :, :, :].rearrange("p a b c -> p (a b c)")]
        chunks = [(o, min(CH, N_W1 - o)) for o in range(0, N_W1, CH)]

        block = ctx.enter_context(nc.Block())

        @block.sync
        def _(sp):
            sp.dma_start(xin[:, :, :], x[0].rearrange("(t p) c -> p t c", p=P)).then_inc(xin_in, 16)
            for n, (o, m) in enumerate(chunks):
                if n >= 2:
                    sp.wait_ge(split, n - 1)
                sp.dma_start(stage[n % 2][:, 0:m], w1[:, o:o + m]).then_inc(stage_in[n % 2], 16)
            sp.dma_start(cst[:, :], k1).then_inc(const_in, 16)
            sp.dma_start(cs[:, :, :, :], rope).then_inc(const_in, 16)
            sp.dma_start(idn[:, :], ident).then_inc(const_in, 16)

            def rows(t, b):
                return t[bass.ds(b, 1)].rearrange("o (t p) c -> p (o t) c", p=P)

            def body(b, attend, prepare, fetch):
                it = b + 1
                if attend:
                    sp.dma_start(xres[:, :, :], rows(x, b)).then_inc(xres_in, 16)
                if prepare and fetch:
                    sp.wait_ge(xn_ready, T)
                    sp.dma_start(xin[:, :, :], rows(x, b + 2)).then_inc(xin_in, 16)
                if prepare and fetch:
                    sp.wait_ge(xin_in, (b + 3) * 16)
                    sp.sem_inc(fetched, 1)
                if attend:
                    sp.wait_ge(xres_in, (b + 1) * 16)
                    sp.wait_ge(stored, (b + PRIME) * 16)
                    sp.sem_inc(last_add, 1)
                    for s in (("b_w0",), ("b_w1a",)):
                        fills(attend, prepare, fetch)[0].wait_drained(sp, s)
                    sp.dma_start(rows(x1, b), x1b[:, :, :]).then_inc(stored, 16)
                sp.wait_ge(arrive, 4)
                sp.sem_clear(range(first, last + 1))
                sp.sem_inc(go, 1)

            PRIME = 1
            sp.sem_inc(stored, 16)
            body(-1, False, True, True)
            if batches > 2:
                with sp.Fori(0, batches - 2) as b:
                    body(b, True, True, True)
            body(batches - 2, True, True, False)
            body(batches - 1, True, False, False)
            sp.wait_ge(stored, (batches + PRIME) * 16)
            sp.wait_ge(passed, 4 * (batches + 1))

        @block.gpsimd
        def _(pool):
            own = [0]

            def link(ins):
                own[0] += 1
                ins.then_inc(s_own["pool"], 1)
                pool.wait_ge(s_own["pool"], own[0])

            pool.wait_ge(const_in, 48)
            def body(b, attend, prepare, fetch):
                own[0] = 0
                fb, fa = fills(attend, prepare, fetch)
                for s in self_stages(attend, prepare, fetch):
                    kind, a = s[0], s[1:]
                    if kind == "a_norm":
                        pool.wait_ge(guess, 1 + (not attend and a[0]))
                        for n in range(3):
                            link(nc.gpsimd.tensor_tensor(nt[:, :], rstd[:, :], rstd[:, :], ALU.mult))
                            link(nc.gpsimd.tensor_tensor(nt[:, :], nt[:, :], var[:, :], ALU.mult))
                            link(nc.gpsimd.tensor_scalar(nt[:, :], nt[:, :], -0.5, 1.5, ALU.mult, ALU.add))
                            i = nc.gpsimd.tensor_tensor(rstd[:, :], rstd[:, :], nt[:, :], ALU.mult)
                            if n < 2:
                                link(i)
                            else:
                                i.then_inc(rstd_ready, 1)
                    elif kind == "a_ix":
                        t, = a
                        pool.wait_ge(ist_hi, t + 1)
                        nc.gpsimd.tensor_scalar(wt1[:, t, :], wth[:, t, :], 1.0, None, ALU.add).then_inc(wt_ready, 1)
                    elif kind == "b_pj":
                        g, t = a
                        n = g * T + t
                        pool.wait_ge(turned, n + 1)
                        if g:
                            pool.wait_ge(stacked, n - 1)
                        nc.gpsimd.tensor_tensor(rs[:, t, :], t1[:, t, :], t2[:, t, :], ALU.add).then_inc(summed, 1)
                    elif kind == "b_r":
                        g, t = a
                        n = g * T + t
                        q = rs[:, t, 0:RG * D].rearrange("p (h d) -> p h d", d=D)
                        qs = st[:, t, 0:RG * 2 * D].rearrange("p (h s d) -> p h s d", s=2, d=D)
                        k, ks = rs[:, t, RG * D:ROT], st[:, t, RG * 2 * D:ST].rearrange("p (s d) -> p s d", d=D)
                        pool.wait_ge(rounded, n + 1)
                        nc.gpsimd.tensor_tensor(qs[:, :, 1, :], q, qs[:, :, 0, :].bitcast(F), ALU.subtract)
                        nc.gpsimd.tensor_tensor(ks[:, 1, :], k, ks[:, 0, :].bitcast(F), ALU.subtract)\
                            .then_inc(stacked, 1)
                    elif kind == "b_v":
                        g, t = a
                        n = g * T + t
                        pool.wait_ge(va_hi, n + 1)
                        nc.gpsimd.tensor_tensor(va["l"][:, t, g, :, :], vf[:, g % 2, t, :].unsqueeze(1).broadcast_to([P, 2, D]),
                                                va["h"][:, t, g, :, :].bitcast(F), ALU.subtract).then_inc(va_ready, 1)
                    elif kind == "b_n":
                        u, = a
                        pool.wait_ge(rinv_ready, u + 1)
                        two = pr[:, u % 2, 2:4, :]
                        nc.gpsimd.tensor_tensor(two, two, rinv[:, u % 2, 2:4].unsqueeze(2).broadcast_to([P, 2, L]),
                                                ALU.mult).then_inc(pr_ready[1], 1)
                    elif kind == "b_h":
                        u, = a
                        g, t = u // T, u % T
                        pool.wait_ge(ot_hi, u + 1)
                        to = [ot[k][:, 2 * g:2 * g + 2, t * P:(t + 1) * P] for k in "hl"]
                        nc.gpsimd.tensor_tensor(to[1], on[:, u % 2, :, :], to[0].bitcast(F), ALU.subtract)\
                            .then_inc(ot_ready, 1)
            iterations(pool, body)

        @block.scalar
        def _(act):
            for n, (o, m) in enumerate(chunks):
                act.wait_ge(stage_in[n % 2], 16 * (n // 2 + 1))
                nc.scalar.activation(wh[:, o:o + m], stage[n % 2][:, 0:m], ACT.Copy).then_inc(w_hi, 1)
            act.wait_ge(const_in, 48)
            act.wait_ge(split, len(chunks) + 1)

            def body(b, attend, prepare, fetch):
                fb, fa = fills(attend, prepare, fetch)
                for s in self_stages(attend, prepare, fetch):
                    kind, a = s[0], s[1:]
                    if kind == "a_xt":
                        fa.wait_full(act, s)
                        if attend:
                            fb.wait_full(act, ("b_pj", 0, 1))
                            act.wait_ge(xct_ready, 2)
                        nc.scalar.activation(xnt["h"][:, :, :], fa.bank(s)[:, :].rearrange("p (c l) -> p c l", l=L),
                                             ACT.Copy).then_inc(xnt_hi, 1)
                    elif kind == "a_ix":
                        t, = a
                        fa.wait_full(act, s)
                        ps = fa.bank(s)
                        hs = ist[:, t, 0:HI * 2 * D].rearrange("p (h s d) -> p h s d", s=2, d=D)
                        ks = ist[:, t, HI * 2 * D:ST].rearrange("p (s d) -> p s d", d=D)
                        nc.scalar.activation(hs[:, :, 0, :], ps[:, 0:HI * D].rearrange("p (h d) -> p h d", d=D), ACT.Copy)
                        nc.scalar.activation(ks[:, 0:3:2, :], ps[:, HI * D:HI * D + D].unsqueeze(1).broadcast_to([P, 2, D]),
                                             ACT.Copy)
                        nc.scalar.activation(wth[:, t, :], ps[:, HI * D + D:NIDX], ACT.Tanh, scale=0.5).then_inc(ist_hi, 1)
                    elif kind == "a_iqx":
                        j, = a
                        fa.wait_full(act, s)
                        fa.drained(nc.scalar.activation(iqt[:, 2 * j:2 * j + 2, :],
                                   fa.bank(s)[:, :].rearrange("p (h l) -> p h l", l=L), ACT.Copy), s)
                    elif kind == "a_ikx":
                        fa.wait_full(act, s)
                        fa.drained(nc.scalar.activation(ikt[:, :, :],
                                   fa.bank(s)[:, :].rearrange("p (h l) -> p h l", l=L), ACT.Copy), s)
                    elif kind == "a_si":
                        t, j = a
                        fa.wait_full(act, s)
                        if t:
                            act.wait_ge(sig_used, j + 1)
                        for i in range(2):
                            h = 2 * j + i
                            ins = nc.scalar.activation(sig[:, j, i, :], fa.bank(s)[:, i * L:(i + 1) * L], ACT.Tanh,
                                                       bias=half[:, K_BI + h:K_BI + h + 1], scale=0.5)
                        fa.drained(ins, s)
                    elif kind == "b_vg":
                        fb.wait_drained(act, s)
                        nc.scalar.activation(vg[:, :, :], vg[:, :, :], ACT.Tanh, scale=0.5).then_inc(vg_ready, 1)
                    elif kind == "b_cp":
                        nc.scalar.activation(xct["h"][:, :, :], xnt["h"][:, :, :].bitcast(F), ACT.Copy)\
                            .then_inc(xct_ready, 1)
                    elif kind == "b_og":
                        j, = a
                        fb.wait_full(act, s)
                        for i in range(2):
                            m = 2 * j + i
                            ins = nc.scalar.activation(g1t[:, m, :], fb.bank(s)[:, i * L:(i + 1) * L], ACT.Tanh,
                                                       bias=half[:, K_BOG + m:K_BOG + m + 1], scale=0.5)
                        fb.drained(ins, s)
                    elif kind == "b_r":
                        g, t = a
                        n = g * T + t
                        act.wait_ge(summed, n + 1)
                        if g:
                            fb.wait_full(act, ("b_qx", g - 1, RG // 2 - 1))
                        q = rs[:, t, 0:RG * D].rearrange("p (h d) -> p h d", d=D)
                        qs = st[:, t, 0:RG * 2 * D].rearrange("p (h s d) -> p h s d", s=2, d=D)
                        k, ks = rs[:, t, RG * D:ROT], st[:, t, RG * 2 * D:ST].rearrange("p (s d) -> p s d", d=D)
                        nc.scalar.activation(qs[:, :, 0, :], q, ACT.Copy)
                        nc.scalar.activation(ks[:, 0:3:2, :], k.unsqueeze(1).broadcast_to([P, 2, D]), ACT.Copy)\
                            .then_inc(rounded, 1)
                    elif kind == "b_v":
                        g, t = a
                        fb.wait_drained(act, ("b_pj", g, t))
                        nc.scalar.activation(va["h"][:, t, g, :, :], vf[:, g % 2, t, :].unsqueeze(1).broadcast_to([P, 2, D]),
                                             ACT.Copy).then_inc(va_hi, 1)
                    elif kind == "b_kx":
                        g, = a
                        fb.wait_full(act, s)
                        fb.drained(nc.scalar.activation(kt[:, g % 2, :, :],
                                   fb.bank(s)[:, :].rearrange("p (h l) -> p h l", l=L), ACT.Copy), s)
                    elif kind == "b_qx":
                        g, j = a
                        fb.wait_full(act, s)
                        fb.drained(nc.scalar.activation(qt[:, g % 2, 2 * j:2 * j + 2, :],
                                   fb.bank(s)[:, :].rearrange("p (h l) -> p h l", l=L), ACT.Copy), s)
                    elif kind == "b_e":
                        u, = a
                        act.wait_ge(nm_ready, u + 1)
                        if u >= 2:
                            fb.wait_full(act, ("b_t", u - 2, 1))
                        for h in range(RG):
                            ins = nc.scalar.activation(pr[:, u % 2, h, :], sm[:, u % 2, h, :], ACT.Exp,
                                                       bias=nm[:, u % 2, h:h + 1], scale=SCALE,
                                                       accum_out=rsum[:, u % 2, h:h + 1])
                        ins.then_inc(exp_done, 1)
                    elif kind == "b_t":
                        u, j = a
                        fb.wait_full(act, s)
                        if u >= 2:
                            fb.wait_full(act, ("b_o", u - 2))
                        nc.scalar.activation(pt["h"][:, u % 2, :, j * 2 * P:(j + 1) * 2 * P],
                                             fb.bank(s)[:, :].rearrange("p (k n) -> p k n", k=T), ACT.Copy)\
                            .then_inc(pt_hi, 1)
                    elif kind == "b_h":
                        u, = a
                        g, t = u // T, u % T
                        act.wait_ge(on_ready, u + 1)
                        fb.wait_drained(act, ("b_o", u))
                        nc.scalar.activation(ot["h"][:, 2 * g:2 * g + 2, t * P:(t + 1) * P], on[:, u % 2, :, :], ACT.Copy)\
                            .then_inc(ot_hi, 1)
            iterations(act, body)

        @block.vector
        def _(dve):
            own = [0]

            def link(ins):
                own[0] += 1
                ins.then_inc(s_own["dve"], 1)
                dve.wait_ge(s_own["dve"], own[0])

            for n, (o, m) in enumerate(chunks):
                dve.wait_ge(w_hi, n + 1)
                nc.vector.tensor_tensor(wl[:, o:o + m], stage[n % 2][:, 0:m], wh[:, o:o + m].bitcast(F),
                                        ALU.subtract).then_inc(split, 1)
            dve.wait_ge(const_in, 48)
            nc.vector.tensor_scalar(half[:, :], cst[:, :], 0.5, None, ALU.mult).then_inc(split, 1)
            dve.wait_ge(xin_in, 16)

            def body(b, attend, prepare, fetch):
                own[0] = 0
                fb, fa = fills(attend, prepare, fetch)
                for s in self_stages(attend, prepare, fetch):
                    kind, a = s[0], s[1:]
                    if kind == "a_norm":
                        if a[0]:
                            dve.wait_ge(fetched, 1)
                        for t in range(T):
                            i = nc.vector.bn_stats(stats[:, t, :], xin[:, t, :])
                        link(i)
                        for t in range(T):
                            i = nc.vector.bn_aggr(mv[:, t, :], stats[:, t, :])
                        link(i)
                        link(nc.vector.tensor_scalar(var[:, :], mv[:, :, 1], EPS, None, ALU.add))
                        link(nc.vector.tensor_scalar(nt[:, :].bitcast(I32), var[:, :].bitcast(I32), 1, None,
                                                     ALU.logical_shift_right))
                        nc.vector.tensor_scalar(rstd[:, :].bitcast(I32), nt[:, :].bitcast(I32), -1.0, float(MAGIC),
                                                ALU.mult, ALU.add).then_inc(guess, 1)
                    elif kind == "a_xn":
                        if not attend:
                            dve.wait_ge(rstd_ready, 1)
                        for t in range(T):
                            nc.vector.tensor_scalar(xn[:, t, :], xin[:, t, :], mv[:, t, 0:1], rstd[:, t:t + 1],
                                                    ALU.subtract, ALU.mult).then_inc(xn_ready, 1)
                    elif kind == "a_xt":
                        dve.wait_ge(xnt_hi, 1)
                        fa.drained(nc.vector.tensor_tensor(xnt["l"][:, :, :],
                                   fa.bank(s)[:, :].rearrange("p (c l) -> p c l", l=L),
                                   xnt["h"][:, :, :].bitcast(F), ALU.subtract), s)
                    elif kind == "a_ix":
                        t, = a
                        dve.wait_ge(ist_hi, t + 1)
                        ps = fa.bank(s)
                        hs = ist[:, t, 0:HI * 2 * D].rearrange("p (h s d) -> p h s d", s=2, d=D)
                        ks = ist[:, t, HI * 2 * D:ST].rearrange("p (s d) -> p s d", d=D)
                        nc.vector.tensor_tensor(hs[:, :, 1, :], ps[:, 0:HI * D].rearrange("p (h d) -> p h d", d=D),
                                                hs[:, :, 0, :].bitcast(F), ALU.subtract)
                        fa.drained(nc.vector.tensor_tensor(ks[:, 1, :], ps[:, HI * D:HI * D + D],
                                                           ks[:, 0, :].bitcast(F), ALU.subtract), s)
                    elif kind == "a_sc":
                        t, j = a
                        if j == 0:
                            dve.wait_ge(wt_ready, t + 1)
                        fa.wait_drained(dve, ("a_si", t, j))
                        for i in range(2):
                            h = 2 * j + i
                            wt = wt1[:, t, h:h + 1]
                            if h == 0:
                                ins = nc.vector.tensor_scalar(score[:, t, :], sig[:, j, i, :], wt, None, ALU.mult)
                            else:
                                ins = nc.vector.scalar_tensor_tensor(score[:, t, :], sig[:, j, i, :], wt,
                                                                     score[:, t, :], ALU.mult, ALU.add)
                            if i == 0:
                                link(ins)
                            else:
                                ins.then_inc(sig_used, 1)
                                dve.wait_ge(sig_used, 2 * t + j + 1)
                    elif kind in ("a_tk", "b_tk"):
                        for t in range(T):
                            nc.vector.max(top8[:, t, :], score[:, t, :]).then_inc(s_own["dve"], 1)
                        for t in range(T):
                            own[0] += 1
                            dve.wait_ge(s_own["dve"], own[0])
                            nc.vector.match_replace(score[:, t, :], top8[:, t, :], score[:, t, :], TAKEN)\
                                .then_inc(s_own["dve"], 1)
                        own[0] += T
                        dve.wait_ge(s_own["dve"], own[0])
                    elif kind == "b_cp":
                        nc.vector.tensor_copy(xct["l"][:, :, :], xnt["l"][:, :, :].bitcast(F)).then_inc(xct_ready, 1)
                    elif kind == "b_mk":
                        link(nc.vector.tensor_scalar(mb[:, :, :], score[:, :, :], TAKEN / 2, MASKED, ALU.is_ge, ALU.mult))
                    elif kind == "b_vg":
                        fb.wait_full(dve, s)
                        ins = nc.vector.tensor_tensor(vg[:, :, :], fb.bank(s)[:, :].rearrange("p (t n) -> p t n", t=T),
                                                      cst[:, K_BVG:K_BVG + G * D].unsqueeze(1).broadcast_to([P, T, G * D]),
                                                      ALU.add)
                        fb.drained(ins, s)
                    elif kind == "b_pj":
                        g, t = a
                        n = g * T + t
                        fb.wait_full(dve, s)
                        if g:
                            dve.wait_ge(summed, n - 1)
                        ps = fb.bank(s)
                        r5 = ps[:, 0:ROT].rearrange("p (h s d) -> p h s d", s=2, d=D // 2)
                        o5 = t2[:, t, :].rearrange("p (h s d) -> p h s d", s=2, d=D // 2)
                        nc.vector.tensor_tensor(t1[:, t, :].rearrange("p (h d) -> p h d", d=D),
                                                ps[:, 0:ROT].rearrange("p (h d) -> p h d", d=D),
                                                cs[:, t, 0, :].unsqueeze(1).broadcast_to([P, RG + 1, D]), ALU.mult)
                        nc.vector.tensor_tensor(o5, r5[:, :, ::-1, :],
                                                cs[:, t, 1, :].rearrange("p (s d) -> p s d", s=2).unsqueeze(1)
                                                .broadcast_to([P, RG + 1, 2, D // 2]), ALU.mult).then_inc(turned, 1)
                        if n == 0:
                            dve.wait_ge(vg_ready, 1)
                        if g >= 2:
                            dve.wait_ge(va_ready, n - 3)
                        fb.drained(nc.vector.scalar_tensor_tensor(vf[:, g % 2, t, :], vg[:, t, g * D:(g + 1) * D], 1.0,
                                                                  ps[:, ROT:NPJ], ALU.add, ALU.mult), s)
                    elif kind == "b_s":
                        u, j = a
                        t = u % T
                        fb.wait_full(dve, s)
                        if u >= 2 and j == 0:
                            dve.wait_ge(exp_done, u - 1)
                        for i in range(2):
                            h = 2 * j + i
                            ins = nc.vector.tensor_tensor_reduce(
                                out=sm[:, u % 2, h, :], in0=fb.bank(s)[:, i * L:(i + 1) * L], in1=mb[:, t, :],
                                scale=1.0, scalar=LOWEST, op0=ALU.add, op1=ALU.max, accum_out=mx[:, u % 2, h:h + 1])
                        fb.drained(ins, s)
                        if j == 1:
                            fb.wait_drained(dve, s)
                            nc.vector.tensor_scalar(nm[:, u % 2, :], mx[:, u % 2, :], -SCALE, None, ALU.mult)\
                                .then_inc(nm_ready, 1)
                    elif kind == "b_n":
                        u, = a
                        dve.wait_ge(exp_done, u + 1)
                        nc.vector.reciprocal(rinv[:, u % 2, :], rsum[:, u % 2, :]).then_inc(rinv_ready, 1)
                        dve.wait_ge(rinv_ready, u + 1)
                        for h in range(2):
                            ins = nc.vector.tensor_scalar(pr[:, u % 2, h, :], pr[:, u % 2, h, :],
                                                          rinv[:, u % 2, h:h + 1], None, ALU.mult)
                        ins.then_inc(pr_ready[0], 1)
                    elif kind == "b_l":
                        u, j = a
                        dve.wait_ge(pt_hi, 2 * u + j + 1)
                        to = [pt[k][:, u % 2, :, j * 2 * P:(j + 1) * 2 * P] for k in "hl"]
                        fb.drained(nc.vector.tensor_tensor(
                            to[1], fb.bank(("b_t", u, j))[:, :].rearrange("p (k n) -> p k n", k=T), to[0].bitcast(F),
                            ALU.subtract), ("b_t", u, j))
                    elif kind == "b_g":
                        u, = a
                        g, t = u // T, u % T
                        if u == 0:
                            for j in range(HT // 2):
                                fb.wait_drained(dve, ("b_og", j))
                        fb.wait_full(dve, ("b_o", u))
                        if u >= 2:
                            dve.wait_ge(ot_ready, u - 1)
                        o = fb.bank(("b_o", u))[:, :].rearrange("p (i v q) -> p i v q", v=2, q=P)
                        for v, part in enumerate((slice(0, D), slice(D, P))):
                            ins = nc.vector.scalar_tensor_tensor(
                                on[part, u % 2, :, :], g1t[part, 2 * g:2 * g + 2, t * P:(t + 1) * P], 1.0,
                                o[part, :, v, :], ALU.add, ALU.mult)
                            if v == 0:
                                ins.then_inc(on_ready, 1)
                        fb.drained(ins, ("b_o", u))
                    elif kind in ("b_w0", "b_w1b"):
                        t = int(kind == "b_w1b")
                        s = ("b_w1a",) if t else s
                        fb.wait_full(dve, s)
                        if t == 0:
                            dve.wait_ge(last_add, 1)
                        fb.drained(nc.vector.scalar_tensor_tensor(x1b[:, t, :], fb.bank(s)[:, 0:C], 0.25, xres[:, t, :],
                                                                  ALU.mult, ALU.add), s)
            iterations(dve, body)

        @block.tensor
        def _(pe):
            pe.wait_ge(split, len(chunks))
            pe.wait_ge(const_in, 48)

            def mm(out, lhs, rhs, start, stop):
                return nc.tensor.matmul(out, lhs, rhs, start=start, stop=stop)

            def project(out, lhs, rhs, tiles, start=True, stop=True):
                pairs = [(c, a, b) for c in (range(tiles) if isinstance(tiles, int) else tiles) for a, b in PRODUCTS]
                for n, (c, a, b) in enumerate(pairs):
                    ins = mm(out, lhs(a, c), rhs(b, c), start and n == 0, stop and n == len(pairs) - 1)
                return ins

            def weight(o, width, at, n):
                return lambda k, c: w[k][:, o + c * width + at:o + c * width + at + n]

            def body(b, attend, prepare, fetch):
                fb, fa = fills(attend, prepare, fetch)
                for s in self_stages(attend, prepare, fetch):
                    kind, a = s[0], s[1:]
                    if kind == "a_xt":
                        pe.wait_ge(xn_ready, T)
                        fa.wait_free(pe, s)
                        for c in range(CT):
                            for t in range(T):
                                o = c * L + t * P
                                ins = nc.tensor.transpose(fa.bank(s)[:, o:o + P], xn[:, t, c * P:(c + 1) * P], idn[:, :])
                        fa.filled(ins, s)
                    elif kind == "a_ix":
                        t, = a
                        fa.wait_drained(pe, ("a_xt",))
                        fa.wait_free(pe, s)
                        fa.filled(project(fa.bank(s)[:, 0:NIDX], lambda k, c: xnt[k][:, c, t * P:(t + 1) * P],
                                          weight(O_IDX, NIDX, 0, NIDX), CT), s)
                    elif kind == "a_iqx":
                        j, = a
                        for t in range(T):
                            fa.wait_drained(pe, ("a_ix", t))
                        fa.wait_free(pe, s)
                        for i in range(2):
                            for t in range(T):
                                o = i * L + t * P
                                h = 2 * j + i
                                ins = nc.tensor.transpose(fa.bank(s)[:, o:o + P],
                                                          ist[:, t, h * P:(h + 1) * P].bitcast(F), idn[:, :])
                        fa.filled(ins, s)
                    elif kind == "a_ikx":
                        fa.wait_free(pe, s)
                        for i in range(2):
                            for t in range(T):
                                o, f = i * L + t * P, HI * 2 * D + i * D
                                ins = nc.tensor.transpose(fa.bank(s)[:, o:o + P], ist[:, t, f:f + P].bitcast(F), idn[:, :])
                        fa.filled(ins, s)
                    elif kind == "a_si":
                        t, j = a
                        fa.wait_drained(pe, ("a_ikx",))
                        fa.wait_drained(pe, ("a_iqx", j))
                        fa.wait_free(pe, s)
                        for i in range(2):
                            for k in range(2):
                                ins = mm(fa.bank(s)[:, i * L:(i + 1) * L], iqt[:, 2 * j + i, t * P:(t + 1) * P],
                                         ikt[:, k, :], k == 0, k == 1)
                        fa.filled(ins, s)
                    elif kind == "b_vg":
                        for t in range(T):
                            ins = project(fb.bank(s)[:, t * L:(t + 1) * L], lambda k, c: xnt[k][:, c, t * P:(t + 1) * P],
                                          weight(O_VG, G * D, 0, G * D), CT)
                        fb.filled(ins, s)
                    elif kind == "b_og":
                        j, = a
                        pe.wait_ge(xct_ready, 2)
                        fb.wait_free(pe, s)
                        for i in range(2):
                            ins = project(fb.bank(s)[:, i * L:(i + 1) * L], weight(O_OG, H * D, (2 * j + i) * P, P),
                                          lambda k, c: xct[k][:, c, :], CT)
                        fb.filled(ins, s)
                    elif kind == "b_pj":
                        g, t = a
                        src = xct if g else xnt
                        if g:
                            pe.wait_ge(xct_ready, 2)
                        fb.wait_free(pe, s)
                        fb.filled(project(fb.bank(s)[:, 0:NPJ], lambda k, c: src[k][:, c, t * P:(t + 1) * P],
                                          weight(O_PJ, G * NPJ, g * NPJ, NPJ), CT), s)
                    elif kind == "b_kx":
                        g, = a
                        pe.wait_ge(stacked, T * (g + 1))
                        fb.wait_free(pe, s)
                        for i in range(2):
                            for t in range(T):
                                o, f = i * L + t * P, RG * 2 * D + i * D
                                ins = nc.tensor.transpose(fb.bank(s)[:, o:o + P], st[:, t, f:f + P].bitcast(F), idn[:, :])
                        fb.filled(ins, s)
                    elif kind == "b_qx":
                        g, j = a
                        fb.wait_free(pe, s)
                        for i in range(2):
                            for t in range(T):
                                o, h = i * L + t * P, 2 * j + i
                                ins = nc.tensor.transpose(fb.bank(s)[:, o:o + P], st[:, t, h * P:(h + 1) * P].bitcast(F),
                                                          idn[:, :])
                        fb.filled(ins, s)
                    elif kind == "b_s":
                        u, j = a
                        g, t = u // T, u % T
                        fb.wait_drained(pe, ("b_kx", g))
                        fb.wait_drained(pe, ("b_qx", g, j))
                        fb.wait_free(pe, s)
                        for i in range(2):
                            for k in range(2):
                                ins = mm(fb.bank(s)[:, i * L:(i + 1) * L], qt[:, g % 2, 2 * j + i, t * P:(t + 1) * P],
                                         kt[:, g % 2, k, :], k == 0, k == 1)
                        fb.filled(ins, s)
                    elif kind == "b_t":
                        u, j = a
                        pe.wait_ge(pr_ready[j], u + 1)
                        fb.wait_free(pe, s)
                        for k in range(T):
                            for i in range(2):
                                o = k * 2 * P + i * P
                                ins = nc.tensor.transpose(fb.bank(s)[:, o:o + P],
                                                          pr[:, u % 2, 2 * j + i, k * P:(k + 1) * P], idn[:, :])
                        fb.filled(ins, s)
                    elif kind == "b_o":
                        u, = a
                        g = u // T
                        for j in range(2):
                            fb.wait_drained(pe, ("b_t", u, j))
                        pe.wait_ge(va_ready, T * (g + 1))
                        fb.wait_free(pe, s)
                        fb.filled(project(fb.bank(s)[:, :], lambda m, k: va[m][:, k, g, :, :].rearrange("p a d -> p (a d)"),
                                          lambda m, k: pt[m][:, u % 2, k, :], T), s)
                    elif kind == "b_w0":
                        pe.wait_ge(ot_ready, G * T - 1)
                        fb.wait_free(pe, s)
                        fb.filled(project(fb.bank(s)[:, 0:C], lambda k, c: ot[k][:, c, 0:P], weight(O_WO, C, 0, C), HT), s)
                    elif kind == "b_w1a":
                        pe.wait_ge(ot_ready, G * T - T)
                        fb.wait_free(pe, s)
                        project(fb.bank(s)[:, 0:C], lambda k, c: ot[k][:, c, P:2 * P], weight(O_WO, C, 0, C),
                                range(0, HT - 2), stop=False)
                    elif kind == "b_w1b":
                        pe.wait_ge(ot_ready, G * T)
                        fb.filled(project(fb.bank(("b_w1a",))[:, 0:C], lambda k, c: ot[k][:, c, P:2 * P],
                                          weight(O_WO, C, 0, C), range(HT - 2, HT), start=False), ("b_w1a",))
            iterations(pe, body)


LC = 120
HX, DX = 16, 16
HPT = P // DX
HC = 4
XSCALE = DX ** -0.5
NEG = 1.0e9
E, I = 8, 128
NGRP, TOPG, TOPK = 4, 2, 2
GSZ = E // NGRP

O_XQ = 0
O_XK = O_XQ + CT * C
O_XV = O_XK + CT * C
O_XO = O_XV + CT * C
O_GT = O_XO + CT * C
O_G = O_GT + CT * E
O_U = O_G + CT * E * I
O_DN = O_U + CT * E * I
N_W2 = O_DN + E * C

K_XQB = 0
K_XKB = K_XQB + CT
K_XVB = K_XKB + CT
K_XOB = K_XVB + C
K_ESB = K_XOB + C
K_BD = K_ESB + E
K_TRI = K_BD + HPT
K_TRG = K_TRI + E * E
N_K2 = K_TRG + NGRP * NGRP


def cross_stages(feed, prepare):
    out = []

    def f(*stages):
        out.extend(stages if feed else ())

    def c(*stages):
        out.extend(stages if prepare else ())

    c(("c_ct",))
    f(("f_cp",), ("f_gt",))
    c(("c_norm",), ("c_ng",))
    f(("f_rt",))
    c(("c_kv",), ("c_xn",))
    f(("f_gu", 0))
    c(("c_xt",))
    f(("f_cb", 0), ("f_gu", 1), ("f_h", 0), ("f_h", 1), ("f_gu", 2))
    c(("c_q",))
    f(("f_cb", 1), ("f_gu", 3), ("f_h", 2), ("f_h", 3))
    for i in (2, 3):
        f(("f_gu", 2 * i), ("f_cb", i), ("f_gu", 2 * i + 1), ("f_h", 2 * i), ("f_h", 2 * i + 1))
    for t in range(T):
        c(*[("c_l", t, i) for i in range(HX // HC)])
        c(("c_e", t))
    for t in range(T):
        c(("c_m", t))
        c(*[("c_p", t, i) for i in range(HX // HC)])
    c(("c_o",), ("c_w",), ("c_n2",))
    f(("f_dn", 0), ("f_dn", 1))
    c(("c_x2",), ("c_x3",))
    return out


def cross_and_feed(nc, keep, x1, ctxt, gp, mask, out, w2, k2, ident, batches=B):
    with ExitStack() as ctx:
        def sb(name, shape, dt=F):
            return ctx.enter_context(nc.sbuf_tensor("x_" + name, shape, dt))

        sems = []

        def sem(name):
            sems.append(keep.enter_context(nc.semaphore("x_" + name)))
            return sems[-1]

        wh, wl = sb("wh", [P, N_W2], R), sb("wl", [P, N_W2], R)
        w = {"h": wh, "l": wl}
        cst = sb("cst", [P, N_K2])
        idn = sb("idn", [P, P])
        qb4 = sb("qb4", [P, CT])
        xin = sb("xin", [P, T, C])
        cin = sb("cin", [P, C])
        gpt = sb("gpt", [P, T, LC])
        mi = sb("mi", [P, T, LC], I32)
        neg = sb("neg", [P, T, LC])
        stats, mv = sb("stats", [P, T, 6]), sb("mv", [P, T, 2])
        var, rstd, nt = sb("var", [P, T]), sb("rstd", [P, T]), sb("nt", [P, T])
        xn = sb("xn", [P, T, C])
        xnt = {k: sb("xnt" + k, [P, CT, L], R) for k in "hl"}
        ctt = {k: sb("ctt" + k, [P, CT, LC], R) for k in "hl"}
        kf = sb("kf", [P, CT, LC])
        kr = {k: sb("kr" + k, [P, CT, LC], R) for k in "hl"}
        kbd = {k: sb("kbd" + k, [P, CT, HPT, LC], R) for k in "hl"}
        vpad = sb("vpad", [P, CT, HPT, P])
        qf = sb("qf", [P, CT, L])
        qx = {k: sb("qx" + k, [P, CT, L], R) for k in "hl"}
        lm = sb("lm", [P, T, HX, LC])
        mx, nmx = sb("mx", [P, T, HX]), sb("nmx", [P, T, HX])
        sm, rs = sb("sm", [P, T, HX]), sb("rs", [P, T, HX])
        ptc = sb("ptc", [P, HX, L])
        ox = {k: sb("ox" + k, [P, CT, L], R) for k in "hl"}
        xres, xb = sb("xres", [P, T, C]), sb("xb", [P, T, C])
        x2n = sb("x2n", [P, T, C])
        x2t = {k: sb("x2t" + k, [P, CT, L], R) for k in "hl"}
        x2c = sb("x2c", [P, T, C])
        sc, sfc, tmp = sb("sc", [P, T, E]), sb("sfc", [P, T, E]), sb("tmp", [P, T, E])
        gs, gm = sb("gs", [P, T, NGRP]), sb("gm", [P, T, NGRP])
        c1, c2 = sb("c1", [P, T, E, E]), sb("c2", [P, T, E, E])
        rk, cw = sb("rk", [P, T, E]), sb("cw", [P, T, E])
        ws, wr = sb("ws", [P, T]), sb("wr", [P, T])
        sg = sb("sg", [P, 2, L])
        hu = sb("hu", [P, 2, L])
        hf = sb("hf", [P, 2, L])
        hr = {k: sb("hr" + k, [P, E, L], R) for k in "hl"}
        ob = sb("ob", [P, T, C])

        psb = [ctx.enter_context(nc.psum_tensor(f"x_ps{i}", [P, 512], F)) for i in range(8)]
        full, free = [sem(f"full{i}") for i in range(8)], [sem(f"free{i}") for i in range(8)]
        s_own = {e: sem("own_" + e) for e in ("dve", "pool")}
        arrive, fetched = sem("arrive"), sem("fetched")
        guess, rstd_ready, xn_ready = sem("guess"), sem("rstd_ready"), sem("xn_ready")
        xin_read = sem("xin_read")
        ctt_hi, xnt_hi, ox_hi, x2t_hi = sem("ctt_hi"), sem("xnt_hi"), sem("ox_hi"), sem("x2t_hi")
        neg_ready, kf_ready, kbd_ready = sem("neg_ready"), sem("kf_ready"), sem("kbd_ready")
        qx_ready, nmx_ready, exp_done, pc_ready = sem("qx_ready"), sem("nmx_ready"), sem("exp_done"), sem("pc_ready")
        x2c_ready, sc_exp, cw_ready = sem("x2c_ready"), sem("sc_exp"), sem("cw_ready")
        sg_ready, hf_ready, hr_ready = sem("sg_ready"), sem("hf_ready"), sem("hr_ready")
        gp_here, xb_ready, last_add = sem("gp_here"), sem("xb_ready"), sem("last_add")
        xres_here = sem("xres_here")
        in_iteration = list(sems)
        go, passed = sem("go"), sem("passed")
        const_in, split, w_hi = sem("const_in"), sem("split"), sem("w_hi")
        stage_in = [sem("stage_in0"), sem("stage_in1")]
        xin_in, ctx_in, mi_in, gp_in, xres_in = (sem(n) for n in ("xin_in", "ctx_in", "mi_in", "gp_in", "xres_in"))
        stored, zeroed = sem("stored"), sem("zeroed")
        first, last = in_iteration[0].num, in_iteration[-1].num
        assert last - first == len(in_iteration) - 1

        def fills(feed, prepare):
            stages = cross_stages(feed, prepare)
            return (Fills(psb[0:4], full[0:4], free[0:4],
                          [s for s in stages if s[0] in ("f_gt", "f_gu", "f_cb", "f_dn")]),
                    Fills(psb[4:8], full[4:8], free[4:8],
                          [s for s in stages if s[0] in ("c_ct", "c_kv", "c_xt", "c_q", "c_l", "c_p", "c_o", "c_w", "c_x3")]))

        def iterations(eng, body):
            def meet(n):
                eng.drain().then_inc(arrive, 1)
                eng.wait_ge(go, n)
                eng.sem_inc(passed, 1)
            body(-1, False, True, True)
            meet(1)
            if batches > 2:
                with eng.Fori(0, batches - 2) as b:
                    body(b, True, True, True)
                    meet(b + 2)
            body(batches - 2, True, True, False)
            meet(batches)
            body(batches - 1, True, False, False)
            meet(batches + 1)

        CH = 1024
        stage = [ptc[:, :, :].rearrange("p a b -> p (a b)")[:, n * CH:(n + 1) * CH] for n in range(2)]
        chunks = [(o, min(CH, N_W2 - o)) for o in range(0, N_W2, CH)]

        block = ctx.enter_context(nc.Block())

        @block.sync
        def _(sp):
            def rows(t, b):
                return t[bass.ds(b, 1)].rearrange("o (t p) c -> p (o t) c", p=P)

            def fetch_next(b):
                sp.dma_start(xin[:, :, :], rows(x1, b)).then_inc(xin_in, 16)
                sp.dma_start(cin[0:LC, :], ctxt[bass.ds(b, 1)].rearrange("o p c -> p (o c)")).then_inc(ctx_in, 16)
                sp.dma_start(mi[:, :, :], rows(mask, b)).then_inc(mi_in, 16)

            fetch_next(0)
            for n, (o, m) in enumerate(chunks):
                if n >= 2:
                    sp.wait_ge(split, n - 1)
                sp.dma_start(stage[n % 2][:, 0:m], w2[:, o:o + m]).then_inc(stage_in[n % 2], 16)
            sp.dma_start(cst[:, :], k2).then_inc(const_in, 16)
            sp.dma_start(idn[:, :], ident).then_inc(const_in, 16)

            def body(b, feed, prepare, fetch):
                ff, fc = fills(feed, prepare)
                if prepare:
                    sp.dma_start(gpt[:, :, :], rows(gp, b + 1)).then_inc(gp_in, 16)
                    sp.dma_start(xres[:, :, :], rows(x1, b + 1)).then_inc(xres_in, 16)
                if prepare:
                    sp.wait_ge(gp_in, (b + 2) * 16)
                    sp.sem_inc(gp_here, 1)
                    sp.wait_ge(xres_in, (b + 2) * 16)
                    sp.sem_inc(xres_here, 1)
                if prepare and fetch:
                    sp.wait_ge(xin_read, 1)
                    sp.wait_ge(neg_ready, 1)
                    fc.wait_full(sp, ("c_ct",))
                    fetch_next(b + 2)
                if feed:
                    sp.wait_ge(stored, (b + PRIME) * 16)
                    sp.sem_inc(last_add, 1)
                    ff.wait_drained(sp, ("f_dn", 0))
                    ff.wait_drained(sp, ("f_dn", 1))
                    sp.dma_start(rows(out, b), ob[:, :, :]).then_inc(stored, 16)
                if prepare and fetch:
                    for s in (xin_in, ctx_in, mi_in):
                        sp.wait_ge(s, (b + 3) * 16)
                        sp.sem_inc(fetched, 1)
                sp.wait_ge(arrive, 4)
                sp.sem_clear(range(first, last + 1))
                sp.sem_inc(go, 1)

            PRIME = 1
            sp.sem_inc(stored, 16)
            body(-1, False, True, True)
            if batches > 2:
                with sp.Fori(0, batches - 2) as b:
                    body(b, True, True, True)
            body(batches - 2, True, True, False)
            body(batches - 1, True, False, False)
            sp.wait_ge(stored, (batches + PRIME) * 16)
            sp.wait_ge(passed, 4 * (batches + 1))

        @block.gpsimd
        def _(pool):
            own = [0]

            def link(ins):
                own[0] += 1
                ins.then_inc(s_own["pool"], 1)
                pool.wait_ge(s_own["pool"], own[0])

            nc.gpsimd.memset(vpad[:, :, :, :], 0.0).then_inc(zeroed, 1)
            pool.wait_ge(const_in, 32)

            def newton(n_guess):
                pool.wait_ge(guess, n_guess)
                for n in range(3):
                    link(nc.gpsimd.tensor_tensor(nt[:, :], rstd[:, :], rstd[:, :], ALU.mult))
                    link(nc.gpsimd.tensor_tensor(nt[:, :], nt[:, :], var[:, :], ALU.mult))
                    link(nc.gpsimd.tensor_scalar(nt[:, :], nt[:, :], -0.5, 1.5, ALU.mult, ALU.add))
                    i = nc.gpsimd.tensor_tensor(rstd[:, :], rstd[:, :], nt[:, :], ALU.mult)
                    if n < 2:
                        link(i)
                    else:
                        i.then_inc(rstd_ready, 1)

            def body(b, feed, prepare, fetch):
                own[0] = 0
                ff, fc = fills(feed, prepare)
                for s in cross_stages(feed, prepare):
                    kind, a = s[0], s[1:]
                    if kind == "c_norm":
                        newton(1)
                    elif kind == "c_n2":
                        newton(2)
                    elif kind == "c_kv":
                        pool.wait_ge(kf_ready, 1)
                        link(nc.gpsimd.tensor_copy(kr["h"][:, :, :], kf[:, :, :]))
                        link(nc.gpsimd.tensor_tensor(kr["l"][:, :, :], kf[:, :, :], kr["h"][:, :, :].bitcast(F), ALU.subtract))
                        for c in range(CT):
                            for k in "hl":
                                ins = nc.gpsimd.tensor_tensor(
                                    kbd[k][:, c, :, :],
                                    kr[k][:, c, :].bitcast(F).unsqueeze(1).broadcast_to([P, HPT, LC]),
                                    cst[:, K_BD:K_BD + HPT].unsqueeze(2).broadcast_to([P, HPT, LC]), ALU.mult)
                        ins.then_inc(kbd_ready, 1)
                        pool.wait_ge(xres_here, 1)
                        nc.gpsimd.tensor_tensor(xb[:, :, :], xres[:, :, :],
                                                cst[:, K_XOB:K_XOB + C].unsqueeze(1).broadcast_to([P, T, C]),
                                                ALU.add).then_inc(xb_ready, 1)
                    elif kind == "c_q":
                        fc.wait_drained(pool, s)
                        link(nc.gpsimd.tensor_copy(qx["h"][:, :, :], qf[:, :, :]))
                        nc.gpsimd.tensor_tensor(qx["l"][:, :, :], qf[:, :, :], qx["h"][:, :, :].bitcast(F), ALU.subtract)\
                            .then_inc(qx_ready, 1)
                    elif kind == "f_cp":
                        nc.gpsimd.tensor_copy(x2c[:, :, :], x2n[:, :, :]).then_inc(x2c_ready, 1)
                    elif kind == "f_h":
                        e, = a
                        if e % 2:
                            ff.wait_drained(pool, ("f_cb", e // 2))
                        else:
                            pool.wait_ge(hf_ready, e // 2 + 1)
                        link(nc.gpsimd.tensor_copy(hr["h"][:, e, :], hf[:, e % 2, :]))
                        nc.gpsimd.tensor_tensor(hr["l"][:, e, :], hf[:, e % 2, :], hr["h"][:, e, :].bitcast(F), ALU.subtract)\
                            .then_inc(hr_ready, 1)
            iterations(pool, body)

        @block.scalar
        def _(act):
            for n, (o, m) in enumerate(chunks):
                act.wait_ge(stage_in[n % 2], 16 * (n // 2 + 1))
                nc.scalar.activation(wh[:, o:o + m], stage[n % 2][:, 0:m], ACT.Copy).then_inc(w_hi, 1)
            act.wait_ge(const_in, 32)
            act.wait_ge(split, len(chunks) + 1)

            def halves_hi(fl, s, to, width, sem_hi):
                fl.wait_full(act, s)
                nc.scalar.activation(to[:, :, :], fl.bank(s)[:, 0:CT * width].rearrange("p (c l) -> p c l", l=width),
                                     ACT.Copy).then_inc(sem_hi, 1)

            def body(b, feed, prepare, fetch):
                ff, fc = fills(feed, prepare)
                for s in cross_stages(feed, prepare):
                    kind, a = s[0], s[1:]
                    if kind == "c_ct":
                        halves_hi(fc, s, ctt["h"], LC, ctt_hi)
                    elif kind == "c_xt":
                        halves_hi(fc, s, xnt["h"], L, xnt_hi)
                    elif kind == "c_q":
                        fc.wait_full(act, s)
                        for c in range(CT):
                            ins = nc.scalar.activation(qf[:, c, :], fc.bank(s)[:, c * L:(c + 1) * L], ACT.Identity,
                                                       bias=qb4[:, c:c + 1], scale=XSCALE)
                        fc.drained(ins, s)
                    elif kind == "c_e":
                        t, = a
                        act.wait_ge(nmx_ready, t + 1)
                        for h in range(HX):
                            ins = nc.scalar.activation(lm[:, t, h, :], lm[:, t, h, :], ACT.Exp,
                                                       bias=nmx[:, t, h:h + 1], accum_out=sm[:, t, h:h + 1])
                        ins.then_inc(exp_done, 1)
                    elif kind == "c_p":
                        t, i = a
                        fc.wait_full(act, s)
                        fc.drained(nc.scalar.activation(ptc[0:LC, i * HC:(i + 1) * HC, t * P:(t + 1) * P],
                                   fc.bank(s)[0:LC, :].rearrange("p (h q) -> p h q", q=P), ACT.Copy), s)
                    elif kind == "c_o":
                        halves_hi(fc, s, ox["h"], L, ox_hi)
                    elif kind == "c_x3":
                        if feed:
                            ff.wait_full(act, ("f_gu", E - 1))
                        halves_hi(fc, s, x2t["h"], L, x2t_hi)
                    elif kind == "f_gt":
                        ff.wait_full(act, s)
                        ff.drained(nc.scalar.activation(sc[:, :, :], ff.bank(s)[:, 0:T * E].rearrange("p (t e) -> p t e", e=E),
                                                        ACT.Exp, scale=-1.0), s)
                    elif kind == "f_gu":
                        e, = a
                        ff.wait_full(act, s)
                        if e >= 2:
                            ff.wait_drained(act, ("f_gu", e - 2))
                        nc.scalar.activation(sg[:, e % 2, :], ff.bank(s)[:, 0:L], ACT.Silu).then_inc(sg_ready, 1)
            iterations(act, body)

        @block.vector
        def _(dve):
            own = [0]

            def link(ins):
                own[0] += 1
                ins.then_inc(s_own["dve"], 1)
                dve.wait_ge(s_own["dve"], own[0])

            for n, (o, m) in enumerate(chunks):
                dve.wait_ge(w_hi, n + 1)
                nc.vector.tensor_tensor(wl[:, o:o + m], stage[n % 2][:, 0:m], wh[:, o:o + m].bitcast(F),
                                        ALU.subtract).then_inc(split, 1)
            dve.wait_ge(const_in, 32)
            nc.vector.tensor_scalar(qb4[:, :], cst[:, K_XQB:K_XQB + CT], XSCALE, None, ALU.mult).then_inc(split, 1)
            dve.wait_ge(split, len(chunks) + 1)
            dve.wait_ge(zeroed, 1)
            for s in (xin_in, ctx_in, mi_in):
                dve.wait_ge(s, 16)

            def norm_guess(src):
                for t in range(T):
                    i = nc.vector.bn_stats(stats[:, t, :], src[:, t, :])
                link(i)
                for t in range(T):
                    i = nc.vector.bn_aggr(mv[:, t, :], stats[:, t, :])
                link(i)
                link(nc.vector.tensor_scalar(var[:, :], mv[:, :, 1], EPS, None, ALU.add))
                link(nc.vector.tensor_scalar(nt[:, :].bitcast(I32), var[:, :].bitcast(I32), 1, None,
                                             ALU.logical_shift_right))
                nc.vector.tensor_scalar(rstd[:, :].bitcast(I32), nt[:, :].bitcast(I32), -1.0, float(MAGIC),
                                        ALU.mult, ALU.add).then_inc(guess, 1)

            def normalise(src, n):
                dve.wait_ge(rstd_ready, n)
                for t in range(T):
                    ins = nc.vector.tensor_scalar(xn[:, t, :], src[:, t, :], mv[:, t, 0:1], rstd[:, t:t + 1],
                                                  ALU.subtract, ALU.mult)
                    if t == 0:
                        ins.then_inc(xn_ready, 1)
                return ins

            def halves_lo(fl, s, to, width, sem_hi):
                dve.wait_ge(sem_hi, 1)
                fl.drained(nc.vector.tensor_tensor(
                    to["l"][:, :, :], fl.bank(s)[:, 0:CT * width].rearrange("p (c l) -> p c l", l=width),
                    to["h"][:, :, :].bitcast(F), ALU.subtract), s)

            def chosen(score, n, tri, top, out):
                rows = (P, T, n, n)
                own_, other = score.unsqueeze(3).broadcast_to(rows), score.unsqueeze(2).broadcast_to(rows)
                first = cst[:, tri:tri + n * n].rearrange("p (i j) -> p i j", j=n)
                above, equal = c1[:, :, 0:n, 0:n], c2[:, :, 0:n, 0:n]
                for t in range(T):
                    nc.vector.tensor_tensor(above[:, t], other[:, t], own_[:, t], ALU.is_gt)
                    ins = nc.vector.tensor_tensor(equal[:, t], other[:, t], own_[:, t], ALU.is_equal)
                link(ins)
                for t in range(T):
                    ins = nc.vector.tensor_tensor(equal[:, t], equal[:, t], first, ALU.mult)
                link(ins)
                for t in range(T):
                    ins = nc.vector.tensor_tensor(above[:, t], above[:, t], equal[:, t], ALU.add)
                link(ins)
                link(nc.vector.tensor_reduce(rk[:, :, 0:n], above, mybir.AxisListType.X, ALU.add))
                link(nc.vector.tensor_scalar(out, rk[:, :, 0:n], float(top), None, ALU.is_lt))

            def body(b, feed, prepare, fetch):
                own[0] = 0
                ff, fc = fills(feed, prepare)
                for s in cross_stages(feed, prepare):
                    kind, a = s[0], s[1:]
                    if kind == "c_norm":
                        norm_guess(xin)
                    elif kind == "c_xn":
                        normalise(xin, 1).then_inc(xin_read, 1)
                    elif kind == "c_ct":
                        halves_lo(fc, s, ctt, LC, ctt_hi)
                    elif kind == "c_xt":
                        halves_lo(fc, s, xnt, L, xnt_hi)
                    elif kind == "c_ng":
                        nc.vector.tensor_scalar(neg[:, :, :], mi[:, :, :], -1.0, NEG, ALU.add, ALU.mult)\
                            .then_inc(neg_ready, 1)
                    elif kind == "c_kv":
                        fc.wait_full(dve, s)
                        ps = fc.bank(s)
                        for c in range(CT):
                            ins = nc.vector.tensor_scalar(kf[:, c, :], ps[:, c * LC:(c + 1) * LC],
                                                          cst[:, K_XKB + c:K_XKB + c + 1], None, ALU.add)
                        ins.then_inc(kf_ready, 1)
                        for c in range(CT):
                            o = CT * LC + c * P
                            to = vpad[0:LC, c, :, :].rearrange("p j n -> p (j n)")
                            blocks = to.rearrange("p (a b) -> p a b", b=DX)[:, 0:HPT * (P // DX):P // DX + 1, :]
                            ins = nc.vector.tensor_tensor(
                                blocks, ps[0:LC, o:o + P].rearrange("p (j d) -> p j d", d=DX),
                                cst[0:LC, K_XVB + c * P:K_XVB + (c + 1) * P].rearrange("p (j d) -> p j d", d=DX), ALU.add)
                        fc.drained(ins, s)
                    elif kind == "c_l":
                        t, i = a
                        if t == 0 and i == 0:
                            dve.wait_ge(neg_ready, 1)
                        fc.wait_full(dve, s)
                        for j in range(HC):
                            h = i * HC + j
                            ins = nc.vector.tensor_tensor_reduce(
                                out=lm[:, t, h, :], in0=fc.bank(s)[:, j * LC:(j + 1) * LC], in1=neg[:, t, :],
                                scale=1.0, scalar=LOWEST, op0=ALU.add, op1=ALU.max, accum_out=mx[:, t, h:h + 1])
                        fc.drained(ins, s)
                        if i == HX // HC - 1:
                            fc.wait_drained(dve, s)
                            nc.vector.tensor_scalar(nmx[:, t, :], mx[:, t, :], -1.0, None, ALU.mult).then_inc(nmx_ready, 1)
                    elif kind == "c_m":
                        t, = a
                        dve.wait_ge(exp_done, t + 1)
                        link(nc.vector.reciprocal(rs[:, t, :], sm[:, t, :]))
                        if t == 0:
                            dve.wait_ge(gp_here, 1)
                        for h in range(HX):
                            ins = nc.vector.scalar_tensor_tensor(lm[:, t, h, :], lm[:, t, h, :], rs[:, t, h:h + 1],
                                                                 gpt[:, t, :], ALU.mult, ALU.mult)
                            if h % HC == HC - 1:
                                ins.then_inc(pc_ready, 1)
                    elif kind == "c_o":
                        halves_lo(fc, s, ox, L, ox_hi)
                    elif kind == "c_w":
                        fc.wait_full(dve, s)
                        dve.wait_ge(xb_ready, 1)
                        if feed:
                            dve.wait_ge(x2c_ready, 1)
                        fc.drained(nc.vector.tensor_tensor(x2n[:, :, :], fc.bank(s)[:, :].rearrange("p (t n) -> p t n", t=T),
                                                           xb[:, :, :], ALU.add), s)
                    elif kind == "c_n2":
                        fc.wait_drained(dve, ("c_w",))
                        norm_guess(x2n)
                    elif kind == "c_x2":
                        fc.wait_full(dve, ("c_xt",))
                        normalise(x2n, 2).then_inc(xn_ready, 1)
                    elif kind == "c_x3":
                        halves_lo(fc, s, x2t, L, x2t_hi)
                    elif kind == "f_rt":
                        ff.wait_drained(dve, ("f_gt",))
                        link(nc.vector.tensor_scalar(sc[:, :, :], sc[:, :, :], 1.0, None, ALU.add))
                        link(nc.vector.reciprocal(sc[:, :, :], sc[:, :, :]))
                        link(nc.vector.tensor_tensor(sfc[:, :, :], sc[:, :, :],
                                                     cst[:, K_ESB:K_ESB + E].unsqueeze(1).broadcast_to([P, T, E]), ALU.add))
                        pairs = sfc[:, :, :].rearrange("p t (g k) -> p t g k", k=GSZ)
                        link(nc.vector.tensor_tensor(gs[:, :, :], pairs[:, :, :, 0], pairs[:, :, :, 1], ALU.add))
                        chosen(gs[:, :, :], NGRP, K_TRG, TOPG, gm[:, :, :])
                        link(nc.vector.tensor_tensor(tmp[:, :, :].rearrange("p t (g k) -> p t g k", k=GSZ), pairs,
                                                     gm[:, :, :].unsqueeze(3).broadcast_to([P, T, NGRP, GSZ]), ALU.mult))
                        chosen(tmp[:, :, :], E, K_TRI, TOPK, cw[:, :, :])
                        link(nc.vector.tensor_tensor(cw[:, :, :], cw[:, :, :], sc[:, :, :], ALU.mult))
                        link(nc.vector.tensor_reduce(ws[:, :], cw[:, :, :], mybir.AxisListType.X, ALU.add))
                        link(nc.vector.tensor_scalar(ws[:, :], ws[:, :], 1e-20, None, ALU.add))
                        link(nc.vector.reciprocal(wr[:, :], ws[:, :]))
                        nc.vector.tensor_tensor(cw[:, :, :], cw[:, :, :], wr[:, :].unsqueeze(2).broadcast_to([P, T, E]),
                                                ALU.mult).then_inc(cw_ready, 1)
                    elif kind == "f_gu":
                        e, = a
                        dve.wait_ge(sg_ready, e + 1)
                        if e >= 2:
                            if e % 2:
                                ff.wait_drained(dve, ("f_cb", e // 2 - 1))
                            else:
                                dve.wait_ge(hf_ready, e // 2)
                        ff.drained(nc.vector.tensor_tensor(hu[:, e % 2, :], ff.bank(s)[:, L:2 * L], sg[:, e % 2, :],
                                                           ALU.mult), s)
                    elif kind == "f_h":
                        e, = a
                        cb = ("f_cb", e // 2)
                        ff.wait_full(dve, cb)
                        ff.wait_drained(dve, ("f_gu", e))
                        if e >= 2:
                            dve.wait_ge(hr_ready, e - 1)
                        ins = nc.vector.tensor_tensor(hf[:, e % 2, :], ff.bank(cb)[:, (e % 2) * L:(e % 2 + 1) * L],
                                                      hu[:, e % 2, :], ALU.mult)
                        if e % 2:
                            ff.drained(ins, cb)
                        else:
                            ins.then_inc(hf_ready, 1)
                    elif kind == "f_dn":
                        t, = a
                        ff.wait_full(dve, s)
                        if t == 0:
                            dve.wait_ge(last_add, 1)
                            dve.wait_ge(x2c_ready, 1)
                        ff.drained(nc.vector.tensor_tensor(ob[:, t, :], ff.bank(s)[:, 0:C], x2c[:, t, :], ALU.add), s)
            iterations(dve, body)

        @block.tensor
        def _(pe):
            pe.wait_ge(split, len(chunks) + 1)
            pe.wait_ge(const_in, 32)
            pe.wait_ge(zeroed, 1)

            def project(out, lhs, rhs, tiles):
                n, last = 0, len(PRODUCTS) * tiles - 1
                for c in range(tiles):
                    for a, b in PRODUCTS:
                        ins = nc.tensor.matmul(out, lhs(a, c), rhs(b, c), start=(n == 0), stop=(n == last))
                        n += 1
                return ins

            def weight(o, width, at, n):
                return lambda k, c: w[k][:, o + c * width + at:o + c * width + at + n]

            def turn(fl, s):
                fl.wait_free(pe, s)
                for c in range(CT):
                    for t in range(T):
                        o = c * L + t * P
                        ins = nc.tensor.transpose(fl.bank(s)[:, o:o + P], xn[:, t, c * P:(c + 1) * P], idn[:, :])
                fl.filled(ins, s)

            def body(b, feed, prepare, fetch):
                ff, fc = fills(feed, prepare)
                for s in cross_stages(feed, prepare):
                    kind, a = s[0], s[1:]
                    if kind == "c_ct":
                        for c in range(CT):
                            ins = nc.tensor.transpose(fc.bank(s)[:, c * LC:(c + 1) * LC], cin[0:LC, c * P:(c + 1) * P],
                                                      idn[0:LC, 0:LC])
                        fc.filled(ins, s)
                    elif kind == "c_kv":
                        fc.wait_drained(pe, ("c_ct",))
                        fc.wait_free(pe, s)
                        for f in range(CT):
                            project(fc.bank(s)[:, f * LC:(f + 1) * LC], weight(O_XK, C, f * P, P),
                                    lambda k, c: ctt[k][:, c, :], CT)
                        fc.filled(project(fc.bank(s)[0:LC, CT * LC:CT * LC + C], lambda k, c: ctt[k][:, c, :],
                                          weight(O_XV, C, 0, C), CT), s)
                    elif kind == "c_xt":
                        pe.wait_ge(xn_ready, 1)
                        pe.wait_ge(xin_read, 1)
                        turn(fc, s)
                    elif kind == "c_q":
                        fc.wait_drained(pe, ("c_xt",))
                        fc.wait_free(pe, s)
                        for f in range(CT):
                            ins = project(fc.bank(s)[:, f * L:(f + 1) * L], weight(O_XQ, C, f * P, P),
                                          lambda k, c: xnt[k][:, c, :], CT)
                        fc.filled(ins, s)
                    elif kind == "c_l":
                        t, i = a
                        f, o = i // 2, (i % 2) * HC
                        pe.wait_ge(kbd_ready, 1)
                        pe.wait_ge(qx_ready, 1)
                        fc.wait_free(pe, s)
                        fc.filled(project(fc.bank(s)[:, 0:HC * LC], lambda k, c: qx[k][:, f, t * P:(t + 1) * P],
                                          lambda k, c: kbd[k][:, f, o:o + HC, :].rearrange("p j n -> p (j n)"), 1), s)
                    elif kind == "c_p":
                        t, i = a
                        pe.wait_ge(pc_ready, t * (HX // HC) + i + 1)
                        fc.wait_free(pe, s)
                        for j in range(HC):
                            ins = nc.tensor.transpose(fc.bank(s)[0:LC, j * P:(j + 1) * P], lm[:, t, i * HC + j, :], idn[:, :])
                        fc.filled(ins, s)
                    elif kind == "c_o":
                        for t in range(T):
                            for i in range(HX // HC):
                                fc.wait_drained(pe, ("c_p", t, i))
                        fc.wait_free(pe, s)
                        for f in range(CT):
                            for j in range(HPT):
                                ins = nc.tensor.matmul(fc.bank(s)[:, f * L:(f + 1) * L], vpad[0:LC, f, j, :],
                                                       ptc[0:LC, f * HPT + j, :], start=(j == 0), stop=(j == HPT - 1))
                        fc.filled(ins, s)
                    elif kind == "c_w":
                        fc.wait_drained(pe, ("c_o",))
                        fc.wait_free(pe, s)
                        for t in range(T):
                            ins = project(fc.bank(s)[:, t * C:(t + 1) * C], lambda k, c: ox[k][:, c, t * P:(t + 1) * P],
                                          weight(O_XO, C, 0, C), CT)
                        fc.filled(ins, s)
                    elif kind == "c_x3":
                        pe.wait_ge(xn_ready, 3)
                        turn(fc, s)
                    elif kind == "f_gt":
                        for t in range(T):
                            ins = project(ff.bank(s)[:, t * E:(t + 1) * E], lambda k, c: x2t[k][:, c, t * P:(t + 1) * P],
                                          weight(O_GT, E, 0, E), CT)
                        ff.filled(ins, s)
                    elif kind == "f_gu":
                        e, = a
                        ff.wait_free(pe, s)
                        for n, o in enumerate((O_G, O_U)):
                            ins = project(ff.bank(s)[:, n * L:(n + 1) * L], weight(o, E * I, e * I, I),
                                          lambda k, c: x2t[k][:, c, :], CT)
                        ff.filled(ins, s)
                    elif kind == "f_cb":
                        i, = a
                        pe.wait_ge(cw_ready, 1)
                        ff.wait_free(pe, s)
                        for j in range(2):
                            for t in range(T):
                                o, e = j * L + t * P, 2 * i + j
                                ins = nc.tensor.transpose(ff.bank(s)[:, o:o + P], cw[:, t, e:e + 1].broadcast_to([P, P]),
                                                          idn[:, :])
                        ff.filled(ins, s)
                    elif kind == "f_dn":
                        t, = a
                        pe.wait_ge(hr_ready, E)
                        ff.wait_free(pe, s)
                        ff.filled(project(ff.bank(s)[:, 0:C], lambda k, c: hr[k][:, c, t * P:(t + 1) * P],
                                          weight(O_DN, C, 0, C), E), s)
            iterations(pe, body)


def decoder(nc, x, ctxt, gp, mask, w1, k1, rope, w2, k2, ident, out, batches=B):
    x1 = nc.dram_tensor("x1_dram", [batches, L, C], F, kind="Internal").ap()
    with ExitStack() as keep:
        self_attention(nc, keep, x, x1, w1, k1, rope, ident, batches)
        cross_and_feed(nc, keep, x1, ctxt, gp, mask, out, w2, k2, ident, batches)


def tiles(w):
    return w.reshape(-1, P, w.shape[1]).transpose(1, 0, 2).reshape(P, -1)


def everywhere(v):
    return np.broadcast_to(v.reshape(1, -1), (P, v.size))


def packed(i):
    a = {n[8:]: np.asarray(v) for n, v in i.items() if n.startswith("L0_attn_")}
    c = {n[9:]: np.asarray(v) for n, v in i.items() if n.startswith("L0_xattn_")}
    f = {n[7:]: np.asarray(v) for n, v in i.items() if n.startswith("L0_ffn_")}
    groups = []
    for g in range(G):
        q, kv = slice(g * RG * D, (g + 1) * RG * D), slice(g * D, (g + 1) * D)
        groups += [a["Wq"][:, q], a["Wk"][:, kv], a["Wv"][:, kv]]
    w1 = [tiles(np.concatenate([a["Wqi"], a["Wki"], a["Wwi"]], 1)), tiles(np.concatenate(groups, 1)),
          tiles(a["Wvg"]), tiles(a["Wog"]), tiles(a["Wo"])]
    k1 = [everywhere(a["bvg"]), everywhere(a["bi"]), a["bog"].reshape(HT, P).T]
    half = np.arange(0, D, 2, dtype=np.float32) / np.float32(D)
    angle = np.outer(np.arange(L, dtype=np.float32), np.float32(1) / np.float32(10000) ** half).astype(np.float32)
    cos, sin = np.cos(angle), np.sin(angle)
    rope = np.stack([np.concatenate([cos, cos], 1), np.concatenate([-sin, sin], 1)], 1)
    rope = rope.reshape(T, P, 2, D).transpose(1, 0, 2, 3)
    experts = [w.reshape(E * I, C).T for w in (f["gate_proj"], f["up_proj"])]
    w2 = [tiles(c["wq_k"]), tiles(c["wk_k"]), tiles(c["wv_k"]), tiles(c["wo_k"]), tiles(f["gate_weight"].T),
          tiles(experts[0]), tiles(experts[1]), f["down_proj"].transpose(2, 0, 1).reshape(I, E * C)]
    own = (np.arange(P)[:, None] // DX == np.arange(HPT)[None, :]).astype(np.float32)
    k2 = [c["wq_b"].reshape(CT, P).T, c["wk_b"].reshape(CT, P).T, everywhere(c["wv_b"]), everywhere(c["wo_b"]),
          everywhere(f["e_score_correction_bias"]), own, everywhere(np.tril(np.ones((E, E), np.float32), -1)),
          everywhere(np.tril(np.ones((NGRP, NGRP), np.float32), -1))]
    return {"w1": np.concatenate(w1, 1), "k1": np.concatenate(k1, 1), "rope": rope, "w2": np.concatenate(w2, 1),
            "k2": np.concatenate(k2, 1), "ident": np.eye(P, dtype=np.float32)}


def kernel(**inputs):
    import concourse.bacc as bacc
    from concourse.bass_utils import run_bass_kernel_spmd

    arrays = {"x": inputs["x"], "ctx": inputs["ctx_1024"], "gp": inputs["fside_BxSxS2_0"],
              "mask": inputs["mask_BxSxS2_ik1"], **packed(inputs)}
    arrays = {"in_" + n: np.ascontiguousarray(a) for n, a in arrays.items()}
    nc = bacc.Bacc("TRN2", target_bir_lowering=False, num_devices=1)
    t = {n[3:]: nc.dram_tensor(n, list(a.shape), mybir.dt.from_np(a.dtype), kind="ExternalInput").ap()
         for n, a in arrays.items()}
    out = nc.dram_tensor("out_dram", [B, L, C], F, kind="ExternalOutput").ap()
    decoder(nc, t["x"], t["ctx"], t["gp"], t["mask"], t["w1"], t["k1"], t["rope"], t["w2"], t["k2"], t["ident"], out)
    return run_bass_kernel_spmd(nc, [arrays], core_ids=[0]).results[0]["out_dram"]
```

```python
from contextlib import ExitStack

import numpy as np

import concourse.bass as bass
from concourse import mybir

F = mybir.dt.float32
R = mybir.dt.float32r
I32 = mybir.dt.int32
ALU = mybir.AluOpType
ACT = mybir.ActivationFunctionType

B, L, C = 32, 256, 256
P = 128
T = L // P
CT = C // P
H, G, D = 16, 4, 64
RG = H // G
HI = 4
KSEL = 64
SCALE = D ** -0.5
EPS = 1e-5
MASKED = -1e30
LOWEST = -3.0e38
TAKEN = -64.0
MAGIC = 0x5F3759DF

NIDX = HI * D + D + HI
NPJ = RG * D + 2 * D
ROT = RG * D + D
ST = RG * 2 * D + 3 * D
HT = H * D // P

O_IDX = 0
O_PJ = O_IDX + CT * NIDX
O_VG = O_PJ + CT * G * NPJ
O_OG = O_VG + CT * G * D
O_WO = O_OG + CT * H * D
N_W1 = O_WO + HT * C

K_BVG = 0
K_BI = K_BVG + G * D
K_BOG = K_BI + HI
N_K1 = K_BOG + HT

PRODUCTS = (("h", "h"), ("h", "l"), ("l", "h"))


class Fills:

    def __init__(self, banks, full, free, names):
        self.banks, self.full, self.free = banks, full, free
        self.at = {name: (n % len(banks), n // len(banks)) for n, name in enumerate(names)}

    def bank(self, name):
        return self.banks[self.at[name][0]]

    def wait_free(self, eng, name):
        b, n = self.at[name]
        if n:
            eng.wait_ge(self.free[b], n)

    def wait_full(self, eng, name):
        b, n = self.at[name]
        eng.wait_ge(self.full[b], n + 1)

    def wait_drained(self, eng, name):
        b, n = self.at[name]
        eng.wait_ge(self.free[b], n + 1)

    def filled(self, ins, name):
        ins.then_inc(self.full[self.at[name][0]], 1)

    def drained(self, ins, name):
        ins.then_inc(self.free[self.at[name][0]], 1)


NTK = KSEL // 8
NTA = 4
AHEAD = 2


def self_stages(attend, prepare, fetch):
    units = G * T
    norm = [("a_norm", 1)] if fetch else []
    ahead = []
    if prepare:
        ahead = [[("a_xn",)], [("a_xt",)], [("a_ix", 0), ("a_ix", 1)],
                 [("a_iqx", 0), ("a_iqx", 1), ("a_ikx",)], [("a_si", 0, 0), ("a_si", 0, 1)],
                 [("a_si", 1, 0), ("a_si", 1, 1)]] + [[("a_tk", r)] for r in range(NTA)]
        scores = {4: [("a_sc", 0, 0), ("a_sc", 0, 1)], 5: [("a_sc", 1, 0), ("a_sc", 1, 1)]}
    if not attend:
        return [("a_norm", 0)] + [s for n, slot in enumerate(ahead) for s in slot + scores.get(n, [])] + norm
    if not prepare:
        ahead, scores = [[], [], []], {}

    def logits(u):
        return [("b_s", u, 0), ("b_s", u, 1)]

    def projected(g):
        return [("b_pj", g, 0), ("b_pj", g, 1)]

    def rounded(g):
        return [("b_r", g, 0), ("b_r", g, 1)]

    def values(g):
        return [("b_v", g, 0), ("b_v", g, 1)]

    def stacks(g):
        return [("b_kx", g), ("b_qx", g, 0), ("b_qx", g, 1)]

    late = [("b_tk", r) for r in range(NTA, NTK)]
    out = ahead[0] + [("b_vg",)] + projected(0) + [("b_cp",), ("b_og", 0)] + rounded(0) + late[:2]
    out += ahead[1] + [("b_og", 1), ("b_og", 2), ("b_og", 3)]
    out += late[2:] + [("b_mk",)] + stacks(0) + projected(1) + rounded(1) + logits(0) + [("b_e", 0)]
    out += logits(1) + ahead[2] + [("b_n", 0), ("b_e", 1)] + values(0) + stacks(1) + values(1)
    for u in range(units):
        g = u // T + 2
        if u % T == 1 and g < G:
            out += rounded(g)
        if u + 1 < units:
            out += [("b_n", u + 1)]
        out += [("b_t", u, 0), ("b_t", u, 1)]
        if u + AHEAD < units:
            out += logits(u + AHEAD) + [("b_e", u + AHEAD)]
        out += [("b_l", u, 0), ("b_l", u, 1)]
        if u >= 2:
            out += [("b_h", u - 2)]
        if u >= 1:
            out += [("b_o", u - 1)]
        if u == units - 1:
            out += [("b_o", u)]
        more = u + 3 < len(ahead) and u < units - 1
        if more:
            out += ahead[u + 3]
        if u >= 1:
            out += [("b_g", u - 1)]
        if u % T == 0 and g < G:
            out += projected(g)
        if more:
            out += scores.get(u + 3, [])
        if u % T == 1 and g < G:
            out += stacks(g) + values(g)
        if u == units - 2:
            out += norm
    u = units - 1
    out += [("b_h", u - 1), ("b_g", u), ("b_h", u), ("b_w1a",), ("b_w0",), ("b_w1b",)]
    return out + [s for slot in ahead[u + 3:] for s in slot]


def self_attention(nc, keep, x, x1, w1, k1, rope, ident, batches=B):
    with ExitStack() as ctx:
        def sb(name, shape, dt=F):
            return ctx.enter_context(nc.sbuf_tensor("s_" + name, shape, dt))

        sems = []

        def sem(name):
            sems.append(keep.enter_context(nc.semaphore("s_" + name)))
            return sems[-1]

        wh, wl = sb("wh", [P, N_W1], R), sb("wl", [P, N_W1], R)
        w = {"h": wh, "l": wl}
        cst = sb("cst", [P, N_K1])
        half = sb("half", [P, N_K1])
        cs = sb("cs", [P, T, 2, D])
        idn = sb("idn", [P, P])
        xin = sb("xin", [P, T, C])
        stats, mv = sb("stats", [P, T, 6]), sb("mv", [P, T, 2])
        var, rstd, nt = sb("var", [P, T]), sb("rstd", [P, T]), sb("nt", [P, T])
        xn = sb("xn", [P, T, C])
        xnt = {k: sb("xnt" + k, [P, CT, L], R) for k in "hl"}
        ist = sb("ist", [P, T, ST], R)
        wth, wt1 = sb("wth", [P, T, HI]), sb("wt1", [P, T, HI])
        iqt = sb("iqt", [P, HI, L], R)
        ikt = sb("ikt", [P, 2, L], R)
        sig = sb("sig", [P, 2, 2, L])
        score = sb("score", [P, T, L])
        top8 = sb("top8", [P, T, 8])
        xct = {k: sb("xct" + k, [P, CT, L], R) for k in "hl"}
        mb = sb("mb", [P, T, L])
        vg = sb("vg", [P, T, G * D])
        g1t = sb("g1t", [P, HT, L])
        t1, t2, rs = sb("t1", [P, T, ROT]), sb("t2", [P, T, ROT]), sb("rs", [P, T, ROT])
        st = sb("st", [P, T, ST], R)
        kt = sb("kt", [P, 2, 2, L], R)
        qt = sb("qt", [P, 2, RG, L], R)
        vf = sb("vf", [P, 2, T, D])
        va = {k: sb("va" + k, [P, T, G, 2, D], R) for k in "hl"}
        sm = sb("sm", [P, 2, RG, L])
        mx, nm = sb("mx", [P, 2, RG]), sb("nm", [P, 2, RG])
        pr = sb("pr", [P, 2, RG, L])
        rsum, rinv = sb("rsum", [P, 2, RG]), sb("rinv", [P, 2, RG])
        pt = {k: sb("pt" + k, [P, 2, T, RG * P], R) for k in "hl"}
        on = sb("on", [P, 2, 2, P])
        ot = {k: sb("ot" + k, [P, HT, L], R) for k in "hl"}
        xres = sb("xres", [P, T, C])
        x1b = sb("x1b", [P, T, C])

        psb = [ctx.enter_context(nc.psum_tensor(f"s_ps{i}", [P, 512], F)) for i in range(8)]
        full, free = [sem(f"full{i}") for i in range(8)], [sem(f"free{i}") for i in range(8)]
        s_own = {e: sem("own_" + e) for e in ("dve", "pool")}
        arrive, fetched = sem("arrive"), sem("fetched")
        guess, rstd_ready, xn_ready = sem("guess"), sem("rstd_ready"), sem("xn_ready")
        xnt_hi = sem("xnt_hi")
        ist_hi = sem("ist_hi")
        sig_ready, sig_used = sem("sig_ready"), sem("sig_used")
        wt_ready = sem("wt_ready")
        xct_ready, vg_ready = sem("xct_ready"), sem("vg_ready")
        turned, summed, rounded, stacked = sem("turned"), sem("summed"), sem("rounded"), sem("stacked")
        va_hi, va_ready = sem("va_hi"), sem("va_ready")
        nm_ready, exp_done = sem("nm_ready"), sem("exp_done")
        rinv_ready, pt_hi = sem("rinv_ready"), sem("pt_hi")
        pr_ready = [sem("pr_ready0"), sem("pr_ready1")]
        on_ready, ot_hi, ot_ready = sem("on_ready"), sem("ot_hi"), sem("ot_ready")
        last_add = sem("last_add")
        in_iteration = list(sems)
        go, passed = sem("go"), sem("passed")
        const_in, split = sem("const_in"), sem("split")
        stage_in = [sem("stage_in0"), sem("stage_in1")]
        xin_in, xres_in, stored = sem("xin_in"), sem("xres_in"), sem("stored")
        w_hi = sem("w_hi")
        first, last = in_iteration[0].num, in_iteration[-1].num
        assert last - first == len(in_iteration) - 1

        def fills(attend, prepare, fetch):
            b, a = [], []
            for s in self_stages(attend, prepare, fetch):
                if s[0] in ("a_xt", "a_ix", "a_iqx", "a_ikx", "a_si"):
                    a.append(s)
                elif s[0] in ("b_vg", "b_og", "b_pj", "b_kx", "b_qx", "b_s", "b_t", "b_o", "b_w0",
                              "b_w1a"):
                    b.append(s)
            return (Fills(psb[0:5], full[0:5], free[0:5], b),
                    Fills(psb[5:8], full[5:8], free[5:8], a))

        def iterations(eng, body):
            def meet(n):
                eng.drain().then_inc(arrive, 1)
                eng.wait_ge(go, n)
                eng.sem_inc(passed, 1)
            body(-1, False, True, True)
            meet(1)
            if batches > 2:
                with eng.Fori(0, batches - 2) as b:
                    body(b, True, True, True)
                    meet(b + 2)
            body(batches - 2, True, True, False)
            meet(batches)
            body(batches - 1, True, False, False)
            meet(batches + 1)

        CH = 1024
        stage = [sm[:, :, :, :].rearrange("p a b c -> p (a b c)"),
                 pr[:, :, :, :].rearrange("p a b c -> p (a b c)")]
        chunks = [(o, min(CH, N_W1 - o)) for o in range(0, N_W1, CH)]

        block = ctx.enter_context(nc.Block())

        @block.sync
        def _(sp):
            sp.dma_start(xin[:, :, :], x[0].rearrange("(t p) c -> p t c", p=P)).then_inc(xin_in, 16)
            for n, (o, m) in enumerate(chunks):
                if n >= 2:
                    sp.wait_ge(split, n - 1)
                sp.dma_start(stage[n % 2][:, 0:m], w1[:, o:o + m]).then_inc(stage_in[n % 2], 16)
            sp.dma_start(cst[:, :], k1).then_inc(const_in, 16)
            sp.dma_start(cs[:, :, :, :], rope).then_inc(const_in, 16)
            sp.dma_start(idn[:, :], ident).then_inc(const_in, 16)

            def rows(t, b):
                return t[bass.ds(b, 1)].rearrange("o (t p) c -> p (o t) c", p=P)

            def body(b, attend, prepare, fetch):
                it = b + 1
                if attend:
                    sp.dma_start(xres[:, :, :], rows(x, b)).then_inc(xres_in, 16)
                if prepare and fetch:
                    sp.wait_ge(xn_ready, T)
                    sp.dma_start(xin[:, :, :], rows(x, b + 2)).then_inc(xin_in, 16)
                if prepare and fetch:
                    sp.wait_ge(xin_in, (b + 3) * 16)
                    sp.sem_inc(fetched, 1)
                if attend:
                    sp.wait_ge(xres_in, (b + 1) * 16)
                    sp.wait_ge(stored, (b + PRIME) * 16)
                    sp.sem_inc(last_add, 1)
                    for s in (("b_w0",), ("b_w1a",)):
                        fills(attend, prepare, fetch)[0].wait_drained(sp, s)
                    sp.dma_start(rows(x1, b), x1b[:, :, :]).then_inc(stored, 16)
                sp.wait_ge(arrive, 4)
                sp.sem_clear(range(first, last + 1))
                sp.sem_inc(go, 1)

            PRIME = 1
            sp.sem_inc(stored, 16)
            body(-1, False, True, True)
            if batches > 2:
                with sp.Fori(0, batches - 2) as b:
                    body(b, True, True, True)
            body(batches - 2, True, True, False)
            body(batches - 1, True, False, False)
            sp.wait_ge(stored, (batches + PRIME) * 16)
            sp.wait_ge(passed, 4 * (batches + 1))

        @block.gpsimd
        def _(pool):
            own = [0]

            def link(ins):
                own[0] += 1
                ins.then_inc(s_own["pool"], 1)
                pool.wait_ge(s_own["pool"], own[0])

            pool.wait_ge(const_in, 48)
            def body(b, attend, prepare, fetch):
                own[0] = 0
                fb, fa = fills(attend, prepare, fetch)
                for s in self_stages(attend, prepare, fetch):
                    kind, a = s[0], s[1:]
                    if kind == "a_norm":
                        pool.wait_ge(guess, 1 + (not attend and a[0]))
                        for n in range(3):
                            link(nc.gpsimd.tensor_tensor(nt[:, :], rstd[:, :], rstd[:, :], ALU.mult))
                            link(nc.gpsimd.tensor_tensor(nt[:, :], nt[:, :], var[:, :], ALU.mult))
                            link(nc.gpsimd.tensor_scalar(nt[:, :], nt[:, :], -0.5, 1.5, ALU.mult, ALU.add))
                            i = nc.gpsimd.tensor_tensor(rstd[:, :], rstd[:, :], nt[:, :], ALU.mult)
                            if n < 2:
                                link(i)
                            else:
                                i.then_inc(rstd_ready, 1)
                    elif kind == "a_ix":
                        t, = a
                        pool.wait_ge(ist_hi, t + 1)
                        nc.gpsimd.tensor_scalar(wt1[:, t, :], wth[:, t, :], 1.0, None, ALU.add).then_inc(wt_ready, 1)
                    elif kind == "b_pj":
                        g, t = a
                        n = g * T + t
                        pool.wait_ge(turned, n + 1)
                        if g:
                            pool.wait_ge(stacked, n - 1)
                        nc.gpsimd.tensor_tensor(rs[:, t, :], t1[:, t, :], t2[:, t, :], ALU.add).then_inc(summed, 1)
                    elif kind == "b_r":
                        g, t = a
                        n = g * T + t
                        q = rs[:, t, 0:RG * D].rearrange("p (h d) -> p h d", d=D)
                        qs = st[:, t, 0:RG * 2 * D].rearrange("p (h s d) -> p h s d", s=2, d=D)
                        k, ks = rs[:, t, RG * D:ROT], st[:, t, RG * 2 * D:ST].rearrange("p (s d) -> p s d", d=D)
                        pool.wait_ge(rounded, n + 1)
                        nc.gpsimd.tensor_tensor(qs[:, :, 1, :], q, qs[:, :, 0, :].bitcast(F), ALU.subtract)
                        nc.gpsimd.tensor_tensor(ks[:, 1, :], k, ks[:, 0, :].bitcast(F), ALU.subtract)\
                            .then_inc(stacked, 1)
                    elif kind == "b_v":
                        g, t = a
                        n = g * T + t
                        pool.wait_ge(va_hi, n + 1)
                        nc.gpsimd.tensor_tensor(va["l"][:, t, g, :, :], vf[:, g % 2, t, :].unsqueeze(1).broadcast_to([P, 2, D]),
                                                va["h"][:, t, g, :, :].bitcast(F), ALU.subtract).then_inc(va_ready, 1)
                    elif kind == "b_n":
                        u, = a
                        pool.wait_ge(rinv_ready, u + 1)
                        two = pr[:, u % 2, 2:4, :]
                        nc.gpsimd.tensor_tensor(two, two, rinv[:, u % 2, 2:4].unsqueeze(2).broadcast_to([P, 2, L]),
                                                ALU.mult).then_inc(pr_ready[1], 1)
                    elif kind == "b_h":
                        u, = a
                        g, t = u // T, u % T
                        pool.wait_ge(ot_hi, u + 1)
                        to = [ot[k][:, 2 * g:2 * g + 2, t * P:(t + 1) * P] for k in "hl"]
                        nc.gpsimd.tensor_tensor(to[1], on[:, u % 2, :, :], to[0].bitcast(F), ALU.subtract)\
                            .then_inc(ot_ready, 1)
            iterations(pool, body)

        @block.scalar
        def _(act):
            for n, (o, m) in enumerate(chunks):
                act.wait_ge(stage_in[n % 2], 16 * (n // 2 + 1))
                nc.scalar.activation(wh[:, o:o + m], stage[n % 2][:, 0:m], ACT.Copy).then_inc(w_hi, 1)
            act.wait_ge(const_in, 48)
            act.wait_ge(split, len(chunks) + 1)

            def body(b, attend, prepare, fetch):
                fb, fa = fills(attend, prepare, fetch)
                for s in self_stages(attend, prepare, fetch):
                    kind, a = s[0], s[1:]
                    if kind == "a_xt":
                        fa.wait_full(act, s)
                        if attend:
                            fb.wait_full(act, ("b_pj", 0, 1))
                            act.wait_ge(xct_ready, 2)
                        nc.scalar.activation(xnt["h"][:, :, :], fa.bank(s)[:, :].rearrange("p (c l) -> p c l", l=L),
                                             ACT.Copy).then_inc(xnt_hi, 1)
                    elif kind == "a_ix":
                        t, = a
                        fa.wait_full(act, s)
                        ps = fa.bank(s)
                        hs = ist[:, t, 0:HI * 2 * D].rearrange("p (h s d) -> p h s d", s=2, d=D)
                        ks = ist[:, t, HI * 2 * D:ST].rearrange("p (s d) -> p s d", d=D)
                        nc.scalar.activation(hs[:, :, 0, :], ps[:, 0:HI * D].rearrange("p (h d) -> p h d", d=D), ACT.Copy)
                        nc.scalar.activation(ks[:, 0:3:2, :], ps[:, HI * D:HI * D + D].unsqueeze(1).broadcast_to([P, 2, D]),
                                             ACT.Copy)
                        nc.scalar.activation(wth[:, t, :], ps[:, HI * D + D:NIDX], ACT.Tanh, scale=0.5).then_inc(ist_hi, 1)
                    elif kind == "a_iqx":
                        j, = a
                        fa.wait_full(act, s)
                        fa.drained(nc.scalar.activation(iqt[:, 2 * j:2 * j + 2, :],
                                   fa.bank(s)[:, :].rearrange("p (h l) -> p h l", l=L), ACT.Copy), s)
                    elif kind == "a_ikx":
                        fa.wait_full(act, s)
                        fa.drained(nc.scalar.activation(ikt[:, :, :],
                                   fa.bank(s)[:, :].rearrange("p (h l) -> p h l", l=L), ACT.Copy), s)
                    elif kind == "a_si":
                        t, j = a
                        fa.wait_full(act, s)
                        if t:
                            act.wait_ge(sig_used, j + 1)
                        for i in range(2):
                            h = 2 * j + i
                            ins = nc.scalar.activation(sig[:, j, i, :], fa.bank(s)[:, i * L:(i + 1) * L], ACT.Tanh,
                                                       bias=half[:, K_BI + h:K_BI + h + 1], scale=0.5)
                        fa.drained(ins, s)
                    elif kind == "b_vg":
                        fb.wait_drained(act, s)
                        nc.scalar.activation(vg[:, :, :], vg[:, :, :], ACT.Tanh, scale=0.5).then_inc(vg_ready, 1)
                    elif kind == "b_cp":
                        nc.scalar.activation(xct["h"][:, :, :], xnt["h"][:, :, :].bitcast(F), ACT.Copy)\
                            .then_inc(xct_ready, 1)
                    elif kind == "b_og":
                        j, = a
                        fb.wait_full(act, s)
                        for i in range(2):
                            m = 2 * j + i
                            ins = nc.scalar.activation(g1t[:, m, :], fb.bank(s)[:, i * L:(i + 1) * L], ACT.Tanh,
                                                       bias=half[:, K_BOG + m:K_BOG + m + 1], scale=0.5)
                        fb.drained(ins, s)
                    elif kind == "b_r":
                        g, t = a
                        n = g * T + t
                        act.wait_ge(summed, n + 1)
                        if g:
                            fb.wait_full(act, ("b_qx", g - 1, RG // 2 - 1))
                        q = rs[:, t, 0:RG * D].rearrange("p (h d) -> p h d", d=D)
                        qs = st[:, t, 0:RG * 2 * D].rearrange("p (h s d) -> p h s d", s=2, d=D)
                        k, ks = rs[:, t, RG * D:ROT], st[:, t, RG * 2 * D:ST].rearrange("p (s d) -> p s d", d=D)
                        nc.scalar.activation(qs[:, :, 0, :], q, ACT.Copy)
                        nc.scalar.activation(ks[:, 0:3:2, :], k.unsqueeze(1).broadcast_to([P, 2, D]), ACT.Copy)\
                            .then_inc(rounded, 1)
                    elif kind == "b_v":
                        g, t = a
                        fb.wait_drained(act, ("b_pj", g, t))
                        nc.scalar.activation(va["h"][:, t, g, :, :], vf[:, g % 2, t, :].unsqueeze(1).broadcast_to([P, 2, D]),
                                             ACT.Copy).then_inc(va_hi, 1)
                    elif kind == "b_kx":
                        g, = a
                        fb.wait_full(act, s)
                        fb.drained(nc.scalar.activation(kt[:, g % 2, :, :],
                                   fb.bank(s)[:, :].rearrange("p (h l) -> p h l", l=L), ACT.Copy), s)
                    elif kind == "b_qx":
                        g, j = a
                        fb.wait_full(act, s)
                        fb.drained(nc.scalar.activation(qt[:, g % 2, 2 * j:2 * j + 2, :],
                                   fb.bank(s)[:, :].rearrange("p (h l) -> p h l", l=L), ACT.Copy), s)
                    elif kind == "b_e":
                        u, = a
                        act.wait_ge(nm_ready, u + 1)
                        if u >= 2:
                            fb.wait_full(act, ("b_t", u - 2, 1))
                        for h in range(RG):
                            ins = nc.scalar.activation(pr[:, u % 2, h, :], sm[:, u % 2, h, :], ACT.Exp,
                                                       bias=nm[:, u % 2, h:h + 1], scale=SCALE,
                                                       accum_out=rsum[:, u % 2, h:h + 1])
                        ins.then_inc(exp_done, 1)
                    elif kind == "b_t":
                        u, j = a
                        fb.wait_full(act, s)
                        if u >= 2:
                            fb.wait_full(act, ("b_o", u - 2))
                        nc.scalar.activation(pt["h"][:, u % 2, :, j * 2 * P:(j + 1) * 2 * P],
                                             fb.bank(s)[:, :].rearrange("p (k n) -> p k n", k=T), ACT.Copy)\
                            .then_inc(pt_hi, 1)
                    elif kind == "b_h":
                        u, = a
                        g, t = u // T, u % T
                        act.wait_ge(on_ready, u + 1)
                        fb.wait_drained(act, ("b_o", u))
                        nc.scalar.activation(ot["h"][:, 2 * g:2 * g + 2, t * P:(t + 1) * P], on[:, u % 2, :, :], ACT.Copy)\
                            .then_inc(ot_hi, 1)
            iterations(act, body)

        @block.vector
        def _(dve):
            own = [0]

            def link(ins):
                own[0] += 1
                ins.then_inc(s_own["dve"], 1)
                dve.wait_ge(s_own["dve"], own[0])

            for n, (o, m) in enumerate(chunks):
                dve.wait_ge(w_hi, n + 1)
                nc.vector.tensor_tensor(wl[:, o:o + m], stage[n % 2][:, 0:m], wh[:, o:o + m].bitcast(F),
                                        ALU.subtract).then_inc(split, 1)
            dve.wait_ge(const_in, 48)
            nc.vector.tensor_scalar(half[:, :], cst[:, :], 0.5, None, ALU.mult).then_inc(split, 1)
            dve.wait_ge(xin_in, 16)

            def body(b, attend, prepare, fetch):
                own[0] = 0
                fb, fa = fills(attend, prepare, fetch)
                for s in self_stages(attend, prepare, fetch):
                    kind, a = s[0], s[1:]
                    if kind == "a_norm":
                        if a[0]:
                            dve.wait_ge(fetched, 1)
                        for t in range(T):
                            i = nc.vector.bn_stats(stats[:, t, :], xin[:, t, :])
                        link(i)
                        for t in range(T):
                            i = nc.vector.bn_aggr(mv[:, t, :], stats[:, t, :])
                        link(i)
                        link(nc.vector.tensor_scalar(var[:, :], mv[:, :, 1], EPS, None, ALU.add))
                        link(nc.vector.tensor_scalar(nt[:, :].bitcast(I32), var[:, :].bitcast(I32), 1, None,
                                                     ALU.logical_shift_right))
                        nc.vector.tensor_scalar(rstd[:, :].bitcast(I32), nt[:, :].bitcast(I32), -1.0, float(MAGIC),
                                                ALU.mult, ALU.add).then_inc(guess, 1)
                    elif kind == "a_xn":
                        if not attend:
                            dve.wait_ge(rstd_ready, 1)
                        for t in range(T):
                            nc.vector.tensor_scalar(xn[:, t, :], xin[:, t, :], mv[:, t, 0:1], rstd[:, t:t + 1],
                                                    ALU.subtract, ALU.mult).then_inc(xn_ready, 1)
                    elif kind == "a_xt":
                        dve.wait_ge(xnt_hi, 1)
                        fa.drained(nc.vector.tensor_tensor(xnt["l"][:, :, :],
                                   fa.bank(s)[:, :].rearrange("p (c l) -> p c l", l=L),
                                   xnt["h"][:, :, :].bitcast(F), ALU.subtract), s)
                    elif kind == "a_ix":
                        t, = a
                        dve.wait_ge(ist_hi, t + 1)
                        ps = fa.bank(s)
                        hs = ist[:, t, 0:HI * 2 * D].rearrange("p (h s d) -> p h s d", s=2, d=D)
                        ks = ist[:, t, HI * 2 * D:ST].rearrange("p (s d) -> p s d", d=D)
                        nc.vector.tensor_tensor(hs[:, :, 1, :], ps[:, 0:HI * D].rearrange("p (h d) -> p h d", d=D),
                                                hs[:, :, 0, :].bitcast(F), ALU.subtract)
                        fa.drained(nc.vector.tensor_tensor(ks[:, 1, :], ps[:, HI * D:HI * D + D],
                                                           ks[:, 0, :].bitcast(F), ALU.subtract), s)
                    elif kind == "a_sc":
                        t, j = a
                        if j == 0:
                            dve.wait_ge(wt_ready, t + 1)
                        fa.wait_drained(dve, ("a_si", t, j))
                        for i in range(2):
                            h = 2 * j + i
                            wt = wt1[:, t, h:h + 1]
                            if h == 0:
                                ins = nc.vector.tensor_scalar(score[:, t, :], sig[:, j, i, :], wt, None, ALU.mult)
                            else:
                                ins = nc.vector.scalar_tensor_tensor(score[:, t, :], sig[:, j, i, :], wt,
                                                                     score[:, t, :], ALU.mult, ALU.add)
                            if i == 0:
                                link(ins)
                            else:
                                ins.then_inc(sig_used, 1)
                                dve.wait_ge(sig_used, 2 * t + j + 1)
                    elif kind in ("a_tk", "b_tk"):
                        for t in range(T):
                            nc.vector.max(top8[:, t, :], score[:, t, :]).then_inc(s_own["dve"], 1)
                        for t in range(T):
                            own[0] += 1
                            dve.wait_ge(s_own["dve"], own[0])
                            nc.vector.match_replace(score[:, t, :], top8[:, t, :], score[:, t, :], TAKEN)\
                                .then_inc(s_own["dve"], 1)
                        own[0] += T
                        dve.wait_ge(s_own["dve"], own[0])
                    elif kind == "b_cp":
                        nc.vector.tensor_copy(xct["l"][:, :, :], xnt["l"][:, :, :].bitcast(F)).then_inc(xct_ready, 1)
                    elif kind == "b_mk":
                        link(nc.vector.tensor_scalar(mb[:, :, :], score[:, :, :], TAKEN / 2, MASKED, ALU.is_ge, ALU.mult))
                    elif kind == "b_vg":
                        fb.wait_full(dve, s)
                        ins = nc.vector.tensor_tensor(vg[:, :, :], fb.bank(s)[:, :].rearrange("p (t n) -> p t n", t=T),
                                                      cst[:, K_BVG:K_BVG + G * D].unsqueeze(1).broadcast_to([P, T, G * D]),
                                                      ALU.add)
                        fb.drained(ins, s)
                    elif kind == "b_pj":
                        g, t = a
                        n = g * T + t
                        fb.wait_full(dve, s)
                        if g:
                            dve.wait_ge(summed, n - 1)
                        ps = fb.bank(s)
                        r5 = ps[:, 0:ROT].rearrange("p (h s d) -> p h s d", s=2, d=D // 2)
                        o5 = t2[:, t, :].rearrange("p (h s d) -> p h s d", s=2, d=D // 2)
                        nc.vector.tensor_tensor(t1[:, t, :].rearrange("p (h d) -> p h d", d=D),
                                                ps[:, 0:ROT].rearrange("p (h d) -> p h d", d=D),
                                                cs[:, t, 0, :].unsqueeze(1).broadcast_to([P, RG + 1, D]), ALU.mult)
                        nc.vector.tensor_tensor(o5, r5[:, :, ::-1, :],
                                                cs[:, t, 1, :].rearrange("p (s d) -> p s d", s=2).unsqueeze(1)
                                                .broadcast_to([P, RG + 1, 2, D // 2]), ALU.mult).then_inc(turned, 1)
                        if n == 0:
                            dve.wait_ge(vg_ready, 1)
                        if g >= 2:
                            dve.wait_ge(va_ready, n - 3)
                        fb.drained(nc.vector.scalar_tensor_tensor(vf[:, g % 2, t, :], vg[:, t, g * D:(g + 1) * D], 1.0,
                                                                  ps[:, ROT:NPJ], ALU.add, ALU.mult), s)
                    elif kind == "b_s":
                        u, j = a
                        t = u % T
                        fb.wait_full(dve, s)
                        if u >= 2 and j == 0:
                            dve.wait_ge(exp_done, u - 1)
                        for i in range(2):
                            h = 2 * j + i
                            ins = nc.vector.tensor_tensor_reduce(
                                out=sm[:, u % 2, h, :], in0=fb.bank(s)[:, i * L:(i + 1) * L], in1=mb[:, t, :],
                                scale=1.0, scalar=LOWEST, op0=ALU.add, op1=ALU.max, accum_out=mx[:, u % 2, h:h + 1])
                        fb.drained(ins, s)
                        if j == 1:
                            fb.wait_drained(dve, s)
                            nc.vector.tensor_scalar(nm[:, u % 2, :], mx[:, u % 2, :], -SCALE, None, ALU.mult)\
                                .then_inc(nm_ready, 1)
                    elif kind == "b_n":
                        u, = a
                        dve.wait_ge(exp_done, u + 1)
                        nc.vector.reciprocal(rinv[:, u % 2, :], rsum[:, u % 2, :]).then_inc(rinv_ready, 1)
                        dve.wait_ge(rinv_ready, u + 1)
                        for h in range(2):
                            ins = nc.vector.tensor_scalar(pr[:, u % 2, h, :], pr[:, u % 2, h, :],
                                                          rinv[:, u % 2, h:h + 1], None, ALU.mult)
                        ins.then_inc(pr_ready[0], 1)
                    elif kind == "b_l":
                        u, j = a
                        dve.wait_ge(pt_hi, 2 * u + j + 1)
                        to = [pt[k][:, u % 2, :, j * 2 * P:(j + 1) * 2 * P] for k in "hl"]
                        fb.drained(nc.vector.tensor_tensor(
                            to[1], fb.bank(("b_t", u, j))[:, :].rearrange("p (k n) -> p k n", k=T), to[0].bitcast(F),
                            ALU.subtract), ("b_t", u, j))
                    elif kind == "b_g":
                        u, = a
                        g, t = u // T, u % T
                        if u == 0:
                            for j in range(HT // 2):
                                fb.wait_drained(dve, ("b_og", j))
                        fb.wait_full(dve, ("b_o", u))
                        if u >= 2:
                            dve.wait_ge(ot_ready, u - 1)
                        o = fb.bank(("b_o", u))[:, :].rearrange("p (i v q) -> p i v q", v=2, q=P)
                        for v, part in enumerate((slice(0, D), slice(D, P))):
                            ins = nc.vector.scalar_tensor_tensor(
                                on[part, u % 2, :, :], g1t[part, 2 * g:2 * g + 2, t * P:(t + 1) * P], 1.0,
                                o[part, :, v, :], ALU.add, ALU.mult)
                            if v == 0:
                                ins.then_inc(on_ready, 1)
                        fb.drained(ins, ("b_o", u))
                    elif kind in ("b_w0", "b_w1b"):
                        t = int(kind == "b_w1b")
                        s = ("b_w1a",) if t else s
                        fb.wait_full(dve, s)
                        if t == 0:
                            dve.wait_ge(last_add, 1)
                        fb.drained(nc.vector.scalar_tensor_tensor(x1b[:, t, :], fb.bank(s)[:, 0:C], 0.25, xres[:, t, :],
                                                                  ALU.mult, ALU.add), s)
            iterations(dve, body)

        @block.tensor
        def _(pe):
            pe.wait_ge(split, len(chunks))
            pe.wait_ge(const_in, 48)

            def mm(out, lhs, rhs, start, stop):
                return nc.tensor.matmul(out, lhs, rhs, start=start, stop=stop)

            def project(out, lhs, rhs, tiles, start=True, stop=True):
                pairs = [(c, a, b) for c in (range(tiles) if isinstance(tiles, int) else tiles) for a, b in PRODUCTS]
                for n, (c, a, b) in enumerate(pairs):
                    ins = mm(out, lhs(a, c), rhs(b, c), start and n == 0, stop and n == len(pairs) - 1)
                return ins

            def weight(o, width, at, n):
                return lambda k, c: w[k][:, o + c * width + at:o + c * width + at + n]

            def body(b, attend, prepare, fetch):
                fb, fa = fills(attend, prepare, fetch)
                for s in self_stages(attend, prepare, fetch):
                    kind, a = s[0], s[1:]
                    if kind == "a_xt":
                        pe.wait_ge(xn_ready, T)
                        fa.wait_free(pe, s)
                        for c in range(CT):
                            for t in range(T):
                                o = c * L + t * P
                                ins = nc.tensor.transpose(fa.bank(s)[:, o:o + P], xn[:, t, c * P:(c + 1) * P], idn[:, :])
                        fa.filled(ins, s)
                    elif kind == "a_ix":
                        t, = a
                        fa.wait_drained(pe, ("a_xt",))
                        fa.wait_free(pe, s)
                        fa.filled(project(fa.bank(s)[:, 0:NIDX], lambda k, c: xnt[k][:, c, t * P:(t + 1) * P],
                                          weight(O_IDX, NIDX, 0, NIDX), CT), s)
                    elif kind == "a_iqx":
                        j, = a
                        for t in range(T):
                            fa.wait_drained(pe, ("a_ix", t))
                        fa.wait_free(pe, s)
                        for i in range(2):
                            for t in range(T):
                                o = i * L + t * P
                                h = 2 * j + i
                                ins = nc.tensor.transpose(fa.bank(s)[:, o:o + P],
                                                          ist[:, t, h * P:(h + 1) * P].bitcast(F), idn[:, :])
                        fa.filled(ins, s)
                    elif kind == "a_ikx":
                        fa.wait_free(pe, s)
                        for i in range(2):
                            for t in range(T):
                                o, f = i * L + t * P, HI * 2 * D + i * D
                                ins = nc.tensor.transpose(fa.bank(s)[:, o:o + P], ist[:, t, f:f + P].bitcast(F), idn[:, :])
                        fa.filled(ins, s)
                    elif kind == "a_si":
                        t, j = a
                        fa.wait_drained(pe, ("a_ikx",))
                        fa.wait_drained(pe, ("a_iqx", j))
                        fa.wait_free(pe, s)
                        for i in range(2):
                            for k in range(2):
                                ins = mm(fa.bank(s)[:, i * L:(i + 1) * L], iqt[:, 2 * j + i, t * P:(t + 1) * P],
                                         ikt[:, k, :], k == 0, k == 1)
                        fa.filled(ins, s)
                    elif kind == "b_vg":
                        for t in range(T):
                            ins = project(fb.bank(s)[:, t * L:(t + 1) * L], lambda k, c: xnt[k][:, c, t * P:(t + 1) * P],
                                          weight(O_VG, G * D, 0, G * D), CT)
                        fb.filled(ins, s)
                    elif kind == "b_og":
                        j, = a
                        pe.wait_ge(xct_ready, 2)
                        fb.wait_free(pe, s)
                        for i in range(2):
                            ins = project(fb.bank(s)[:, i * L:(i + 1) * L], weight(O_OG, H * D, (2 * j + i) * P, P),
                                          lambda k, c: xct[k][:, c, :], CT)
                        fb.filled(ins, s)
                    elif kind == "b_pj":
                        g, t = a
                        src = xct if g else xnt
                        if g:
                            pe.wait_ge(xct_ready, 2)
                        fb.wait_free(pe, s)
                        fb.filled(project(fb.bank(s)[:, 0:NPJ], lambda k, c: src[k][:, c, t * P:(t + 1) * P],
                                          weight(O_PJ, G * NPJ, g * NPJ, NPJ), CT), s)
                    elif kind == "b_kx":
                        g, = a
                        pe.wait_ge(stacked, T * (g + 1))
                        fb.wait_free(pe, s)
                        for i in range(2):
                            for t in range(T):
                                o, f = i * L + t * P, RG * 2 * D + i * D
                                ins = nc.tensor.transpose(fb.bank(s)[:, o:o + P], st[:, t, f:f + P].bitcast(F), idn[:, :])
                        fb.filled(ins, s)
                    elif kind == "b_qx":
                        g, j = a
                        fb.wait_free(pe, s)
                        for i in range(2):
                            for t in range(T):
                                o, h = i * L + t * P, 2 * j + i
                                ins = nc.tensor.transpose(fb.bank(s)[:, o:o + P], st[:, t, h * P:(h + 1) * P].bitcast(F),
                                                          idn[:, :])
                        fb.filled(ins, s)
                    elif kind == "b_s":
                        u, j = a
                        g, t = u // T, u % T
                        fb.wait_drained(pe, ("b_kx", g))
                        fb.wait_drained(pe, ("b_qx", g, j))
                        fb.wait_free(pe, s)
                        for i in range(2):
                            for k in range(2):
                                ins = mm(fb.bank(s)[:, i * L:(i + 1) * L], qt[:, g % 2, 2 * j + i, t * P:(t + 1) * P],
                                         kt[:, g % 2, k, :], k == 0, k == 1)
                        fb.filled(ins, s)
                    elif kind == "b_t":
                        u, j = a
                        pe.wait_ge(pr_ready[j], u + 1)
                        fb.wait_free(pe, s)
                        for k in range(T):
                            for i in range(2):
                                o = k * 2 * P + i * P
                                ins = nc.tensor.transpose(fb.bank(s)[:, o:o + P],
                                                          pr[:, u % 2, 2 * j + i, k * P:(k + 1) * P], idn[:, :])
                        fb.filled(ins, s)
                    elif kind == "b_o":
                        u, = a
                        g = u // T
                        for j in range(2):
                            fb.wait_drained(pe, ("b_t", u, j))
                        pe.wait_ge(va_ready, T * (g + 1))
                        fb.wait_free(pe, s)
                        fb.filled(project(fb.bank(s)[:, :], lambda m, k: va[m][:, k, g, :, :].rearrange("p a d -> p (a d)"),
                                          lambda m, k: pt[m][:, u % 2, k, :], T), s)
                    elif kind == "b_w0":
                        pe.wait_ge(ot_ready, G * T - 1)
                        fb.wait_free(pe, s)
                        fb.filled(project(fb.bank(s)[:, 0:C], lambda k, c: ot[k][:, c, 0:P], weight(O_WO, C, 0, C), HT), s)
                    elif kind == "b_w1a":
                        pe.wait_ge(ot_ready, G * T - T)
                        fb.wait_free(pe, s)
                        project(fb.bank(s)[:, 0:C], lambda k, c: ot[k][:, c, P:2 * P], weight(O_WO, C, 0, C),
                                range(0, HT - 2), stop=False)
                    elif kind == "b_w1b":
                        pe.wait_ge(ot_ready, G * T)
                        fb.filled(project(fb.bank(("b_w1a",))[:, 0:C], lambda k, c: ot[k][:, c, P:2 * P],
                                          weight(O_WO, C, 0, C), range(HT - 2, HT), start=False), ("b_w1a",))
            iterations(pe, body)


LC = 120
HX, DX = 16, 16
HPT = P // DX
HC = 4
XSCALE = DX ** -0.5
NEG = 1.0e9
E, I = 8, 128
NGRP, TOPG, TOPK = 4, 2, 2
GSZ = E // NGRP

O_XQ = 0
O_XK = O_XQ + CT * C
O_XV = O_XK + CT * C
O_XO = O_XV + CT * C
O_GT = O_XO + CT * C
O_G = O_GT + CT * E
O_U = O_G + CT * E * I
O_DN = O_U + CT * E * I
N_W2 = O_DN + E * C

K_XQB = 0
K_XKB = K_XQB + CT
K_XVB = K_XKB + CT
K_XOB = K_XVB + C
K_ESB = K_XOB + C
K_BD = K_ESB + E
K_TRI = K_BD + HPT
K_TRG = K_TRI + E * E
N_K2 = K_TRG + NGRP * NGRP


RT = 20


def cross_stages(feed, prepare, fetch):
    out = []
    routing = [("f_rt", n) for n in range(RT)] if feed else []

    def f(*stages):
        out.extend(stages if feed else ())

    def c(*stages):
        out.extend(stages if prepare else ())

    def keys(k):
        c(("c_ct", k), ("c_kv", k), ("c_kb", k))

    def route(n):
        out.extend(routing[:n])
        del routing[:n]

    if not feed:
        c(("c_norm", 0), ("c_ct", 0), ("c_kv", 0), ("c_kb", 0, 0), ("c_kb", 0, 1), ("c_v", 0), ("c_xn", 0), ("c_xt", 0))
        c(("c_q", 0, 0), ("c_q", 0, 1))
    units = [(i, t) for i in range(HX // HC) for t in range(T)]
    last = len(units) - 1

    def ahead(*stages):
        c(*(stages if fetch else ()))

    def logits(n):
        if n <= last:
            c(("c_l",) + units[n])
            if n >= 2:
                route(2)
            c(("c_lx",) + units[n])

    c(("c_ng",))
    logits(0)
    f(("f_gt",), ("f_gu", 0), ("f_cp",))
    logits(1)
    f(("f_g2",), ("f_gv", 0))
    c(("c_xb",))
    gates = {0: 1, 1: 2, 2: 3, 3: 4, 4: 5, 6: 6}
    for n, u in enumerate(units):
        logits(n + 2)
        c(("c_e",) + u)
        if n >= 6:
            f(("f_hh", 2 * (n - 6)), ("f_hh", 2 * (n - 6) + 1))
        if n >= 1:
            c(("c_r",) + units[n - 1])
        if n in gates:
            f(("f_gu", gates[n]))
        if n >= 1:
            c(("c_m",) + units[n - 1])
        if n in gates:
            f(("f_gv", gates[n]))
        if n:
            route(4)
        if n >= 2:
            c(("c_p",) + units[n - 2])
        if n == 1:
            ahead(("c_ct", 1))
        if n == 2:
            ahead(("c_kv", 1))
        if n == 3:
            ahead(("c_kb", 1, 0))
        if n == 5:
            ahead(("c_kb", 1, 1))
        if n >= 5:
            m = n - 5
            f(("f_cb", m), ("f_h", 2 * m), ("f_h", 2 * m + 1))
        if n == 6:
            c(("c_o", 0))
    f(("f_hh", 4), ("f_hh", 5))
    c(("c_r",) + units[-1], ("c_m",) + units[-1], ("c_ol", 0), ("c_p",) + units[-2])
    f(("f_gu", 7), ("f_cb", 3))
    c(("c_p",) + units[-1])
    f(("f_gv", 7), ("f_h", 6), ("f_h", 7))
    ahead(("c_norm", 1))
    c(("c_o", 1))
    f(("f_hh", 6), ("f_hh", 7))
    c(("c_ol", 1))
    ahead(("c_xn", 1), ("c_xt", 1))
    c(("c_w",), ("c_n2",), ("c_x2",))
    ahead(("c_q", 1, 0), ("c_q", 1, 1))
    f(("f_dn", 0), ("f_dn", 1))
    c(("c_x3",))
    ahead(("c_v", 1))
    return out


def cross_and_feed(nc, keep, x1, ctxt, gp, mask, out, w2, k2, ident, batches=B):
    with ExitStack() as ctx:
        def sb(name, shape, dt=F):
            return ctx.enter_context(nc.sbuf_tensor("x_" + name, shape, dt))

        sems = []

        def sem(name):
            sems.append(keep.enter_context(nc.semaphore("x_" + name)))
            return sems[-1]

        wh, wl = sb("wh", [P, N_W2], R), sb("wl", [P, N_W2], R)
        w = {"h": wh, "l": wl}
        cst = sb("cst", [P, N_K2])
        idn = sb("idn", [P, P])
        qb4 = sb("qb4", [P, CT])
        xin = sb("xin", [P, T, C])
        cin = sb("cin", [P, C])
        gpt = sb("gpt", [P, T, LC])
        mi = sb("mi", [P, T, LC], I32)
        neg = sb("neg", [P, T, LC])
        stats, mv = sb("stats", [P, T, 6]), sb("mv", [P, T, 2])
        var, rstd, nt = sb("var", [P, T]), sb("rstd", [P, T]), sb("nt", [P, T])
        stats2, mv2 = sb("stats2", [P, T, 6]), sb("mv2", [P, T, 2])
        var2, rstd2, nt2 = sb("var2", [P, T]), sb("rstd2", [P, T]), sb("nt2", [P, T])
        xn = sb("xn", [P, T, C])
        xnt = {k: sb("xnt" + k, [P, CT, L], R) for k in "hl"}
        ctt = {k: sb("ctt" + k, [P, CT, LC], R) for k in "hl"}
        kf = sb("kf", [P, CT, LC])
        kr = {k: sb("kr" + k, [P, CT, LC], R) for k in "hl"}
        kbd = {k: sb("kbd" + k, [P, CT, HPT, LC], R) for k in "hl"}
        vf = sb("vf", [P, C])
        vpad = sb("vpad", [P, CT, HPT, P])
        qf = sb("qf", [P, CT, L])
        qx = {k: sb("qx" + k, [P, CT, L], R) for k in "hl"}
        lm = sb("lm", [P, T, HX, LC])
        mx, nmx = sb("mx", [P, T, HX]), sb("nmx", [P, T, HX])
        sm, rs = sb("sm", [P, T, HX]), sb("rs", [P, T, HX])
        ptc = sb("ptc", [P, HX, L])
        ox = {k: sb("ox" + k, [P, CT, L], R) for k in "hl"}
        xres, xb = sb("xres", [P, T, C]), sb("xb", [P, T, C])
        x2n = sb("x2n", [P, T, C])
        x2t = {k: sb("x2t" + k, [P, CT, L], R) for k in "hl"}
        x2c = sb("x2c", [P, T, C])
        gl = sb("gl", [E, L])
        sc, sfc, tmp = sb("sc", [P, T, E]), sb("sfc", [P, T, E]), sb("tmp", [P, T, E])
        gs, gm = sb("gs", [P, T, NGRP]), sb("gm", [P, T, NGRP])
        c1, c2 = sb("c1", [P, T, E, E]), sb("c2", [P, T, E, E])
        rk, cw = sb("rk", [P, T, E]), sb("cw", [P, T, E])
        ws, wr = sb("ws", [P, T]), sb("wr", [P, T])
        sg = sb("sg", [P, 2, L])
        gs2 = sb("gs2", [P, 2, L])
        hu = sb("hu", [P, E, L])
        hf = sb("hf", [P, 4, L])
        hr = {k: sb("hr" + k, [P, E, L], R) for k in "hl"}
        ob = sb("ob", [P, T, C])

        psb = [ctx.enter_context(nc.psum_tensor(f"x_ps{i}", [P, 512], F)) for i in range(8)]
        full, free = [sem(f"full{i}") for i in range(8)], [sem(f"free{i}") for i in range(8)]
        s_own = {e: sem("own_" + e) for e in ("dve", "pool")}
        arrive, mi_here = sem("arrive"), sem("mi_here")
        guess, rstd_ready, xn_ready = sem("guess"), sem("rstd_ready"), sem("xn_ready")
        xin_read, xin_here, ctx_here = sem("xin_read"), sem("xin_here"), sem("ctx_here")
        v_ready, q_hi, rt_step, gs_ready = sem("v_ready"), sem("q_hi"), sem("rt_step"), sem("gs_ready")
        hr_hi, rs_ready = sem("hr_hi"), sem("rs_ready")
        ctt_hi, xnt_hi, ox_hi, x2t_hi = sem("ctt_hi"), sem("xnt_hi"), sem("ox_hi"), sem("x2t_hi")
        neg_ready, kf_ready, kbd_ready = sem("neg_ready"), sem("kf_ready"), sem("kbd_ready")
        qx_ready, nmx_ready, exp_done, pc_ready = sem("qx_ready"), sem("nmx_ready"), sem("exp_done"), sem("pc_ready")
        x2c_ready = sem("x2c_ready")
        sg_ready, hf_ready, hr_ready = sem("sg_ready"), sem("hf_ready"), sem("hr_ready")
        gp_here, xb_ready, last_add = sem("gp_here"), sem("xb_ready"), sem("last_add")
        xres_here = sem("xres_here")
        in_iteration = list(sems)
        go, passed = sem("go"), sem("passed")
        const_in, split, w_hi = sem("const_in"), sem("split"), sem("w_hi")
        stage_in = [sem("stage_in0"), sem("stage_in1")]
        xin_in, ctx_in, mi_in, gp_in, xres_in = (sem(n) for n in ("xin_in", "ctx_in", "mi_in", "gp_in", "xres_in"))
        stored, zeroed = sem("stored"), sem("zeroed")
        first, last = in_iteration[0].num, in_iteration[-1].num
        assert last - first == len(in_iteration) - 1

        def fills(feed, prepare, fetch):
            stages = cross_stages(feed, prepare, fetch)
            return (Fills(psb[0:4], full[0:4], free[0:4],
                          [s for s in stages if s[0] in ("f_gt", "f_g2", "f_gu", "f_cb", "f_dn")]),
                    Fills(psb[4:8], full[4:8], free[4:8],
                          [s for s in stages if s[0] in ("c_ct", "c_kv", "c_xt", "c_q", "c_l", "c_p", "c_o", "c_w", "c_x3")]))

        def iterations(eng, body):
            def meet(n):
                eng.drain().then_inc(arrive, 1)
                eng.wait_ge(go, n)
                eng.sem_inc(passed, 1)
            body(-1, False, True, True)
            meet(1)
            if batches > 2:
                with eng.Fori(0, batches - 2) as b:
                    body(b, True, True, True)
                    meet(b + 2)
            body(batches - 2, True, True, False)
            meet(batches)
            body(batches - 1, True, False, False)
            meet(batches + 1)

        def nth(feed, k):
            return 1 if feed else 1 + k

        CH = 1024
        stage = [ptc[:, :, :].rearrange("p a b -> p (a b)")[:, n * CH:(n + 1) * CH] for n in range(2)]
        chunks = [(o, min(CH, N_W2 - o)) for o in range(0, N_W2, CH)]

        block = ctx.enter_context(nc.Block())

        @block.sync
        def _(sp):
            def rows(t, b):
                return t[bass.ds(b, 1)].rearrange("o (t p) c -> p (o t) c", p=P)

            def fetch_x(b):
                sp.dma_start(xin[:, :, :], rows(x1, b)).then_inc(xin_in, 16)

            def fetch_context(b):
                sp.dma_start(cin[0:LC, :], ctxt[bass.ds(b, 1)].rearrange("o p c -> p (o c)")).then_inc(ctx_in, 16)

            def fetch_mask(b):
                sp.dma_start(mi[:, :, :], rows(mask, b)).then_inc(mi_in, 16)

            fetch_x(0)
            fetch_context(0)
            fetch_mask(0)
            for n, (o, m) in enumerate(chunks):
                if n >= 2:
                    sp.wait_ge(split, n - 1)
                sp.dma_start(stage[n % 2][:, 0:m], w2[:, o:o + m]).then_inc(stage_in[n % 2], 16)
            sp.dma_start(cst[:, :], k2).then_inc(const_in, 16)
            sp.dma_start(idn[:, :], ident).then_inc(const_in, 16)

            def body(b, feed, prepare, fetch):
                ff, fc = fills(feed, prepare, fetch)
                if prepare:
                    sp.dma_start(gpt[:, :, :], rows(gp, b + 1)).then_inc(gp_in, 16)
                    sp.dma_start(xres[:, :, :], rows(x1, b + 1)).then_inc(xres_in, 16)
                if prepare:
                    sp.wait_ge(gp_in, (b + 2) * 16)
                    sp.sem_inc(gp_here, 1)
                    sp.wait_ge(xres_in, (b + 2) * 16)
                    sp.sem_inc(xres_here, 1)
                if fetch:
                    if not feed:
                        fc.wait_full(sp, ("c_ct", 0))
                        sp.wait_ge(xin_read, 1)
                    fetch_context(b + 2)
                    fetch_x(b + 2)
                    sp.wait_ge(neg_ready, 1)
                    fetch_mask(b + 2)
                    for fetched, here in ((xin_in, xin_here), (ctx_in, ctx_here), (mi_in, mi_here)):
                        sp.wait_ge(fetched, (b + 3) * 16)
                        sp.sem_inc(here, 1)
                if feed:
                    sp.wait_ge(stored, (b + PRIME) * 16)
                    sp.sem_inc(last_add, 1)
                    ff.wait_drained(sp, ("f_dn", 0))
                    ff.wait_drained(sp, ("f_dn", 1))
                    sp.dma_start(rows(out, b), ob[:, :, :]).then_inc(stored, 16)
                sp.wait_ge(arrive, 4)
                sp.sem_clear(range(first, last + 1))
                sp.sem_inc(go, 1)

            PRIME = 1
            sp.sem_inc(stored, 16)
            body(-1, False, True, True)
            if batches > 2:
                with sp.Fori(0, batches - 2) as b:
                    body(b, True, True, True)
            body(batches - 2, True, True, False)
            body(batches - 1, True, False, False)
            sp.wait_ge(stored, (batches + PRIME) * 16)
            sp.wait_ge(passed, 4 * (batches + 1))

        @block.gpsimd
        def _(pool):
            own = [0]

            def link(ins):
                own[0] += 1
                ins.then_inc(s_own["pool"], 1)
                pool.wait_ge(s_own["pool"], own[0])

            nc.gpsimd.memset(vpad[:, :, :, :], 0.0).then_inc(zeroed, 1)
            pool.wait_ge(const_in, 32)

            def body(b, feed, prepare, fetch):
                own[0] = 0
                ff, fc = fills(feed, prepare, fetch)
                for s in cross_stages(feed, prepare, fetch):
                    kind, a = s[0], s[1:]
                    if kind == "c_norm":
                        pool.wait_ge(guess, nth(feed, a[0]))
                        for n in range(3):
                            link(nc.gpsimd.tensor_tensor(nt[:, :], rstd[:, :], rstd[:, :], ALU.mult))
                            link(nc.gpsimd.tensor_tensor(nt[:, :], nt[:, :], var[:, :], ALU.mult))
                            link(nc.gpsimd.tensor_scalar(nt[:, :], nt[:, :], -0.5, 1.5, ALU.mult, ALU.add))
                            i = nc.gpsimd.tensor_tensor(rstd[:, :], rstd[:, :], nt[:, :], ALU.mult)
                            if n < 2:
                                link(i)
                            else:
                                i.then_inc(rstd_ready, 1)
                    elif kind == "c_kb":
                        k, c = a
                        pool.wait_ge(kf_ready, nth(feed, k))
                        link(nc.gpsimd.tensor_copy(kr["h"][:, c, :], kf[:, c, :]))
                        link(nc.gpsimd.tensor_tensor(kr["l"][:, c, :], kf[:, c, :], kr["h"][:, c, :].bitcast(F), ALU.subtract))
                        if k:
                            fc.wait_full(pool, ("c_l", (c + 1) * HPT // HC - 1, T - 1))
                        for half in "hl":
                            ins = nc.gpsimd.tensor_tensor(
                                kbd[half][:, c, :, :],
                                kr[half][:, c, :].bitcast(F).unsqueeze(1).broadcast_to([P, HPT, LC]),
                                cst[:, K_BD:K_BD + HPT].unsqueeze(2).broadcast_to([P, HPT, LC]), ALU.mult)
                        ins.then_inc(kbd_ready, 1)
                    elif kind == "c_v":
                        k, = a
                        pool.wait_ge(kf_ready, nth(feed, k))
                        if k:
                            fc.wait_full(pool, ("c_o", CT - 1))
                        for c in range(CT):
                            to = vpad[0:LC, c, :, :].rearrange("p j n -> p (j n)")
                            blocks = to.rearrange("p (a b) -> p a b", b=DX)[:, 0:HPT * (P // DX):P // DX + 1, :]
                            ins = nc.gpsimd.tensor_copy(blocks, vf[0:LC, c * P:(c + 1) * P]
                                                        .rearrange("p (j d) -> p j d", d=DX))
                        ins.then_inc(v_ready, 1)
                    elif kind == "c_xb":
                        pool.wait_ge(xres_here, 1)
                        nc.gpsimd.tensor_tensor(xb[:, :, :], xres[:, :, :],
                                                cst[:, K_XOB:K_XOB + C].unsqueeze(1).broadcast_to([P, T, C]),
                                                ALU.add).then_inc(xb_ready, 1)
                    elif kind == "f_hh":
                        e, = a
                        pool.wait_ge(hr_hi, e + 1)
                        nc.gpsimd.tensor_tensor(hr["l"][:, e, :], hf[:, e % 4, :], hr["h"][:, e, :].bitcast(F), ALU.subtract)\
                            .then_inc(hr_ready, 1)
            iterations(pool, body)

        @block.scalar
        def _(act):
            for n, (o, m) in enumerate(chunks):
                act.wait_ge(stage_in[n % 2], 16 * (n // 2 + 1))
                nc.scalar.activation(wh[:, o:o + m], stage[n % 2][:, 0:m], ACT.Copy).then_inc(w_hi, 1)
            act.wait_ge(const_in, 32)
            act.wait_ge(split, len(chunks) + 1)

            def halves_hi(fl, s, to, width, sem_hi):
                fl.wait_full(act, s)
                nc.scalar.activation(to[:, :, :], fl.bank(s)[:, 0:CT * width].rearrange("p (c l) -> p c l", l=width),
                                     ACT.Copy).then_inc(sem_hi, 1)

            def body(b, feed, prepare, fetch):
                ff, fc = fills(feed, prepare, fetch)
                for s in cross_stages(feed, prepare, fetch):
                    kind, a = s[0], s[1:]
                    if kind == "c_ct":
                        halves_hi(fc, s, ctt["h"], LC, ctt_hi)
                    elif kind == "f_gt":
                        ff.wait_full(act, s)
                        ff.drained(nc.scalar.activation(gl[0:E, :], ff.bank(s)[0:E, 0:L], ACT.Copy), s)
                    elif kind == "c_xt":
                        halves_hi(fc, s, xnt["h"], L, xnt_hi)
                    elif kind == "c_q":
                        k, f = a
                        if k and not feed:
                            act.wait_ge(qx_ready, CT)
                        fc.wait_full(act, s)
                        fc.drained(nc.scalar.activation(qf[:, f, :], fc.bank(s)[:, 0:L], ACT.Identity,
                                                        bias=qb4[:, f:f + 1], scale=XSCALE), s)
                        fc.wait_drained(act, s)
                        nc.scalar.activation(qx["h"][:, f, :], qf[:, f, :], ACT.Copy).then_inc(q_hi, 1)
                    elif kind == "c_e":
                        i, t = a
                        act.wait_ge(nmx_ready, i * T + t + 1)
                        for h in range(i * HC, (i + 1) * HC):
                            ins = nc.scalar.activation(lm[:, t, h, :], lm[:, t, h, :], ACT.Exp,
                                                       bias=nmx[:, t, h:h + 1], accum_out=sm[:, t, h:h + 1])
                        ins.then_inc(exp_done, 1)
                    elif kind == "c_p":
                        i, t = a
                        fc.wait_full(act, s)
                        fc.drained(nc.scalar.activation(ptc[0:LC, i * HC:(i + 1) * HC, t * P:(t + 1) * P],
                                   fc.bank(s)[0:LC, :].rearrange("p (h q) -> p h q", q=P), ACT.Copy), s)
                    elif kind == "c_ol":
                        f, = a
                        fc.wait_full(act, ("c_o", f))
                        nc.scalar.activation(ox["h"][:, f, :], fc.bank(("c_o", f))[:, 0:L], ACT.Copy).then_inc(ox_hi, 1)
                    elif kind == "c_x3":
                        if feed:
                            ff.wait_full(act, ("f_gu", E - 1))
                        halves_hi(fc, s, x2t["h"], L, x2t_hi)
                    elif kind == "f_cp":
                        nc.scalar.activation(x2c[:, :, :], x2n[:, :, :], ACT.Copy).then_inc(x2c_ready, 1)
                    elif kind == "f_g2":
                        ff.wait_full(act, s)
                        ff.drained(nc.scalar.activation(sc[:, :, :], ff.bank(s)[:, 0:T * E].rearrange("p (t e) -> p t e", e=E),
                                                        ACT.Exp, scale=-1.0), s)
                    elif kind == "f_hh":
                        e, = a
                        if e % 2:
                            ff.wait_drained(act, ("f_cb", e // 2))
                        else:
                            act.wait_ge(hf_ready, e // 2 + 1)
                        nc.scalar.activation(hr["h"][:, e, :], hf[:, e % 4, :], ACT.Copy).then_inc(hr_hi, 1)
                    elif kind == "f_gu":
                        e, = a
                        ff.wait_full(act, s)
                        if e >= 2:
                            ff.wait_drained(act, ("f_gu", e - 2))
                        nc.scalar.activation(sg[:, e % 2, :], ff.bank(s)[:, 0:L], ACT.Tanh, scale=0.5).then_inc(sg_ready, 1)
            iterations(act, body)

        @block.vector
        def _(dve):
            own = [0]

            def link(ins):
                own[0] += 1
                ins.then_inc(s_own["dve"], 1)
                dve.wait_ge(s_own["dve"], own[0])

            for n, (o, m) in enumerate(chunks):
                dve.wait_ge(w_hi, n + 1)
                nc.vector.tensor_tensor(wl[:, o:o + m], stage[n % 2][:, 0:m], wh[:, o:o + m].bitcast(F),
                                        ALU.subtract).then_inc(split, 1)
            dve.wait_ge(const_in, 32)
            nc.vector.tensor_scalar(qb4[:, :], cst[:, K_XQB:K_XQB + CT], XSCALE, None, ALU.mult).then_inc(split, 1)
            dve.wait_ge(split, len(chunks) + 1)
            dve.wait_ge(zeroed, 1)
            for s in (xin_in, mi_in):
                dve.wait_ge(s, 16)

            def norm_guess(src, stats, mv, var, nt, rstd):
                for t in range(T):
                    i = nc.vector.bn_stats(stats[:, t, :], src[:, t, :])
                link(i)
                for t in range(T):
                    i = nc.vector.bn_aggr(mv[:, t, :], stats[:, t, :])
                link(i)
                link(nc.vector.tensor_scalar(var[:, :], mv[:, :, 1], EPS, None, ALU.add))
                link(nc.vector.tensor_scalar(nt[:, :].bitcast(I32), var[:, :].bitcast(I32), 1, None,
                                             ALU.logical_shift_right))
                return nc.vector.tensor_scalar(rstd[:, :].bitcast(I32), nt[:, :].bitcast(I32), -1.0, float(MAGIC),
                                               ALU.mult, ALU.add)

            def normalise(src, mv, rstd):
                for t in range(T):
                    ins = nc.vector.tensor_scalar(xn[:, t, :], src[:, t, :], mv[:, t, 0:1], rstd[:, t:t + 1],
                                                  ALU.subtract, ALU.mult)
                return ins

            def halves_lo(fl, s, to, width, sem_hi, n=1):
                dve.wait_ge(sem_hi, n)
                fl.drained(nc.vector.tensor_tensor(
                    to["l"][:, :, :], fl.bank(s)[:, 0:CT * width].rearrange("p (c l) -> p c l", l=width),
                    to["h"][:, :, :].bitcast(F), ALU.subtract), s)

            def chosen(score, n, tri, top, out):
                rows = (P, T, n, n)
                own_, other = score.unsqueeze(3).broadcast_to(rows), score.unsqueeze(2).broadcast_to(rows)
                first = cst[:, tri:tri + n * n].rearrange("p (i j) -> p i j", j=n)
                above, equal = c1[:, :, 0:n, 0:n], c2[:, :, 0:n, 0:n]

                def compare():
                    for t in range(T):
                        nc.vector.tensor_tensor(above[:, t], other[:, t], own_[:, t], ALU.is_gt)
                        ins = nc.vector.tensor_tensor(equal[:, t], other[:, t], own_[:, t], ALU.is_equal)
                    return ins

                def before():
                    for t in range(T):
                        ins = nc.vector.tensor_tensor(equal[:, t], equal[:, t], first, ALU.mult)
                    return ins

                def both():
                    for t in range(T):
                        ins = nc.vector.tensor_tensor(above[:, t], above[:, t], equal[:, t], ALU.add)
                    return ins

                def rank():
                    return nc.vector.tensor_reduce(rk[:, :, 0:n], above, mybir.AxisListType.X, ALU.add)

                def top_ones():
                    return nc.vector.tensor_scalar(out, rk[:, :, 0:n], float(top), None, ALU.is_lt)

                return [compare, before, both, rank, top_ones]

            pairs = sfc[:, :, :].rearrange("p t (g k) -> p t g k", k=GSZ)
            routing = [
                lambda: nc.vector.tensor_scalar(sc[:, :, :], sc[:, :, :], 1.0, None, ALU.add),
                lambda: nc.vector.reciprocal(sc[:, :, :], sc[:, :, :]),
                lambda: nc.vector.tensor_tensor(sfc[:, :, :], sc[:, :, :],
                                                cst[:, K_ESB:K_ESB + E].unsqueeze(1).broadcast_to([P, T, E]), ALU.add),
                lambda: nc.vector.tensor_tensor(gs[:, :, :], pairs[:, :, :, 0], pairs[:, :, :, 1], ALU.add),
                *chosen(gs[:, :, :], NGRP, K_TRG, TOPG, gm[:, :, :]),
                lambda: nc.vector.tensor_tensor(tmp[:, :, :].rearrange("p t (g k) -> p t g k", k=GSZ), pairs,
                                                gm[:, :, :].unsqueeze(3).broadcast_to([P, T, NGRP, GSZ]), ALU.mult),
                *chosen(tmp[:, :, :], E, K_TRI, TOPK, cw[:, :, :]),
                lambda: nc.vector.tensor_tensor(cw[:, :, :], cw[:, :, :], sc[:, :, :], ALU.mult),
                lambda: nc.vector.tensor_reduce(ws[:, :], cw[:, :, :], mybir.AxisListType.X, ALU.add),
                lambda: nc.vector.tensor_scalar(ws[:, :], ws[:, :], 1e-20, 2.0, ALU.add, ALU.mult),
                lambda: nc.vector.reciprocal(wr[:, :], ws[:, :]),
                lambda: nc.vector.tensor_tensor(cw[:, :, :], cw[:, :, :], wr[:, :].unsqueeze(2).broadcast_to([P, T, E]),
                                                ALU.mult)]
            assert len(routing) == RT

            def body(b, feed, prepare, fetch):
                own[0] = 0
                ff, fc = fills(feed, prepare, fetch)
                for s in cross_stages(feed, prepare, fetch):
                    kind, a = s[0], s[1:]
                    if kind == "c_norm":
                        if a[0]:
                            dve.wait_ge(xin_here, 1)
                        norm_guess(xin, stats, mv, var, nt, rstd).then_inc(guess, 1)
                    elif kind == "c_xn":
                        dve.wait_ge(rstd_ready, nth(feed, a[0]))
                        if a[0] and not feed:
                            fc.wait_full(dve, ("c_xt", 0))
                        normalise(xin, mv, rstd).then_inc(xin_read, 1)
                    elif kind == "c_ct":
                        halves_lo(fc, s, ctt, LC, ctt_hi, nth(feed, a[0]))
                    elif kind == "c_xt":
                        halves_lo(fc, s, xnt, L, xnt_hi, nth(feed, a[0]))
                    elif kind == "c_ng":
                        nc.vector.tensor_scalar(neg[:, :, :], mi[:, :, :], -1.0, NEG, ALU.add, ALU.mult)\
                            .then_inc(neg_ready, 1)
                    elif kind == "c_kv":
                        k, = a
                        if k and not feed:
                            dve.wait_ge(kbd_ready, CT)
                            dve.wait_ge(v_ready, 1)
                        fc.wait_full(dve, s)
                        ps = fc.bank(s)
                        for c in range(CT):
                            nc.vector.tensor_scalar(kf[:, c, :], ps[:, c * LC:(c + 1) * LC],
                                                    cst[:, K_XKB + c:K_XKB + c + 1], None, ALU.add)
                        fc.drained(nc.vector.tensor_tensor(vf[0:LC, :], ps[0:LC, CT * LC:CT * LC + C],
                                                           cst[0:LC, K_XVB:K_XVB + C], ALU.add), s)
                        fc.wait_drained(dve, s)
                        dve.sem_inc(kf_ready, 1)
                    elif kind == "c_q":
                        k, f = a
                        dve.wait_ge(q_hi, CT * (nth(feed, k) - 1) + f + 1)
                        nc.vector.tensor_tensor(qx["l"][:, f, :], qf[:, f, :], qx["h"][:, f, :].bitcast(F), ALU.subtract)\
                            .then_inc(qx_ready, 1)
                    elif kind == "c_l":
                        i, t = a
                        if i == 0 and t == 0:
                            dve.wait_ge(neg_ready, 1)
                        fc.wait_full(dve, s)
                        for j in range(HC):
                            h = i * HC + j
                            ins = nc.vector.tensor_tensor_reduce(
                                out=lm[:, t, h, :], in0=fc.bank(s)[:, j * LC:(j + 1) * LC], in1=neg[:, t, :],
                                scale=1.0, scalar=LOWEST, op0=ALU.add, op1=ALU.max, accum_out=mx[:, t, h:h + 1])
                        fc.drained(ins, s)
                    elif kind == "c_lx":
                        i, t = a
                        fc.wait_drained(dve, ("c_l", i, t))
                        heads = slice(i * HC, (i + 1) * HC)
                        nc.vector.tensor_scalar(nmx[:, t, heads], mx[:, t, heads], -1.0, None, ALU.mult).then_inc(nmx_ready, 1)
                    elif kind == "c_r":
                        i, t = a
                        dve.wait_ge(exp_done, i * T + t + 1)
                        heads = slice(i * HC, (i + 1) * HC)
                        nc.vector.reciprocal(rs[:, t, heads], sm[:, t, heads]).then_inc(rs_ready, 1)
                    elif kind == "c_m":
                        i, t = a
                        dve.wait_ge(rs_ready, i * T + t + 1)
                        if i == 0 and t == 0:
                            dve.wait_ge(gp_here, 1)
                        for h in range(i * HC, (i + 1) * HC):
                            ins = nc.vector.scalar_tensor_tensor(lm[:, t, h, :], lm[:, t, h, :], rs[:, t, h:h + 1],
                                                                 gpt[:, t, :], ALU.mult, ALU.mult)
                        ins.then_inc(pc_ready, 1)
                    elif kind == "c_ol":
                        f, = a
                        s = ("c_o", f)
                        dve.wait_ge(ox_hi, f + 1)
                        fc.drained(nc.vector.tensor_tensor(ox["l"][:, f, :], fc.bank(s)[:, 0:L],
                                                           ox["h"][:, f, :].bitcast(F), ALU.subtract), s)
                    elif kind == "c_w":
                        fc.wait_full(dve, s)
                        dve.wait_ge(xb_ready, 1)
                        if feed:
                            dve.wait_ge(x2c_ready, 1)
                        fc.drained(nc.vector.tensor_tensor(x2n[:, :, :], fc.bank(s)[:, :].rearrange("p (t n) -> p t n", t=T),
                                                           xb[:, :, :], ALU.add), s)
                    elif kind == "c_n2":
                        fc.wait_drained(dve, ("c_w",))
                        link(norm_guess(x2n, stats2, mv2, var2, nt2, rstd2))
                        for n in range(3):
                            link(nc.vector.scalar_tensor_tensor(nt2[:, :], rstd2[:, :], -0.5, rstd2[:, :], ALU.mult, ALU.mult))
                            link(nc.vector.tensor_tensor(nt2[:, :], nt2[:, :], var2[:, :], ALU.mult))
                            link(nc.vector.scalar_tensor_tensor(rstd2[:, :], nt2[:, :], 1.5, rstd2[:, :], ALU.add, ALU.mult))
                    elif kind == "c_x2":
                        if fetch:
                            fc.wait_full(dve, ("c_xt", 1))
                        normalise(x2n, mv2, rstd2).then_inc(xn_ready, 1)
                    elif kind == "c_x3":
                        halves_lo(fc, s, x2t, L, x2t_hi)
                    elif kind == "f_rt":
                        n, = a
                        if n == 0:
                            ff.wait_drained(dve, ("f_g2",))
                        else:
                            dve.wait_ge(rt_step, n)
                        routing[n]().then_inc(rt_step, 1)
                    elif kind == "f_gu":
                        e, = a
                        dve.wait_ge(sg_ready, e + 1)
                        if e >= 2:
                            ff.wait_drained(dve, ("f_gu", e - 2))
                        nc.vector.scalar_tensor_tensor(gs2[:, e % 2, :], sg[:, e % 2, :], 1.0, ff.bank(s)[:, 0:L],
                                                       ALU.add, ALU.mult).then_inc(gs_ready, 1)
                    elif kind == "f_gv":
                        e, = a
                        gu = ("f_gu", e)
                        dve.wait_ge(gs_ready, e + 1)
                        ff.drained(nc.vector.tensor_tensor(hu[:, e, :], ff.bank(gu)[:, L:2 * L],
                                                           gs2[:, e % 2, :], ALU.mult), gu)
                    elif kind == "f_h":
                        e, = a
                        cb = ("f_cb", e // 2)
                        ff.wait_full(dve, cb)
                        ff.wait_drained(dve, ("f_gu", e))
                        if e >= 4:
                            dve.wait_ge(hr_ready, e - 3)
                        ins = nc.vector.tensor_tensor(hf[:, e % 4, :], ff.bank(cb)[:, (e % 2) * L:(e % 2 + 1) * L],
                                                      hu[:, e, :], ALU.mult)
                        if e % 2:
                            ff.drained(ins, cb)
                        else:
                            ins.then_inc(hf_ready, 1)
                    elif kind == "f_dn":
                        t, = a
                        ff.wait_full(dve, s)
                        if t == 0:
                            dve.wait_ge(last_add, 1)
                            dve.wait_ge(x2c_ready, 1)
                        ff.drained(nc.vector.tensor_tensor(ob[:, t, :], ff.bank(s)[:, 0:C], x2c[:, t, :], ALU.add), s)
            iterations(dve, body)

        @block.tensor
        def _(pe):
            pe.wait_ge(split, len(chunks) + 1)
            pe.wait_ge(const_in, 32)
            pe.wait_ge(zeroed, 1)
            pe.wait_ge(ctx_in, 16)

            def project(out, lhs, rhs, tiles):
                n, last = 0, len(PRODUCTS) * tiles - 1
                for c in range(tiles):
                    for a, b in PRODUCTS:
                        ins = nc.tensor.matmul(out, lhs(a, c), rhs(b, c), start=(n == 0), stop=(n == last))
                        n += 1
                return ins

            def weight(o, width, at, n):
                return lambda k, c: w[k][:, o + c * width + at:o + c * width + at + n]

            def turn(fl, s):
                fl.wait_free(pe, s)
                for c in range(CT):
                    for t in range(T):
                        o = c * L + t * P
                        ins = nc.tensor.transpose(fl.bank(s)[:, o:o + P], xn[:, t, c * P:(c + 1) * P], idn[:, :])
                fl.filled(ins, s)

            def body(b, feed, prepare, fetch):
                ff, fc = fills(feed, prepare, fetch)
                for s in cross_stages(feed, prepare, fetch):
                    kind, a = s[0], s[1:]
                    if kind == "c_ct":
                        if a[0]:
                            pe.wait_ge(ctx_here, 1)
                        fc.wait_free(pe, s)
                        for c in range(CT):
                            ins = nc.tensor.transpose(fc.bank(s)[:, c * LC:(c + 1) * LC], cin[0:LC, c * P:(c + 1) * P],
                                                      idn[0:LC, 0:LC])
                        fc.filled(ins, s)
                    elif kind == "c_kv":
                        fc.wait_drained(pe, ("c_ct", a[0]))
                        fc.wait_free(pe, s)
                        for f in range(CT):
                            project(fc.bank(s)[:, f * LC:(f + 1) * LC], weight(O_XK, C, f * P, P),
                                    lambda k, c: ctt[k][:, c, :], CT)
                        fc.filled(project(fc.bank(s)[0:LC, CT * LC:CT * LC + C], lambda k, c: ctt[k][:, c, :],
                                          weight(O_XV, C, 0, C), CT), s)
                    elif kind == "c_xt":
                        pe.wait_ge(xin_read, nth(feed, a[0]))
                        turn(fc, s)
                    elif kind == "c_q":
                        k, f = a
                        fc.wait_drained(pe, ("c_xt", k))
                        fc.wait_free(pe, s)
                        fc.filled(project(fc.bank(s)[:, 0:L], weight(O_XQ, C, f * P, P), lambda k, c: xnt[k][:, c, :], CT), s)
                    elif kind == "c_l":
                        i, t = a
                        f, o = i // 2, (i % 2) * HC
                        if not feed:
                            pe.wait_ge(kbd_ready, CT)
                            pe.wait_ge(qx_ready, CT)
                        fc.wait_free(pe, s)
                        fc.filled(project(fc.bank(s)[:, 0:HC * LC], lambda k, c: qx[k][:, f, t * P:(t + 1) * P],
                                          lambda k, c: kbd[k][:, f, o:o + HC, :].rearrange("p j n -> p (j n)"), 1), s)
                    elif kind == "c_p":
                        i, t = a
                        pe.wait_ge(pc_ready, i * T + t + 1)
                        fc.wait_free(pe, s)
                        for j in range(HC):
                            ins = nc.tensor.transpose(fc.bank(s)[0:LC, j * P:(j + 1) * P], lm[:, t, i * HC + j, :], idn[:, :])
                        fc.filled(ins, s)
                    elif kind == "c_o":
                        f, = a
                        if not feed:
                            pe.wait_ge(v_ready, 1)
                        fc.wait_free(pe, s)
                        for j in range(HPT):
                            if j % HC == 0:
                                for t in range(T):
                                    fc.wait_drained(pe, ("c_p", (f * HPT + j) // HC, t))
                            ins = nc.tensor.matmul(fc.bank(s)[:, 0:L], vpad[0:LC, f, j, :], ptc[0:LC, f * HPT + j, :],
                                                   start=(j == 0), stop=(j == HPT - 1))
                        fc.filled(ins, s)
                    elif kind == "c_w":
                        for f in range(CT):
                            fc.wait_drained(pe, ("c_o", f))
                        fc.wait_free(pe, s)
                        for t in range(T):
                            ins = project(fc.bank(s)[:, t * C:(t + 1) * C], lambda k, c: ox[k][:, c, t * P:(t + 1) * P],
                                          weight(O_XO, C, 0, C), CT)
                        fc.filled(ins, s)
                    elif kind == "c_x3":
                        pe.wait_ge(xn_ready, 1)
                        turn(fc, s)
                    elif kind == "f_gt":
                        ff.filled(project(ff.bank(s)[0:E, 0:L], weight(O_GT, E, 0, E), lambda k, c: x2t[k][:, c, :], CT), s)
                    elif kind == "f_g2":
                        ff.wait_drained(pe, ("f_gt",))
                        for t in range(T):
                            ins = nc.tensor.transpose(ff.bank(s)[:, t * E:(t + 1) * E], gl[:, t * P:(t + 1) * P],
                                                      idn[0:E, 0:E])
                        ff.filled(ins, s)
                    elif kind == "f_gu":
                        e, = a
                        ff.wait_free(pe, s)
                        for n, o in enumerate((O_G, O_U)):
                            ins = project(ff.bank(s)[:, n * L:(n + 1) * L], weight(o, E * I, e * I, I),
                                          lambda k, c: x2t[k][:, c, :], CT)
                        ff.filled(ins, s)
                    elif kind == "f_cb":
                        i, = a
                        pe.wait_ge(rt_step, RT)
                        ff.wait_free(pe, s)
                        for j in range(2):
                            for t in range(T):
                                o, e = j * L + t * P, 2 * i + j
                                ins = nc.tensor.transpose(ff.bank(s)[:, o:o + P], cw[:, t, e:e + 1].broadcast_to([P, P]),
                                                          idn[:, :])
                        ff.filled(ins, s)
                    elif kind == "f_dn":
                        t, = a
                        pe.wait_ge(hr_ready, E)
                        ff.wait_free(pe, s)
                        ff.filled(project(ff.bank(s)[:, 0:C], lambda k, c: hr[k][:, c, t * P:(t + 1) * P],
                                          weight(O_DN, C, 0, C), E), s)
            iterations(pe, body)


def decoder(nc, x, ctxt, gp, mask, w1, k1, rope, w2, k2, ident, out, batches=B):
    x1 = nc.dram_tensor("x1_dram", [batches, L, C], F, kind="Internal").ap()
    with ExitStack() as keep:
        self_attention(nc, keep, x, x1, w1, k1, rope, ident, batches)
        cross_and_feed(nc, keep, x1, ctxt, gp, mask, out, w2, k2, ident, batches)


def tiles(w):
    return w.reshape(-1, P, w.shape[1]).transpose(1, 0, 2).reshape(P, -1)


def everywhere(v):
    return np.broadcast_to(v.reshape(1, -1), (P, v.size))


def packed(i):
    a = {n[8:]: np.asarray(v) for n, v in i.items() if n.startswith("L0_attn_")}
    c = {n[9:]: np.asarray(v) for n, v in i.items() if n.startswith("L0_xattn_")}
    f = {n[7:]: np.asarray(v) for n, v in i.items() if n.startswith("L0_ffn_")}
    groups = []
    for g in range(G):
        q, kv = slice(g * RG * D, (g + 1) * RG * D), slice(g * D, (g + 1) * D)
        groups += [a["Wq"][:, q], a["Wk"][:, kv], a["Wv"][:, kv]]
    w1 = [tiles(np.concatenate([a["Wqi"], a["Wki"], a["Wwi"]], 1)), tiles(np.concatenate(groups, 1)),
          tiles(a["Wvg"]), tiles(a["Wog"]), tiles(a["Wo"])]
    k1 = [everywhere(a["bvg"]), everywhere(a["bi"]), a["bog"].reshape(HT, P).T]
    half = np.arange(0, D, 2, dtype=np.float32) / np.float32(D)
    angle = np.outer(np.arange(L, dtype=np.float32), np.float32(1) / np.float32(10000) ** half).astype(np.float32)
    cos, sin = np.cos(angle), np.sin(angle)
    rope = np.stack([np.concatenate([cos, cos], 1), np.concatenate([-sin, sin], 1)], 1)
    rope = rope.reshape(T, P, 2, D).transpose(1, 0, 2, 3)
    experts = [w.reshape(E * I, C).T for w in (f["gate_proj"], f["up_proj"])]
    w2 = [tiles(c["wq_k"]), tiles(c["wk_k"]), tiles(c["wv_k"]), tiles(c["wo_k"]), tiles(f["gate_weight"].T),
          tiles(experts[0]), tiles(experts[1]), f["down_proj"].transpose(2, 0, 1).reshape(I, E * C)]
    own = (np.arange(P)[:, None] // DX == np.arange(HPT)[None, :]).astype(np.float32)
    k2 = [c["wq_b"].reshape(CT, P).T, c["wk_b"].reshape(CT, P).T, everywhere(c["wv_b"]), everywhere(c["wo_b"]),
          everywhere(f["e_score_correction_bias"]), own, everywhere(np.tril(np.ones((E, E), np.float32), -1)),
          everywhere(np.tril(np.ones((NGRP, NGRP), np.float32), -1))]
    return {"w1": np.concatenate(w1, 1), "k1": np.concatenate(k1, 1), "rope": rope, "w2": np.concatenate(w2, 1),
            "k2": np.concatenate(k2, 1), "ident": np.eye(P, dtype=np.float32)}


def kernel(**inputs):
    import concourse.bacc as bacc
    from concourse.bass_utils import run_bass_kernel_spmd

    arrays = {"x": inputs["x"], "ctx": inputs["ctx_1024"], "gp": inputs["fside_BxSxS2_0"],
              "mask": inputs["mask_BxSxS2_ik1"], **packed(inputs)}
    arrays = {"in_" + n: np.ascontiguousarray(a) for n, a in arrays.items()}
    nc = bacc.Bacc("TRN2", target_bir_lowering=False, num_devices=1)
    t = {n[3:]: nc.dram_tensor(n, list(a.shape), mybir.dt.from_np(a.dtype), kind="ExternalInput").ap()
         for n, a in arrays.items()}
    out = nc.dram_tensor("out_dram", [B, L, C], F, kind="ExternalOutput").ap()
    decoder(nc, t["x"], t["ctx"], t["gp"], t["mask"], t["w1"], t["k1"], t["rope"], t["w2"], t["k2"], t["ident"], out)
    return run_bass_kernel_spmd(nc, [arrays], core_ids=[0]).results[0]["out_dram"]
```

```python
from contextlib import ExitStack

import numpy as np

import concourse.bass as bass
from concourse import mybir

F = mybir.dt.float32
R = mybir.dt.float32r
I32 = mybir.dt.int32
ALU = mybir.AluOpType
ACT = mybir.ActivationFunctionType

B, L, C = 32, 256, 256
P = 128
T = L // P
CT = C // P
H, G, D = 16, 4, 64
RG = H // G
HI = 4
KSEL = 64
SCALE = D ** -0.5
EPS = 1e-5
MASKED = -1e30
LOWEST = -3.0e38
TAKEN = -64.0
MAGIC = 0x5F3759DF

NIDX = HI * D + D + HI
NPJ = RG * D + 2 * D
ROT = RG * D + D
ST = RG * 2 * D + 3 * D
HT = H * D // P

O_IDX = 0
O_PJ = O_IDX + CT * NIDX
O_VG = O_PJ + CT * G * NPJ
O_OG = O_VG + CT * G * D
O_WO = O_OG + CT * H * D
N_W1 = O_WO + HT * C

K_BVG = 0
K_BI = K_BVG + G * D
K_BOG = K_BI + HI
N_K1 = K_BOG + HT

PRODUCTS = (("h", "h"), ("h", "l"), ("l", "h"))


class Fills:

    def __init__(self, banks, full, free, names):
        self.banks, self.full, self.free = banks, full, free
        self.at = {name: (n % len(banks), n // len(banks)) for n, name in enumerate(names)}

    def bank(self, name):
        return self.banks[self.at[name][0]]

    def wait_free(self, eng, name):
        b, n = self.at[name]
        if n:
            eng.wait_ge(self.free[b], n)

    def wait_full(self, eng, name):
        b, n = self.at[name]
        eng.wait_ge(self.full[b], n + 1)

    def wait_drained(self, eng, name):
        b, n = self.at[name]
        eng.wait_ge(self.free[b], n + 1)

    def filled(self, ins, name):
        ins.then_inc(self.full[self.at[name][0]], 1)

    def drained(self, ins, name):
        ins.then_inc(self.free[self.at[name][0]], 1)


NTK = KSEL // 8


def ordered(text):
    return [(word.split(".")[0],) + tuple(int(n) for n in word.split(".")[1:]) for word in text.split()]


SELF_ORDER = ordered("""
    b_cp a_xn b_vg b_pj.0.0 b_pj.0.1 b_tk.2 b_tk.3 b_tk.4 b_tk.5 a_xt b_og.0 b_r.0.0 b_r.0.1 b_og.1
    b_og.2 b_og.3 b_tk.6 b_tk.7 b_mk b_kx.0 b_qx.0.0 b_qx.0.1 b_pj.1.0 b_pj.1.1 b_r.1.0 b_r.1.1
    b_s.0.0 b_s.0.1 b_e.0 b_s.1.0 b_s.1.1 a_ix.0 a_ix.1 b_n.0 b_e.1 b_kx.1 b_qx.1.0 b_v.0.0 b_v.0.1
    b_n.1 b_qx.1.1 b_v.1.0 b_v.1.1 b_t.0.0 b_t.0.1 b_s.2.0 b_e.2 b_s.2.1 b_l.0.0 b_l.0.1 a_iqx.0
    b_pj.2.0 a_iqx.1 b_pj.2.1 a_ikx b_r.2.0 b_r.2.1 b_t.1.0 b_s.3.0 b_t.1.1 b_n.2 b_s.3.1 b_e.3
    a_si.0.0 b_l.1.0 b_o.0 b_l.1.1 a_si.0.1 b_g.0 a_sc.0.0 a_sc.0.1 b_kx.2 b_qx.2.0 b_qx.2.1 b_v.2.0
    b_v.2.1 b_n.3 b_t.2.0 b_t.2.1 b_e.4 b_s.4.0 b_s.4.1 b_l.2.0 b_l.2.1 b_h.0 b_o.1 a_si.1.0
    a_si.1.1 b_g.1 b_pj.3.0 b_pj.3.1 a_sc.1.0 a_sc.1.1 b_r.3.0 b_r.3.1 b_s.5.0 b_s.5.1 b_n.4 b_l.3.0
    b_t.3.0 b_t.3.1 b_e.5 b_l.3.1 b_o.2 b_g.2 b_kx.3 b_qx.3.0 a_tk.0 b_h.1 b_qx.3.1 b_v.3.0 b_v.3.1
    b_n.5 b_t.4.0 b_t.4.1 b_s.6.0 b_s.6.1 b_e.6 b_l.4.0 b_h.2 b_g.3 b_l.4.1 a_tk.1 b_o.3 b_n.6
    b_t.5.0 b_t.5.1 b_s.7.0 b_s.7.1 b_e.7 b_h.3 b_o.4 b_g.4 b_l.5.0 b_l.5.1 b_n.7 b_t.6.0 b_t.6.1
    b_l.6.0 b_h.4 b_o.5 b_l.6.1 a_norm.1 b_g.5 b_l.7.0 b_t.7.0 b_o.6 b_t.7.1 b_o.7 b_h.5 b_l.7.1
    b_g.6 b_h.6 b_g.7 b_h.7 b_w1a b_w0 b_w1b
""")
assert sorted(s[1] for s in SELF_ORDER if s[0] in ("a_tk", "b_tk")) == list(range(NTK))
assert sum(s[0] == "b_o" for s in SELF_ORDER) == G * T


def self_stages(attend, prepare, fetch):
    def takes_part(stage):
        if stage[0].startswith("b_"):
            return attend
        return fetch if stage == ("a_norm", 1) else prepare
    return ([] if attend else [("a_norm", 0), ("w_lo",)]) + [s for s in SELF_ORDER if takes_part(s)]


def self_attention(nc, keep, x, x1, w1, k1, rope, ident, batches=B):
    with ExitStack() as ctx:
        def sb(name, shape, dt=F):
            return ctx.enter_context(nc.sbuf_tensor("s_" + name, shape, dt))

        sems = []

        def sem(name):
            sems.append(keep.enter_context(nc.semaphore("s_" + name)))
            return sems[-1]

        wh, wl = sb("wh", [P, N_W1], R), sb("wl", [P, N_W1], R)
        w = {"h": wh, "l": wl}
        cst = sb("cst", [P, N_K1])
        half = sb("half", [P, N_K1])
        cs = sb("cs", [P, T, 2, D])
        idn = sb("idn", [P, P])
        xin = sb("xin", [P, T, C])
        stats, mv = sb("stats", [P, T, 6]), sb("mv", [P, T, 2])
        var, rstd, nt = sb("var", [P, T]), sb("rstd", [P, T]), sb("nt", [P, T])
        xn = sb("xn", [P, T, C])
        xnt = {k: sb("xnt" + k, [P, CT, L], R) for k in "hl"}
        ist = sb("ist", [P, T, ST], R)
        wth, wt1 = sb("wth", [P, T, HI]), sb("wt1", [P, T, HI])
        iqt = sb("iqt", [P, HI, L], R)
        ikt = sb("ikt", [P, 2, L], R)
        sig = sb("sig", [P, 2, 2, L])
        score = sb("score", [P, T, L])
        top8 = sb("top8", [P, T, 8])
        xct = {k: sb("xct" + k, [P, CT, L], R) for k in "hl"}
        mb = sb("mb", [P, T, L])
        vg = sb("vg", [P, T, G * D])
        g1t = sb("g1t", [P, HT, L])
        t1, t2, rs = sb("t1", [P, T, ROT]), sb("t2", [P, T, ROT]), sb("rs", [P, T, ROT])
        st = sb("st", [P, T, ST], R)
        kt = sb("kt", [P, 2, 2, L], R)
        qt = sb("qt", [P, 2, RG, L], R)
        vf = sb("vf", [P, 2, T, D])
        va = {k: sb("va" + k, [P, T, G, 2, D], R) for k in "hl"}
        sm = sb("sm", [P, 2, RG, L])
        mx, nm = sb("mx", [P, 2, RG]), sb("nm", [P, 2, RG])
        pr = sb("pr", [P, 2, RG, L])
        rsum, rinv = sb("rsum", [P, 2, RG]), sb("rinv", [P, 2, RG])
        pt = {k: sb("pt" + k, [P, 2, T, RG * P], R) for k in "hl"}
        on = sb("on", [P, 2, 2, P])
        ot = {k: sb("ot" + k, [P, HT, L], R) for k in "hl"}
        xres = sb("xres", [P, T, C])
        x1b = sb("x1b", [P, T, C])

        psb = [ctx.enter_context(nc.psum_tensor(f"s_ps{i}", [P, 512], F)) for i in range(8)]
        full, free = [sem(f"full{i}") for i in range(8)], [sem(f"free{i}") for i in range(8)]
        s_own = {e: sem("own_" + e) for e in ("dve", "pool")}
        arrive, fetched = sem("arrive"), sem("fetched")
        guess, rstd_ready, xn_ready = sem("guess"), sem("rstd_ready"), sem("xn_ready")
        xnt_hi = sem("xnt_hi")
        ist_hi = sem("ist_hi")
        sig_used = sem("sig_used")
        wt_ready = sem("wt_ready")
        xct_ready, vg_ready = sem("xct_ready"), sem("vg_ready")
        turned, summed, rounded, stacked = sem("turned"), sem("summed"), sem("rounded"), sem("stacked")
        va_hi, va_ready = sem("va_hi"), sem("va_ready")
        nm_ready, exp_done = sem("nm_ready"), sem("exp_done")
        rinv_ready, pt_hi = sem("rinv_ready"), sem("pt_hi")
        pr_ready = [sem("pr_ready0"), sem("pr_ready1")]
        on_ready, ot_hi, ot_ready = sem("on_ready"), sem("ot_hi"), sem("ot_ready")
        last_add = sem("last_add")
        in_iteration = list(sems)
        go, passed = sem("go"), sem("passed")
        const_in, split = sem("const_in"), sem("split")
        stage_in = [sem(f"stage_in{n}") for n in range(6)]
        late_split, halved = sem("late_split"), sem("halved")
        xin_in, xres_in, stored = sem("xin_in"), sem("xres_in"), sem("stored")
        w_hi = sem("w_hi")
        first, last = in_iteration[0].num, in_iteration[-1].num
        assert last - first == len(in_iteration) - 1

        def fills(attend, prepare, fetch):
            b, a = [], []
            for s in self_stages(attend, prepare, fetch):
                if s[0] in ("a_xt", "a_ix", "a_iqx", "a_ikx", "a_si"):
                    a.append(s)
                elif s[0] in ("b_vg", "b_og", "b_pj", "b_kx", "b_qx", "b_s", "b_t", "b_o", "b_w0",
                              "b_w1a"):
                    b.append(s)
            return (Fills(psb[0:5], full[0:5], free[0:5], b),
                    Fills(psb[5:8], full[5:8], free[5:8], a))

        def iterations(eng, body):
            def meet(n):
                eng.drain().then_inc(arrive, 1)
                eng.wait_ge(go, n)
                eng.sem_inc(passed, 1)
            body(-1, False, True, True)
            meet(1)
            if batches > 2:
                with eng.Fori(0, batches - 2) as b:
                    body(b, True, True, True)
                    meet(b + 2)
            body(batches - 2, True, True, False)
            meet(batches)
            body(batches - 1, True, False, False)
            meet(batches + 1)

        CH, EARLY = 1024, 6
        stage = [v[:, n * CH:(n + 1) * CH] for v in (sm[:, :, :, :].rearrange("p a b c -> p (a b c)"),
                                                     pr[:, :, :, :].rearrange("p a b c -> p (a b c)"),
                                                     g1t[:, :, :].rearrange("p a b -> p (a b)")) for n in range(2)]
        chunks = [(o, min(CH, N_W1 - o)) for o in range(0, N_W1, CH)]

        block = ctx.enter_context(nc.Block())

        @block.sync
        def _(sp):
            sp.dma_start(xin[:, :, :], x[0].rearrange("(t p) c -> p t c", p=P)).then_inc(xin_in, 16)
            for n, (o, m) in enumerate(chunks):
                if n >= len(stage):
                    sp.wait_ge(split, n - len(stage) + 1)
                sp.dma_start(stage[n % len(stage)][:, 0:m], w1[:, o:o + m]).then_inc(stage_in[n % len(stage)], 16)
                if n == 0:
                    sp.dma_start(idn[:, :], ident).then_inc(const_in, 16)
                    sp.dma_start(cst[:, :], k1).then_inc(const_in, 16)
                    sp.dma_start(cs[:, :, :, :], rope).then_inc(const_in, 16)

            def rows(t, b):
                return t[bass.ds(b, 1)].rearrange("o (t p) c -> p (o t) c", p=P)

            def body(b, attend, prepare, fetch):
                it = b + 1
                if attend:
                    sp.dma_start(xres[:, :, :], rows(x, b)).then_inc(xres_in, 16)
                if prepare and fetch:
                    sp.wait_ge(xn_ready, T)
                    sp.dma_start(xin[:, :, :], rows(x, b + 2)).then_inc(xin_in, 16)
                if prepare and fetch:
                    sp.wait_ge(xin_in, (b + 3) * 16)
                    sp.sem_inc(fetched, 1)
                if attend:
                    sp.wait_ge(xres_in, (b + 1) * 16)
                    sp.wait_ge(stored, (b + PRIME) * 16)
                    sp.sem_inc(last_add, 1)
                    for s in (("b_w0",), ("b_w1a",)):
                        fills(attend, prepare, fetch)[0].wait_drained(sp, s)
                    sp.dma_start(rows(x1, b), x1b[:, :, :]).then_inc(stored, 16)
                sp.wait_ge(arrive, 4)
                sp.sem_clear(range(first, last + 1))
                sp.sem_inc(go, 1)

            PRIME = 1
            sp.sem_inc(stored, 16)
            body(-1, False, True, True)
            if batches > 2:
                with sp.Fori(0, batches - 2) as b:
                    body(b, True, True, True)
            body(batches - 2, True, True, False)
            body(batches - 1, True, False, False)
            sp.wait_ge(stored, (batches + PRIME) * 16)
            sp.wait_ge(passed, 4 * (batches + 1))

        @block.gpsimd
        def _(pool):
            own = [0]

            def link(ins):
                own[0] += 1
                ins.then_inc(s_own["pool"], 1)
                pool.wait_ge(s_own["pool"], own[0])

            def body(b, attend, prepare, fetch):
                own[0] = 0
                fb, fa = fills(attend, prepare, fetch)
                for s in self_stages(attend, prepare, fetch):
                    kind, a = s[0], s[1:]
                    if kind == "w_lo":
                        for n, (o, m) in list(enumerate(chunks))[EARLY:]:
                            pool.wait_ge(w_hi, n + 1)
                            nc.gpsimd.tensor_tensor(wl[:, o:o + m], stage[n % len(stage)][:, 0:m],
                                                    wh[:, o:o + m].bitcast(F), ALU.subtract).then_inc(late_split, 1)
                    elif kind == "a_norm":
                        pool.wait_ge(guess, 1 + (not attend and a[0]))
                        for n in range(3):
                            link(nc.gpsimd.tensor_tensor(nt[:, :], rstd[:, :], rstd[:, :], ALU.mult))
                            link(nc.gpsimd.tensor_tensor(nt[:, :], nt[:, :], var[:, :], ALU.mult))
                            link(nc.gpsimd.tensor_scalar(nt[:, :], nt[:, :], -0.5, 1.5, ALU.mult, ALU.add))
                            i = nc.gpsimd.tensor_tensor(rstd[:, :], rstd[:, :], nt[:, :], ALU.mult)
                            if n < 2:
                                link(i)
                            else:
                                i.then_inc(rstd_ready, 1)
                    elif kind == "a_ix":
                        t, = a
                        pool.wait_ge(ist_hi, t + 1)
                        nc.gpsimd.tensor_scalar(wt1[:, t, :], wth[:, t, :], 1.0, None, ALU.add).then_inc(wt_ready, 1)
                    elif kind == "b_pj":
                        g, t = a
                        n = g * T + t
                        pool.wait_ge(turned, n + 1)
                        if g:
                            pool.wait_ge(stacked, n - 1)
                        nc.gpsimd.tensor_tensor(rs[:, t, :], t1[:, t, :], t2[:, t, :], ALU.add).then_inc(summed, 1)
                    elif kind == "b_r":
                        g, t = a
                        n = g * T + t
                        q = rs[:, t, 0:RG * D].rearrange("p (h d) -> p h d", d=D)
                        qs = st[:, t, 0:RG * 2 * D].rearrange("p (h s d) -> p h s d", s=2, d=D)
                        k, ks = rs[:, t, RG * D:ROT], st[:, t, RG * 2 * D:ST].rearrange("p (s d) -> p s d", d=D)
                        pool.wait_ge(rounded, n + 1)
                        nc.gpsimd.tensor_tensor(qs[:, :, 1, :], q, qs[:, :, 0, :].bitcast(F), ALU.subtract)
                        nc.gpsimd.tensor_tensor(ks[:, 1, :], k, ks[:, 0, :].bitcast(F), ALU.subtract)\
                            .then_inc(stacked, 1)
                    elif kind == "b_v":
                        g, t = a
                        n = g * T + t
                        pool.wait_ge(va_hi, n + 1)
                        nc.gpsimd.tensor_tensor(va["l"][:, t, g, :, :], vf[:, g % 2, t, :].unsqueeze(1).broadcast_to([P, 2, D]),
                                                va["h"][:, t, g, :, :].bitcast(F), ALU.subtract).then_inc(va_ready, 1)
                    elif kind == "b_n":
                        u, = a
                        pool.wait_ge(rinv_ready, u + 1)
                        for j in range(2):
                            two = pr[:, u % 2, 2 * j:2 * j + 2, :]
                            nc.gpsimd.tensor_tensor(two, two, rinv[:, u % 2, 2 * j:2 * j + 2].unsqueeze(2)
                                                    .broadcast_to([P, 2, L]), ALU.mult).then_inc(pr_ready[j], 1)
                    elif kind == "b_h":
                        u, = a
                        g, t = u // T, u % T
                        pool.wait_ge(ot_hi, u + 1)
                        to = [ot[k][:, 2 * g:2 * g + 2, t * P:(t + 1) * P] for k in "hl"]
                        nc.gpsimd.tensor_tensor(to[1], on[:, u % 2, :, :], to[0].bitcast(F), ALU.subtract)\
                            .then_inc(ot_ready, 1)
            iterations(pool, body)

        @block.scalar
        def _(act):
            for n, (o, m) in enumerate(chunks):
                act.wait_ge(stage_in[n % len(stage)], 16 * (n // len(stage) + 1))
                nc.scalar.activation(wh[:, o:o + m], stage[n % len(stage)][:, 0:m], ACT.Copy).then_inc(w_hi, 1)
            act.wait_ge(halved, 1)

            def body(b, attend, prepare, fetch):
                fb, fa = fills(attend, prepare, fetch)
                for s in self_stages(attend, prepare, fetch):
                    kind, a = s[0], s[1:]
                    if kind == "a_xt":
                        fa.wait_full(act, s)
                        if attend:
                            fb.wait_full(act, ("b_pj", 0, 1))
                            act.wait_ge(xct_ready, 2)
                        nc.scalar.activation(xnt["h"][:, :, :], fa.bank(s)[:, :].rearrange("p (c l) -> p c l", l=L),
                                             ACT.Copy).then_inc(xnt_hi, 1)
                    elif kind == "a_ix":
                        t, = a
                        fa.wait_full(act, s)
                        ps = fa.bank(s)
                        hs = ist[:, t, 0:HI * 2 * D].rearrange("p (h s d) -> p h s d", s=2, d=D)
                        ks = ist[:, t, HI * 2 * D:ST].rearrange("p (s d) -> p s d", d=D)
                        nc.scalar.activation(hs[:, :, 0, :], ps[:, 0:HI * D].rearrange("p (h d) -> p h d", d=D), ACT.Copy)
                        nc.scalar.activation(ks[:, 0:3:2, :], ps[:, HI * D:HI * D + D].unsqueeze(1).broadcast_to([P, 2, D]),
                                             ACT.Copy)
                        nc.scalar.activation(wth[:, t, :], ps[:, HI * D + D:NIDX], ACT.Tanh, scale=0.5).then_inc(ist_hi, 1)
                    elif kind == "a_iqx":
                        j, = a
                        fa.wait_full(act, s)
                        fa.drained(nc.scalar.activation(iqt[:, 2 * j:2 * j + 2, :],
                                   fa.bank(s)[:, :].rearrange("p (h l) -> p h l", l=L), ACT.Copy), s)
                    elif kind == "a_ikx":
                        fa.wait_full(act, s)
                        fa.drained(nc.scalar.activation(ikt[:, :, :],
                                   fa.bank(s)[:, :].rearrange("p (h l) -> p h l", l=L), ACT.Copy), s)
                    elif kind == "a_si":
                        t, j = a
                        fa.wait_full(act, s)
                        if t:
                            act.wait_ge(sig_used, j + 1)
                        for i in range(2):
                            h = 2 * j + i
                            ins = nc.scalar.activation(sig[:, j, i, :], fa.bank(s)[:, i * L:(i + 1) * L], ACT.Tanh,
                                                       bias=half[:, K_BI + h:K_BI + h + 1], scale=0.5)
                        fa.drained(ins, s)
                    elif kind == "b_vg":
                        fb.wait_drained(act, s)
                        nc.scalar.activation(vg[:, :, :], vg[:, :, :], ACT.Tanh, scale=0.5).then_inc(vg_ready, 1)
                    elif kind == "b_cp":
                        nc.scalar.activation(xct["h"][:, :, :], xnt["h"][:, :, :].bitcast(F), ACT.Copy)\
                            .then_inc(xct_ready, 1)
                    elif kind == "b_og":
                        j, = a
                        fb.wait_full(act, s)
                        for i in range(2):
                            m = 2 * j + i
                            ins = nc.scalar.activation(g1t[:, m, :], fb.bank(s)[:, i * L:(i + 1) * L], ACT.Tanh,
                                                       bias=half[:, K_BOG + m:K_BOG + m + 1], scale=0.5)
                        fb.drained(ins, s)
                    elif kind == "b_r":
                        g, t = a
                        n = g * T + t
                        act.wait_ge(summed, n + 1)
                        if g:
                            fb.wait_full(act, ("b_qx", g - 1, RG // 2 - 1))
                        q = rs[:, t, 0:RG * D].rearrange("p (h d) -> p h d", d=D)
                        qs = st[:, t, 0:RG * 2 * D].rearrange("p (h s d) -> p h s d", s=2, d=D)
                        k, ks = rs[:, t, RG * D:ROT], st[:, t, RG * 2 * D:ST].rearrange("p (s d) -> p s d", d=D)
                        nc.scalar.activation(qs[:, :, 0, :], q, ACT.Copy)
                        nc.scalar.activation(ks[:, 0:3:2, :], k.unsqueeze(1).broadcast_to([P, 2, D]), ACT.Copy)\
                            .then_inc(rounded, 1)
                    elif kind == "b_v":
                        g, t = a
                        fb.wait_drained(act, ("b_pj", g, t))
                        nc.scalar.activation(va["h"][:, t, g, :, :], vf[:, g % 2, t, :].unsqueeze(1).broadcast_to([P, 2, D]),
                                             ACT.Copy).then_inc(va_hi, 1)
                    elif kind == "b_kx":
                        g, = a
                        fb.wait_full(act, s)
                        fb.drained(nc.scalar.activation(kt[:, g % 2, :, :],
                                   fb.bank(s)[:, :].rearrange("p (h l) -> p h l", l=L), ACT.Copy), s)
                    elif kind == "b_qx":
                        g, j = a
                        fb.wait_full(act, s)
                        fb.drained(nc.scalar.activation(qt[:, g % 2, 2 * j:2 * j + 2, :],
                                   fb.bank(s)[:, :].rearrange("p (h l) -> p h l", l=L), ACT.Copy), s)
                    elif kind == "b_e":
                        u, = a
                        act.wait_ge(nm_ready, u + 1)
                        if u >= 2:
                            fb.wait_full(act, ("b_t", u - 2, 1))
                        for h in range(RG):
                            ins = nc.scalar.activation(pr[:, u % 2, h, :], sm[:, u % 2, h, :], ACT.Exp,
                                                       bias=nm[:, u % 2, h:h + 1], scale=SCALE,
                                                       accum_out=rsum[:, u % 2, h:h + 1])
                        ins.then_inc(exp_done, 1)
                    elif kind == "b_t":
                        u, j = a
                        fb.wait_full(act, s)
                        if u >= 2:
                            fb.wait_full(act, ("b_o", u - 2))
                        nc.scalar.activation(pt["h"][:, u % 2, :, j * 2 * P:(j + 1) * 2 * P],
                                             fb.bank(s)[:, :].rearrange("p (k n) -> p k n", k=T), ACT.Copy)\
                            .then_inc(pt_hi, 1)
                    elif kind == "b_h":
                        u, = a
                        g, t = u // T, u % T
                        act.wait_ge(on_ready, u + 1)
                        fb.wait_drained(act, ("b_o", u))
                        nc.scalar.activation(ot["h"][:, 2 * g:2 * g + 2, t * P:(t + 1) * P], on[:, u % 2, :, :], ACT.Copy)\
                            .then_inc(ot_hi, 1)
            iterations(act, body)

        @block.vector
        def _(dve):
            own = [0]

            def link(ins):
                own[0] += 1
                ins.then_inc(s_own["dve"], 1)
                dve.wait_ge(s_own["dve"], own[0])

            def norm_guess():
                for t in range(T):
                    i = nc.vector.bn_stats(stats[:, t, :], xin[:, t, :])
                link(i)
                for t in range(T):
                    i = nc.vector.bn_aggr(mv[:, t, :], stats[:, t, :])
                link(i)
                link(nc.vector.tensor_scalar(var[:, :], mv[:, :, 1], EPS, None, ALU.add))
                link(nc.vector.tensor_scalar(nt[:, :].bitcast(I32), var[:, :].bitcast(I32), 1, None,
                                             ALU.logical_shift_right))
                nc.vector.tensor_scalar(rstd[:, :].bitcast(I32), nt[:, :].bitcast(I32), -1.0, float(MAGIC),
                                        ALU.mult, ALU.add).then_inc(guess, 1)

            dve.wait_ge(xin_in, 16)
            norm_guess()
            for n, (o, m) in enumerate(chunks[:EARLY]):
                dve.wait_ge(w_hi, n + 1)
                nc.vector.tensor_tensor(wl[:, o:o + m], stage[n][:, 0:m], wh[:, o:o + m].bitcast(F),
                                        ALU.subtract).then_inc(split, 1)
                if n == 0:
                    dve.wait_ge(const_in, 48)
                    nc.vector.tensor_scalar(half[:, :], cst[:, :], 0.5, None, ALU.mult).then_inc(halved, 1)
            used = own[0]

            def body(b, attend, prepare, fetch):
                own[0] = 0 if attend else used
                fb, fa = fills(attend, prepare, fetch)
                for s in self_stages(attend, prepare, fetch):
                    kind, a = s[0], s[1:]
                    if kind == "a_norm":
                        if a[0]:
                            dve.wait_ge(fetched, 1)
                            norm_guess()
                    elif kind == "a_xn":
                        if not attend:
                            dve.wait_ge(rstd_ready, 1)
                        for t in range(T):
                            nc.vector.tensor_scalar(xn[:, t, :], xin[:, t, :], mv[:, t, 0:1], rstd[:, t:t + 1],
                                                    ALU.subtract, ALU.mult).then_inc(xn_ready, 1)
                    elif kind == "a_xt":
                        dve.wait_ge(xnt_hi, 1)
                        fa.drained(nc.vector.tensor_tensor(xnt["l"][:, :, :],
                                   fa.bank(s)[:, :].rearrange("p (c l) -> p c l", l=L),
                                   xnt["h"][:, :, :].bitcast(F), ALU.subtract), s)
                    elif kind == "a_ix":
                        t, = a
                        dve.wait_ge(ist_hi, t + 1)
                        ps = fa.bank(s)
                        hs = ist[:, t, 0:HI * 2 * D].rearrange("p (h s d) -> p h s d", s=2, d=D)
                        ks = ist[:, t, HI * 2 * D:ST].rearrange("p (s d) -> p s d", d=D)
                        nc.vector.tensor_tensor(hs[:, :, 1, :], ps[:, 0:HI * D].rearrange("p (h d) -> p h d", d=D),
                                                hs[:, :, 0, :].bitcast(F), ALU.subtract)
                        fa.drained(nc.vector.tensor_tensor(ks[:, 1, :], ps[:, HI * D:HI * D + D],
                                                           ks[:, 0, :].bitcast(F), ALU.subtract), s)
                    elif kind == "a_sc":
                        t, j = a
                        if j == 0:
                            dve.wait_ge(wt_ready, t + 1)
                        fa.wait_drained(dve, ("a_si", t, j))
                        for i in range(2):
                            h = 2 * j + i
                            wt = wt1[:, t, h:h + 1]
                            if h == 0:
                                ins = nc.vector.tensor_scalar(score[:, t, :], sig[:, j, i, :], wt, None, ALU.mult)
                            else:
                                ins = nc.vector.scalar_tensor_tensor(score[:, t, :], sig[:, j, i, :], wt,
                                                                     score[:, t, :], ALU.mult, ALU.add)
                            if i == 0:
                                link(ins)
                            else:
                                ins.then_inc(sig_used, 1)
                                dve.wait_ge(sig_used, 2 * t + j + 1)
                    elif kind in ("a_tk", "b_tk"):
                        for t in range(T):
                            nc.vector.max(top8[:, t, :], score[:, t, :]).then_inc(s_own["dve"], 1)
                        for t in range(T):
                            own[0] += 1
                            dve.wait_ge(s_own["dve"], own[0])
                            nc.vector.match_replace(score[:, t, :], top8[:, t, :], score[:, t, :], TAKEN)\
                                .then_inc(s_own["dve"], 1)
                        own[0] += T
                        dve.wait_ge(s_own["dve"], own[0])
                    elif kind == "b_cp":
                        nc.vector.tensor_copy(xct["l"][:, :, :], xnt["l"][:, :, :].bitcast(F)).then_inc(xct_ready, 1)
                    elif kind == "b_mk":
                        link(nc.vector.tensor_scalar(mb[:, :, :], score[:, :, :], TAKEN / 2, MASKED, ALU.is_ge, ALU.mult))
                    elif kind == "b_vg":
                        fb.wait_full(dve, s)
                        ins = nc.vector.tensor_tensor(vg[:, :, :], fb.bank(s)[:, :].rearrange("p (t n) -> p t n", t=T),
                                                      cst[:, K_BVG:K_BVG + G * D].unsqueeze(1).broadcast_to([P, T, G * D]),
                                                      ALU.add)
                        fb.drained(ins, s)
                    elif kind == "b_pj":
                        g, t = a
                        n = g * T + t
                        fb.wait_full(dve, s)
                        if g:
                            dve.wait_ge(summed, n - 1)
                        ps = fb.bank(s)
                        r5 = ps[:, 0:ROT].rearrange("p (h s d) -> p h s d", s=2, d=D // 2)
                        o5 = t2[:, t, :].rearrange("p (h s d) -> p h s d", s=2, d=D // 2)
                        nc.vector.tensor_tensor(t1[:, t, :].rearrange("p (h d) -> p h d", d=D),
                                                ps[:, 0:ROT].rearrange("p (h d) -> p h d", d=D),
                                                cs[:, t, 0, :].unsqueeze(1).broadcast_to([P, RG + 1, D]), ALU.mult)
                        nc.vector.tensor_tensor(o5, r5[:, :, ::-1, :],
                                                cs[:, t, 1, :].rearrange("p (s d) -> p s d", s=2).unsqueeze(1)
                                                .broadcast_to([P, RG + 1, 2, D // 2]), ALU.mult).then_inc(turned, 1)
                        if n == 0:
                            dve.wait_ge(vg_ready, 1)
                        if g >= 2:
                            dve.wait_ge(va_ready, n - 3)
                        fb.drained(nc.vector.scalar_tensor_tensor(vf[:, g % 2, t, :], vg[:, t, g * D:(g + 1) * D], 1.0,
                                                                  ps[:, ROT:NPJ], ALU.add, ALU.mult), s)
                    elif kind == "b_s":
                        u, j = a
                        t = u % T
                        fb.wait_full(dve, s)
                        if u >= 2 and j == 0:
                            dve.wait_ge(exp_done, u - 1)
                        for i in range(2):
                            h = 2 * j + i
                            ins = nc.vector.tensor_tensor_reduce(
                                out=sm[:, u % 2, h, :], in0=fb.bank(s)[:, i * L:(i + 1) * L], in1=mb[:, t, :],
                                scale=1.0, scalar=LOWEST, op0=ALU.add, op1=ALU.max, accum_out=mx[:, u % 2, h:h + 1])
                        fb.drained(ins, s)
                        if j == 1:
                            fb.wait_drained(dve, s)
                            nc.vector.tensor_scalar(nm[:, u % 2, :], mx[:, u % 2, :], -SCALE, None, ALU.mult)\
                                .then_inc(nm_ready, 1)
                    elif kind == "b_n":
                        u, = a
                        dve.wait_ge(exp_done, u + 1)
                        nc.vector.reciprocal(rinv[:, u % 2, :], rsum[:, u % 2, :]).then_inc(rinv_ready, 1)
                    elif kind == "b_l":
                        u, j = a
                        dve.wait_ge(pt_hi, 2 * u + j + 1)
                        to = [pt[k][:, u % 2, :, j * 2 * P:(j + 1) * 2 * P] for k in "hl"]
                        fb.drained(nc.vector.tensor_tensor(
                            to[1], fb.bank(("b_t", u, j))[:, :].rearrange("p (k n) -> p k n", k=T), to[0].bitcast(F),
                            ALU.subtract), ("b_t", u, j))
                    elif kind == "b_g":
                        u, = a
                        g, t = u // T, u % T
                        if u == 0:
                            for j in range(HT // 2):
                                fb.wait_drained(dve, ("b_og", j))
                        fb.wait_full(dve, ("b_o", u))
                        if u >= 2:
                            dve.wait_ge(ot_ready, u - 1)
                        o = fb.bank(("b_o", u))[:, :].rearrange("p (i v q) -> p i v q", v=2, q=P)
                        for v, part in enumerate((slice(0, D), slice(D, P))):
                            ins = nc.vector.scalar_tensor_tensor(
                                on[part, u % 2, :, :], g1t[part, 2 * g:2 * g + 2, t * P:(t + 1) * P], 1.0,
                                o[part, :, v, :], ALU.add, ALU.mult)
                            if v == 0:
                                ins.then_inc(on_ready, 1)
                        fb.drained(ins, ("b_o", u))
                    elif kind in ("b_w0", "b_w1b"):
                        t = int(kind == "b_w1b")
                        s = ("b_w1a",) if t else s
                        fb.wait_full(dve, s)
                        if t == 0:
                            dve.wait_ge(last_add, 1)
                        fb.drained(nc.vector.scalar_tensor_tensor(x1b[:, t, :], fb.bank(s)[:, 0:C], 0.25, xres[:, t, :],
                                                                  ALU.mult, ALU.add), s)
            iterations(dve, body)

        @block.tensor
        def _(pe):
            pe.wait_ge(const_in, 48)

            def mm(out, lhs, rhs, start, stop):
                return nc.tensor.matmul(out, lhs, rhs, start=start, stop=stop)

            def project(out, lhs, rhs, tiles, start=True, stop=True):
                pairs = [(c, a, b) for c in (range(tiles) if isinstance(tiles, int) else tiles) for a, b in PRODUCTS]
                for n, (c, a, b) in enumerate(pairs):
                    ins = mm(out, lhs(a, c), rhs(b, c), start and n == 0, stop and n == len(pairs) - 1)
                return ins

            def weight(o, width, at, n):
                return lambda k, c: w[k][:, o + c * width + at:o + c * width + at + n]

            def body(b, attend, prepare, fetch):
                fb, fa = fills(attend, prepare, fetch)
                for s in self_stages(attend, prepare, fetch):
                    kind, a = s[0], s[1:]
                    if kind == "a_xt":
                        pe.wait_ge(xn_ready, T)
                        fa.wait_free(pe, s)
                        for c in range(CT):
                            for t in range(T):
                                o = c * L + t * P
                                ins = nc.tensor.transpose(fa.bank(s)[:, o:o + P], xn[:, t, c * P:(c + 1) * P], idn[:, :])
                        fa.filled(ins, s)
                    elif kind == "a_ix":
                        t, = a
                        if not attend:
                            pe.wait_ge(split, 1)
                        fa.wait_drained(pe, ("a_xt",))
                        fa.wait_free(pe, s)
                        fa.filled(project(fa.bank(s)[:, 0:NIDX], lambda k, c: xnt[k][:, c, t * P:(t + 1) * P],
                                          weight(O_IDX, NIDX, 0, NIDX), CT), s)
                    elif kind == "a_iqx":
                        j, = a
                        for t in range(T):
                            fa.wait_drained(pe, ("a_ix", t))
                        fa.wait_free(pe, s)
                        for i in range(2):
                            for t in range(T):
                                o = i * L + t * P
                                h = 2 * j + i
                                ins = nc.tensor.transpose(fa.bank(s)[:, o:o + P],
                                                          ist[:, t, h * P:(h + 1) * P].bitcast(F), idn[:, :])
                        fa.filled(ins, s)
                    elif kind == "a_ikx":
                        fa.wait_free(pe, s)
                        for i in range(2):
                            for t in range(T):
                                o, f = i * L + t * P, HI * 2 * D + i * D
                                ins = nc.tensor.transpose(fa.bank(s)[:, o:o + P], ist[:, t, f:f + P].bitcast(F), idn[:, :])
                        fa.filled(ins, s)
                    elif kind == "a_si":
                        t, j = a
                        fa.wait_drained(pe, ("a_ikx",))
                        fa.wait_drained(pe, ("a_iqx", j))
                        fa.wait_free(pe, s)
                        for i in range(2):
                            for k in range(2):
                                ins = mm(fa.bank(s)[:, i * L:(i + 1) * L], iqt[:, 2 * j + i, t * P:(t + 1) * P],
                                         ikt[:, k, :], k == 0, k == 1)
                        fa.filled(ins, s)
                    elif kind == "b_vg":
                        for t in range(T):
                            ins = project(fb.bank(s)[:, t * L:(t + 1) * L], lambda k, c: xnt[k][:, c, t * P:(t + 1) * P],
                                          weight(O_VG, G * D, 0, G * D), CT)
                        fb.filled(ins, s)
                    elif kind == "b_og":
                        j, = a
                        pe.wait_ge(xct_ready, 2)
                        fb.wait_free(pe, s)
                        for i in range(2):
                            ins = project(fb.bank(s)[:, i * L:(i + 1) * L], weight(O_OG, H * D, (2 * j + i) * P, P),
                                          lambda k, c: xct[k][:, c, :], CT)
                        fb.filled(ins, s)
                    elif kind == "b_pj":
                        g, t = a
                        src = xct if g else xnt
                        if g:
                            pe.wait_ge(xct_ready, 2)
                        fb.wait_free(pe, s)
                        fb.filled(project(fb.bank(s)[:, 0:NPJ], lambda k, c: src[k][:, c, t * P:(t + 1) * P],
                                          weight(O_PJ, G * NPJ, g * NPJ, NPJ), CT), s)
                    elif kind == "b_kx":
                        g, = a
                        pe.wait_ge(stacked, T * (g + 1))
                        fb.wait_free(pe, s)
                        for i in range(2):
                            for t in range(T):
                                o, f = i * L + t * P, RG * 2 * D + i * D
                                ins = nc.tensor.transpose(fb.bank(s)[:, o:o + P], st[:, t, f:f + P].bitcast(F), idn[:, :])
                        fb.filled(ins, s)
                    elif kind == "b_qx":
                        g, j = a
                        fb.wait_free(pe, s)
                        for i in range(2):
                            for t in range(T):
                                o, h = i * L + t * P, 2 * j + i
                                ins = nc.tensor.transpose(fb.bank(s)[:, o:o + P], st[:, t, h * P:(h + 1) * P].bitcast(F),
                                                          idn[:, :])
                        fb.filled(ins, s)
                    elif kind == "b_s":
                        u, j = a
                        g, t = u // T, u % T
                        fb.wait_drained(pe, ("b_kx", g))
                        fb.wait_drained(pe, ("b_qx", g, j))
                        fb.wait_free(pe, s)
                        for i in range(2):
                            for k in range(2):
                                ins = mm(fb.bank(s)[:, i * L:(i + 1) * L], qt[:, g % 2, 2 * j + i, t * P:(t + 1) * P],
                                         kt[:, g % 2, k, :], k == 0, k == 1)
                        fb.filled(ins, s)
                    elif kind == "b_t":
                        u, j = a
                        pe.wait_ge(pr_ready[j], u + 1)
                        fb.wait_free(pe, s)
                        for k in range(T):
                            for i in range(2):
                                o = k * 2 * P + i * P
                                ins = nc.tensor.transpose(fb.bank(s)[:, o:o + P],
                                                          pr[:, u % 2, 2 * j + i, k * P:(k + 1) * P], idn[:, :])
                        fb.filled(ins, s)
                    elif kind == "b_o":
                        u, = a
                        g = u // T
                        for j in range(2):
                            fb.wait_drained(pe, ("b_t", u, j))
                        pe.wait_ge(va_ready, T * (g + 1))
                        fb.wait_free(pe, s)
                        fb.filled(project(fb.bank(s)[:, :], lambda m, k: va[m][:, k, g, :, :].rearrange("p a d -> p (a d)"),
                                          lambda m, k: pt[m][:, u % 2, k, :], T), s)
                    elif kind == "b_w0":
                        pe.wait_ge(ot_ready, G * T - 1)
                        fb.wait_free(pe, s)
                        fb.filled(project(fb.bank(s)[:, 0:C], lambda k, c: ot[k][:, c, 0:P], weight(O_WO, C, 0, C), HT), s)
                    elif kind == "b_w1a":
                        pe.wait_ge(ot_ready, G * T - T)
                        fb.wait_free(pe, s)
                        project(fb.bank(s)[:, 0:C], lambda k, c: ot[k][:, c, P:2 * P], weight(O_WO, C, 0, C),
                                range(0, HT - 2), stop=False)
                    elif kind == "b_w1b":
                        pe.wait_ge(ot_ready, G * T)
                        fb.filled(project(fb.bank(("b_w1a",))[:, 0:C], lambda k, c: ot[k][:, c, P:2 * P],
                                          weight(O_WO, C, 0, C), range(HT - 2, HT), start=False), ("b_w1a",))
            iterations(pe, body)


LC = 120
HX, DX = 16, 16
HPT = P // DX
HC = 4
XSCALE = DX ** -0.5
NEG = 1.0e9
E, I = 8, 128
NGRP, TOPG, TOPK = 4, 2, 2
GSZ = E // NGRP

O_XQ = 0
O_XK = O_XQ + CT * C
O_XV = O_XK + CT * C
O_XO = O_XV + CT * C
O_GT = O_XO + CT * C
O_G = O_GT + CT * E
O_U = O_G + CT * E * I
O_DN = O_U + CT * E * I
N_W2 = O_DN + E * C

K_XQB = 0
K_XKB = K_XQB + CT
K_XVB = K_XKB + CT
K_XOB = K_XVB + C
K_ESB = K_XOB + C
K_BD = K_ESB + E
K_TRI = K_BD + HPT
K_TRG = K_TRI + E * E
N_K2 = K_TRG + NGRP * NGRP


RT = 20
POOLED = (1, 3)


def finisher(i, t):
    n = i * T + t
    pooled = n in POOLED
    return int(pooled), sum((m in POOLED) == pooled for m in range(n + 1))


CROSS_ORDER = ordered("""
    f_gt c_ng c_l.0.0 c_lx.0.0 f_gu.0 f_cp c_l.0.1 f_rt.0 c_lx.0.1 f_g2 c_xb c_l.1.0 f_gv.0 c_lx.1.0
    c_e.0.0 f_gu.1 f_rt.1 c_l.1.1 f_rt.2 c_r.0.0 f_gv.1 f_rt.3 f_rt.4 f_gu.2 f_rt.5 c_m.0.0 c_lx.1.1
    f_rt.6 f_gv.2 c_l.2.0 f_rt.7 c_e.0.1 c_ct.1 c_r.0.1 f_rt.8 c_lx.2.0 c_l.2.1 c_e.1.0 f_rt.9
    f_gu.3 f_rt.10 c_m.0.1 c_p.0.0 f_gv.3 c_kv.1 f_rt.11 f_rt.12 f_rt.13 f_rt.14 f_gu.4 f_rt.15
    f_gv.4 f_rt.16 f_rt.17 c_lx.2.1 f_rt.18 c_e.1.1 c_r.1.0 c_kb.1.0 c_m.1.0 c_p.0.1 c_m.1.1 c_r.1.1
    f_rt.19 f_gu.5 c_p.1.0 c_l.3.0 f_gv.5 c_lx.3.0 c_e.2.0 c_l.3.1 c_p.1.1 c_lx.3.1 c_r.2.0 c_m.2.0
    c_kb.1.1 c_norm.1 c_e.2.1 f_cb.0 f_h.0 f_h.1 c_e.3.0 f_hh.0 c_r.2.1 f_h.2 c_m.2.1 f_gu.6 c_p.2.0
    f_gv.6 f_cb.1 f_h.3 f_hh.1 c_e.3.1 c_o.0 c_r.3.0 c_p.2.1 f_cb.2 c_m.3.0 f_h.4 f_h.5 f_hh.2
    f_hh.3 f_hh.4 c_p.3.0 c_r.3.1 f_hh.5 c_m.3.1 c_ol.0 c_xn.1 f_gu.7 f_cb.3 f_h.6 c_p.3.1 f_gv.7
    c_xt.1 c_o.1 f_h.7 f_hh.6 f_hh.7 c_ol.1 c_q.1.0 c_q.1.1 c_w c_n2 c_x2 f_dn.0 f_dn.1 c_x3 c_v.1
""")
AHEAD = ordered("""
    c_ct.1 c_kv.1 c_kb.1.0 c_kb.1.1 c_norm.1 c_xn.1 c_xt.1 c_q.1.0 c_q.1.1 c_v.1
""")
FIRST = ordered("""
    c_norm.0 c_ct.0 c_kv.0 c_kb.0.0 c_kb.0.1 c_v.0 c_xn.0 c_xt.0 c_q.0.0 c_q.0.1 w_lo
""")
assert sum(s[0] == "f_rt" for s in CROSS_ORDER) == RT
assert sum(s[0] == "c_e" for s in CROSS_ORDER) == HX // HC * T


def cross_stages(feed, prepare, fetch):
    def takes_part(stage):
        if stage[0].startswith("f_"):
            return feed
        return fetch if stage in AHEAD else prepare
    return ([] if feed else FIRST) + [s for s in CROSS_ORDER if takes_part(s)]


def cross_and_feed(nc, keep, x1, ctxt, gp, mask, out, w2, k2, ident, batches=B):
    with ExitStack() as ctx:
        def sb(name, shape, dt=F):
            return ctx.enter_context(nc.sbuf_tensor("x_" + name, shape, dt))

        sems = []

        def sem(name):
            sems.append(keep.enter_context(nc.semaphore("x_" + name)))
            return sems[-1]

        wh, wl = sb("wh", [P, N_W2], R), sb("wl", [P, N_W2], R)
        w = {"h": wh, "l": wl}
        cst = sb("cst", [P, N_K2])
        idn = sb("idn", [P, P])
        qb4 = sb("qb4", [P, CT])
        xin = sb("xin", [P, T, C])
        cin = sb("cin", [P, C])
        gpt = sb("gpt", [P, T, LC])
        mi = sb("mi", [P, T, LC], I32)
        neg = sb("neg", [P, T, LC])
        stats, mv = sb("stats", [P, T, 6]), sb("mv", [P, T, 2])
        var, rstd, nt = sb("var", [P, T]), sb("rstd", [P, T]), sb("nt", [P, T])
        stats2, mv2 = sb("stats2", [P, T, 6]), sb("mv2", [P, T, 2])
        var2, rstd2, nt2 = sb("var2", [P, T]), sb("rstd2", [P, T]), sb("nt2", [P, T])
        xn = sb("xn", [P, T, C])
        xnt = {k: sb("xnt" + k, [P, CT, L], R) for k in "hl"}
        ctt = {k: sb("ctt" + k, [P, CT, LC], R) for k in "hl"}
        kf = sb("kf", [P, CT, LC])
        kr = {k: sb("kr" + k, [P, CT, LC], R) for k in "hl"}
        kbd = {k: sb("kbd" + k, [P, CT, HPT, LC], R) for k in "hl"}
        vf = sb("vf", [P, C])
        vpad = sb("vpad", [P, CT, HPT, P])
        qf = sb("qf", [P, CT, L])
        qx = {k: sb("qx" + k, [P, CT, L], R) for k in "hl"}
        lm = sb("lm", [P, T, HX, LC])
        mx, nmx = sb("mx", [P, T, HX]), sb("nmx", [P, T, HX])
        sm, rs = sb("sm", [P, T, HX]), sb("rs", [P, T, HX])
        ptc = sb("ptc", [P, HX, L])
        ox = {k: sb("ox" + k, [P, CT, L], R) for k in "hl"}
        xres, xb = sb("xres", [P, T, C]), sb("xb", [P, T, C])
        x2n = sb("x2n", [P, T, C])
        x2t = {k: sb("x2t" + k, [P, CT, L], R) for k in "hl"}
        x2c = sb("x2c", [P, T, C])
        gl = sb("gl", [E, L])
        sc, sfc, tmp = sb("sc", [P, T, E]), sb("sfc", [P, T, E]), sb("tmp", [P, T, E])
        gs, gm = sb("gs", [P, T, NGRP]), sb("gm", [P, T, NGRP])
        c1, c2 = sb("c1", [P, T, E, E]), sb("c2", [P, T, E, E])
        rk, cw = sb("rk", [P, T, E]), sb("cw", [P, T, E])
        ws, wr = sb("ws", [P, T]), sb("wr", [P, T])
        sg = sb("sg", [P, 2, L])
        gs2 = sb("gs2", [P, 2, L])
        hu = sb("hu", [P, E, L])
        hf = sb("hf", [P, 4, L])
        hr = {k: sb("hr" + k, [P, E, L], R) for k in "hl"}
        ob = sb("ob", [P, T, C])

        psb = [ctx.enter_context(nc.psum_tensor(f"x_ps{i}", [P, 512], F)) for i in range(8)]
        full, free = [sem(f"full{i}") for i in range(8)], [sem(f"free{i}") for i in range(8)]
        s_own = {e: sem("own_" + e) for e in ("dve", "pool")}
        arrive, mi_here = sem("arrive"), sem("mi_here")
        guess, rstd_ready, xn_ready = sem("guess"), sem("rstd_ready"), sem("xn_ready")
        xin_read, xin_here, ctx_here = sem("xin_read"), sem("xin_here"), sem("ctx_here")
        v_ready, q_hi, rt_step, gs_ready = sem("v_ready"), sem("q_hi"), sem("rt_step"), sem("gs_ready")
        hr_hi, rs_ready = sem("hr_hi"), sem("rs_ready")
        ctt_hi, xnt_hi, ox_hi, x2t_hi = sem("ctt_hi"), sem("xnt_hi"), sem("ox_hi"), sem("x2t_hi")
        neg_ready, kf_ready, kbd_ready = sem("neg_ready"), sem("kf_ready"), sem("kbd_ready")
        qx_ready, nmx_ready, exp_done = sem("qx_ready"), sem("nmx_ready"), sem("exp_done")
        pc_ready = [sem("pc_ready0"), sem("pc_ready1")]
        x2c_ready = sem("x2c_ready")
        sg_ready, hf_ready, hr_ready = sem("sg_ready"), sem("hf_ready"), sem("hr_ready")
        gp_here, xb_ready, last_add = sem("gp_here"), sem("xb_ready"), sem("last_add")
        xres_here = sem("xres_here")
        in_iteration = list(sems)
        go, passed = sem("go"), sem("passed")
        const_in, split, w_hi = sem("const_in"), sem("split"), sem("w_hi")
        stage_in = [sem(f"stage_in{n}") for n in range(9)]
        late_split, halved = sem("late_split"), sem("halved")
        xin_in, ctx_in, mi_in, gp_in, xres_in = (sem(n) for n in ("xin_in", "ctx_in", "mi_in", "gp_in", "xres_in"))
        stored, zeroed = sem("stored"), sem("zeroed")
        first, last = in_iteration[0].num, in_iteration[-1].num
        assert last - first == len(in_iteration) - 1

        def fills(feed, prepare, fetch):
            stages = cross_stages(feed, prepare, fetch)
            return (Fills(psb[0:4], full[0:4], free[0:4],
                          [s for s in stages if s[0] in ("f_gt", "f_g2", "f_gu", "f_cb", "f_dn")]),
                    Fills(psb[4:8], full[4:8], free[4:8],
                          [s for s in stages if s[0] in ("c_ct", "c_kv", "c_xt", "c_q", "c_l", "c_p", "c_o", "c_w", "c_x3")]))

        def iterations(eng, body):
            def meet(n):
                eng.drain().then_inc(arrive, 1)
                eng.wait_ge(go, n)
                eng.sem_inc(passed, 1)
            body(-1, False, True, True)
            meet(1)
            if batches > 2:
                with eng.Fori(0, batches - 2) as b:
                    body(b, True, True, True)
                    meet(b + 2)
            body(batches - 2, True, True, False)
            meet(batches)
            body(batches - 1, True, False, False)
            meet(batches + 1)

        def finish(eng, unit, link, i, t):
            mine, count = finisher(i, t)
            if mine != int(unit is nc.gpsimd):
                return
            eng.wait_ge(rs_ready, i * T + t + 1)
            if count == 1:
                eng.wait_ge(gp_here, 1)
            heads = slice(i * HC, (i + 1) * HC)
            if mine:
                these = lm[:, t, heads, :]
                link(unit.tensor_tensor(these, these, rs[:, t, heads].unsqueeze(2).broadcast_to([P, HC, LC]), ALU.mult))
                ins = unit.tensor_tensor(these, these, gpt[:, t, :].unsqueeze(1).broadcast_to([P, HC, LC]),
                                         ALU.mult)
            else:
                for h in range(i * HC, (i + 1) * HC):
                    ins = unit.scalar_tensor_tensor(lm[:, t, h, :], lm[:, t, h, :], rs[:, t, h:h + 1], gpt[:, t, :],
                                                    ALU.mult, ALU.mult)
            ins.then_inc(pc_ready[mine], 1)

        def nth(feed, k):
            return 1 if feed else 1 + k

        CH, EARLY = 1024, 6
        stage = [v[:, n * CH:(n + 1) * CH] for v, k in ((lm[:, :, :, :].rearrange("p a b c -> p (a b c)"), 2),
                                                        (ptc[:, :, :].rearrange("p a b -> p (a b)"), 4),
                                                        (hu[:, :, :].rearrange("p a b -> p (a b)"), 2),
                                                        (hf[:, :, :].rearrange("p a b -> p (a b)"), 1))
                 for n in range(k)]
        chunks = [(o, min(CH, N_W2 - o)) for o in range(0, N_W2, CH)]

        block = ctx.enter_context(nc.Block())

        @block.sync
        def _(sp):
            def rows(t, b):
                return t[bass.ds(b, 1)].rearrange("o (t p) c -> p (o t) c", p=P)

            def fetch_x(b):
                sp.dma_start(xin[:, :, :], rows(x1, b)).then_inc(xin_in, 16)

            def fetch_context(b):
                sp.dma_start(cin[0:LC, :], ctxt[bass.ds(b, 1)].rearrange("o p c -> p (o c)")).then_inc(ctx_in, 16)

            def fetch_mask(b):
                sp.dma_start(mi[:, :, :], rows(mask, b)).then_inc(mi_in, 16)

            fetch_x(0)
            fetch_context(0)
            fetch_mask(0)
            for n, (o, m) in enumerate(chunks):
                sp.dma_start(stage[n][:, 0:m], w2[:, o:o + m]).then_inc(stage_in[n], 16)
                if n == 0:
                    sp.dma_start(idn[:, :], ident).then_inc(const_in, 16)
                    sp.dma_start(cst[:, :], k2).then_inc(const_in, 16)

            def body(b, feed, prepare, fetch):
                ff, fc = fills(feed, prepare, fetch)
                if prepare:
                    sp.dma_start(gpt[:, :, :], rows(gp, b + 1)).then_inc(gp_in, 16)
                    sp.dma_start(xres[:, :, :], rows(x1, b + 1)).then_inc(xres_in, 16)
                if prepare:
                    sp.wait_ge(gp_in, (b + 2) * 16)
                    sp.sem_inc(gp_here, 1)
                    sp.wait_ge(xres_in, (b + 2) * 16)
                    sp.sem_inc(xres_here, 1)
                if fetch:
                    if not feed:
                        fc.wait_full(sp, ("c_ct", 0))
                        sp.wait_ge(xin_read, 1)
                    fetch_context(b + 2)
                    fetch_x(b + 2)
                    sp.wait_ge(neg_ready, 1)
                    fetch_mask(b + 2)
                    for fetched, here in ((xin_in, xin_here), (ctx_in, ctx_here), (mi_in, mi_here)):
                        sp.wait_ge(fetched, (b + 3) * 16)
                        sp.sem_inc(here, 1)
                if feed:
                    sp.wait_ge(stored, (b + PRIME) * 16)
                    sp.sem_inc(last_add, 1)
                    ff.wait_drained(sp, ("f_dn", 0))
                    ff.wait_drained(sp, ("f_dn", 1))
                    sp.dma_start(rows(out, b), ob[:, :, :]).then_inc(stored, 16)
                sp.wait_ge(arrive, 4)
                sp.sem_clear(range(first, last + 1))
                sp.sem_inc(go, 1)

            PRIME = 1
            sp.sem_inc(stored, 16)
            body(-1, False, True, True)
            if batches > 2:
                with sp.Fori(0, batches - 2) as b:
                    body(b, True, True, True)
            body(batches - 2, True, True, False)
            body(batches - 1, True, False, False)
            sp.wait_ge(stored, (batches + PRIME) * 16)
            sp.wait_ge(passed, 4 * (batches + 1))

        @block.gpsimd
        def _(pool):
            own = [0]

            def link(ins):
                own[0] += 1
                ins.then_inc(s_own["pool"], 1)
                pool.wait_ge(s_own["pool"], own[0])

            nc.gpsimd.memset(vpad[:, :, :, :], 0.0).then_inc(zeroed, 1)
            pool.wait_ge(const_in, 32)

            def body(b, feed, prepare, fetch):
                own[0] = 0
                ff, fc = fills(feed, prepare, fetch)
                for s in cross_stages(feed, prepare, fetch):
                    kind, a = s[0], s[1:]
                    if kind == "w_lo":
                        for n, (o, m) in list(enumerate(chunks))[EARLY:]:
                            pool.wait_ge(w_hi, n + 1)
                            nc.gpsimd.tensor_tensor(wl[:, o:o + m], stage[n][:, 0:m], wh[:, o:o + m].bitcast(F),
                                                    ALU.subtract).then_inc(late_split, 1)
                    elif kind == "c_norm":
                        pool.wait_ge(guess, nth(feed, a[0]))
                        for n in range(3):
                            link(nc.gpsimd.tensor_tensor(nt[:, :], rstd[:, :], rstd[:, :], ALU.mult))
                            link(nc.gpsimd.tensor_tensor(nt[:, :], nt[:, :], var[:, :], ALU.mult))
                            link(nc.gpsimd.tensor_scalar(nt[:, :], nt[:, :], -0.5, 1.5, ALU.mult, ALU.add))
                            i = nc.gpsimd.tensor_tensor(rstd[:, :], rstd[:, :], nt[:, :], ALU.mult)
                            if n < 2:
                                link(i)
                            else:
                                i.then_inc(rstd_ready, 1)
                    elif kind == "c_kb":
                        k, c = a
                        pool.wait_ge(kf_ready, nth(feed, k))
                        link(nc.gpsimd.tensor_copy(kr["h"][:, c, :], kf[:, c, :]))
                        link(nc.gpsimd.tensor_tensor(kr["l"][:, c, :], kf[:, c, :], kr["h"][:, c, :].bitcast(F), ALU.subtract))
                        if k:
                            fc.wait_full(pool, ("c_l", (c + 1) * HPT // HC - 1, T - 1))
                        for half in "hl":
                            ins = nc.gpsimd.tensor_tensor(
                                kbd[half][:, c, :, :],
                                kr[half][:, c, :].bitcast(F).unsqueeze(1).broadcast_to([P, HPT, LC]),
                                cst[:, K_BD:K_BD + HPT].unsqueeze(2).broadcast_to([P, HPT, LC]), ALU.mult)
                        ins.then_inc(kbd_ready, 1)
                    elif kind == "c_m":
                        finish(pool, nc.gpsimd, link, *a)
                    elif kind == "c_v":
                        k, = a
                        pool.wait_ge(kf_ready, nth(feed, k))
                        if k:
                            fc.wait_full(pool, ("c_o", CT - 1))
                        for c in range(CT):
                            to = vpad[0:LC, c, :, :].rearrange("p j n -> p (j n)")
                            blocks = to.rearrange("p (a b) -> p a b", b=DX)[:, 0:HPT * (P // DX):P // DX + 1, :]
                            ins = nc.gpsimd.tensor_copy(blocks, vf[0:LC, c * P:(c + 1) * P]
                                                        .rearrange("p (j d) -> p j d", d=DX))
                        ins.then_inc(v_ready, 1)
                    elif kind == "c_xb":
                        pool.wait_ge(xres_here, 1)
                        nc.gpsimd.tensor_tensor(xb[:, :, :], xres[:, :, :],
                                                cst[:, K_XOB:K_XOB + C].unsqueeze(1).broadcast_to([P, T, C]),
                                                ALU.add).then_inc(xb_ready, 1)
                    elif kind == "f_hh":
                        e, = a
                        pool.wait_ge(hr_hi, e + 1)
                        nc.gpsimd.tensor_tensor(hr["l"][:, e, :], hf[:, e % 4, :], hr["h"][:, e, :].bitcast(F), ALU.subtract)\
                            .then_inc(hr_ready, 1)
            iterations(pool, body)

        @block.scalar
        def _(act):
            for n, (o, m) in enumerate(chunks):
                act.wait_ge(stage_in[n], 16)
                nc.scalar.activation(wh[:, o:o + m], stage[n][:, 0:m], ACT.Copy).then_inc(w_hi, 1)
            act.wait_ge(halved, 1)
            act.wait_ge(split, EARLY)

            def halves_hi(fl, s, to, width, sem_hi):
                fl.wait_full(act, s)
                nc.scalar.activation(to[:, :, :], fl.bank(s)[:, 0:CT * width].rearrange("p (c l) -> p c l", l=width),
                                     ACT.Copy).then_inc(sem_hi, 1)

            def body(b, feed, prepare, fetch):
                ff, fc = fills(feed, prepare, fetch)
                for s in cross_stages(feed, prepare, fetch):
                    kind, a = s[0], s[1:]
                    if kind == "c_ct":
                        halves_hi(fc, s, ctt["h"], LC, ctt_hi)
                    elif kind == "f_gt":
                        ff.wait_full(act, s)
                        ff.drained(nc.scalar.activation(gl[0:E, :], ff.bank(s)[0:E, 0:L], ACT.Copy), s)
                    elif kind == "c_xt":
                        halves_hi(fc, s, xnt["h"], L, xnt_hi)
                    elif kind == "c_q":
                        k, f = a
                        if k and not feed:
                            act.wait_ge(qx_ready, CT)
                        fc.wait_full(act, s)
                        fc.drained(nc.scalar.activation(qf[:, f, :], fc.bank(s)[:, 0:L], ACT.Identity,
                                                        bias=qb4[:, f:f + 1], scale=XSCALE), s)
                        fc.wait_drained(act, s)
                        nc.scalar.activation(qx["h"][:, f, :], qf[:, f, :], ACT.Copy).then_inc(q_hi, 1)
                    elif kind == "c_e":
                        i, t = a
                        act.wait_ge(nmx_ready, i * T + t + 1)
                        for h in range(i * HC, (i + 1) * HC):
                            ins = nc.scalar.activation(lm[:, t, h, :], lm[:, t, h, :], ACT.Exp,
                                                       bias=nmx[:, t, h:h + 1], accum_out=sm[:, t, h:h + 1])
                        ins.then_inc(exp_done, 1)
                    elif kind == "c_p":
                        i, t = a
                        fc.wait_full(act, s)
                        fc.drained(nc.scalar.activation(ptc[0:LC, i * HC:(i + 1) * HC, t * P:(t + 1) * P],
                                   fc.bank(s)[0:LC, :].rearrange("p (h q) -> p h q", q=P), ACT.Copy), s)
                    elif kind == "c_ol":
                        f, = a
                        fc.wait_full(act, ("c_o", f))
                        nc.scalar.activation(ox["h"][:, f, :], fc.bank(("c_o", f))[:, 0:L], ACT.Copy).then_inc(ox_hi, 1)
                    elif kind == "c_x3":
                        if feed:
                            ff.wait_full(act, ("f_gu", E - 1))
                        halves_hi(fc, s, x2t["h"], L, x2t_hi)
                    elif kind == "f_cp":
                        nc.scalar.activation(x2c[:, :, :], x2n[:, :, :], ACT.Copy).then_inc(x2c_ready, 1)
                    elif kind == "f_g2":
                        ff.wait_full(act, s)
                        ff.drained(nc.scalar.activation(sc[:, :, :], ff.bank(s)[:, 0:T * E].rearrange("p (t e) -> p t e", e=E),
                                                        ACT.Exp, scale=-1.0), s)
                    elif kind == "f_hh":
                        e, = a
                        if e % 2:
                            ff.wait_drained(act, ("f_cb", e // 2))
                        else:
                            act.wait_ge(hf_ready, e // 2 + 1)
                        nc.scalar.activation(hr["h"][:, e, :], hf[:, e % 4, :], ACT.Copy).then_inc(hr_hi, 1)
                    elif kind == "f_gu":
                        e, = a
                        ff.wait_full(act, s)
                        if e >= 2:
                            ff.wait_drained(act, ("f_gu", e - 2))
                        nc.scalar.activation(sg[:, e % 2, :], ff.bank(s)[:, 0:L], ACT.Tanh, scale=0.5).then_inc(sg_ready, 1)
            iterations(act, body)

        @block.vector
        def _(dve):
            own = [0]

            def link(ins):
                own[0] += 1
                ins.then_inc(s_own["dve"], 1)
                dve.wait_ge(s_own["dve"], own[0])

            def norm_guess(src, stats, mv, var, nt, rstd):
                for t in range(T):
                    i = nc.vector.bn_stats(stats[:, t, :], src[:, t, :])
                link(i)
                for t in range(T):
                    i = nc.vector.bn_aggr(mv[:, t, :], stats[:, t, :])
                link(i)
                link(nc.vector.tensor_scalar(var[:, :], mv[:, :, 1], EPS, None, ALU.add))
                link(nc.vector.tensor_scalar(nt[:, :].bitcast(I32), var[:, :].bitcast(I32), 1, None,
                                             ALU.logical_shift_right))
                return nc.vector.tensor_scalar(rstd[:, :].bitcast(I32), nt[:, :].bitcast(I32), -1.0, float(MAGIC),
                                               ALU.mult, ALU.add)

            dve.wait_ge(xin_in, 16)
            norm_guess(xin, stats, mv, var, nt, rstd).then_inc(guess, 1)
            for n, (o, m) in enumerate(chunks[:EARLY]):
                dve.wait_ge(w_hi, n + 1)
                nc.vector.tensor_tensor(wl[:, o:o + m], stage[n][:, 0:m], wh[:, o:o + m].bitcast(F),
                                        ALU.subtract).then_inc(split, 1)
                if n == 0:
                    dve.wait_ge(const_in, 32)
                    nc.vector.tensor_scalar(qb4[:, :], cst[:, K_XQB:K_XQB + CT], XSCALE, None, ALU.mult).then_inc(halved, 1)
            dve.wait_ge(split, EARLY)
            dve.wait_ge(zeroed, 1)
            dve.wait_ge(mi_in, 16)
            used = own[0]

            def normalise(src, mv, rstd):
                for t in range(T):
                    ins = nc.vector.tensor_scalar(xn[:, t, :], src[:, t, :], mv[:, t, 0:1], rstd[:, t:t + 1],
                                                  ALU.subtract, ALU.mult)
                return ins

            def halves_lo(fl, s, to, width, sem_hi, n=1):
                dve.wait_ge(sem_hi, n)
                fl.drained(nc.vector.tensor_tensor(
                    to["l"][:, :, :], fl.bank(s)[:, 0:CT * width].rearrange("p (c l) -> p c l", l=width),
                    to["h"][:, :, :].bitcast(F), ALU.subtract), s)

            def chosen(score, n, tri, top, out):
                rows = (P, T, n, n)
                own_, other = score.unsqueeze(3).broadcast_to(rows), score.unsqueeze(2).broadcast_to(rows)
                first = cst[:, tri:tri + n * n].rearrange("p (i j) -> p i j", j=n)
                above, equal = c1[:, :, 0:n, 0:n], c2[:, :, 0:n, 0:n]

                def compare():
                    for t in range(T):
                        nc.vector.tensor_tensor(above[:, t], other[:, t], own_[:, t], ALU.is_gt)
                        ins = nc.vector.tensor_tensor(equal[:, t], other[:, t], own_[:, t], ALU.is_equal)
                    return ins

                def before():
                    for t in range(T):
                        ins = nc.vector.tensor_tensor(equal[:, t], equal[:, t], first, ALU.mult)
                    return ins

                def both():
                    for t in range(T):
                        ins = nc.vector.tensor_tensor(above[:, t], above[:, t], equal[:, t], ALU.add)
                    return ins

                def rank():
                    return nc.vector.tensor_reduce(rk[:, :, 0:n], above, mybir.AxisListType.X, ALU.add)

                def top_ones():
                    return nc.vector.tensor_scalar(out, rk[:, :, 0:n], float(top), None, ALU.is_lt)

                return [compare, before, both, rank, top_ones]

            pairs = sfc[:, :, :].rearrange("p t (g k) -> p t g k", k=GSZ)
            routing = [
                lambda: nc.vector.tensor_scalar(sc[:, :, :], sc[:, :, :], 1.0, None, ALU.add),
                lambda: nc.vector.reciprocal(sc[:, :, :], sc[:, :, :]),
                lambda: nc.vector.tensor_tensor(sfc[:, :, :], sc[:, :, :],
                                                cst[:, K_ESB:K_ESB + E].unsqueeze(1).broadcast_to([P, T, E]), ALU.add),
                lambda: nc.vector.tensor_tensor(gs[:, :, :], pairs[:, :, :, 0], pairs[:, :, :, 1], ALU.add),
                *chosen(gs[:, :, :], NGRP, K_TRG, TOPG, gm[:, :, :]),
                lambda: nc.vector.tensor_tensor(tmp[:, :, :].rearrange("p t (g k) -> p t g k", k=GSZ), pairs,
                                                gm[:, :, :].unsqueeze(3).broadcast_to([P, T, NGRP, GSZ]), ALU.mult),
                *chosen(tmp[:, :, :], E, K_TRI, TOPK, cw[:, :, :]),
                lambda: nc.vector.tensor_tensor(cw[:, :, :], cw[:, :, :], sc[:, :, :], ALU.mult),
                lambda: nc.vector.tensor_reduce(ws[:, :], cw[:, :, :], mybir.AxisListType.X, ALU.add),
                lambda: nc.vector.tensor_scalar(ws[:, :], ws[:, :], 1e-20, 2.0, ALU.add, ALU.mult),
                lambda: nc.vector.reciprocal(wr[:, :], ws[:, :]),
                lambda: nc.vector.tensor_tensor(cw[:, :, :], cw[:, :, :], wr[:, :].unsqueeze(2).broadcast_to([P, T, E]),
                                                ALU.mult)]
            assert len(routing) == RT

            def body(b, feed, prepare, fetch):
                own[0] = 0 if feed else used
                ff, fc = fills(feed, prepare, fetch)
                for s in cross_stages(feed, prepare, fetch):
                    kind, a = s[0], s[1:]
                    if kind == "c_norm":
                        if a[0]:
                            dve.wait_ge(xin_here, 1)
                            norm_guess(xin, stats, mv, var, nt, rstd).then_inc(guess, 1)
                    elif kind == "c_xn":
                        dve.wait_ge(rstd_ready, nth(feed, a[0]))
                        if a[0] and not feed:
                            fc.wait_full(dve, ("c_xt", 0))
                        normalise(xin, mv, rstd).then_inc(xin_read, 1)
                    elif kind == "c_ct":
                        halves_lo(fc, s, ctt, LC, ctt_hi, nth(feed, a[0]))
                    elif kind == "c_xt":
                        halves_lo(fc, s, xnt, L, xnt_hi, nth(feed, a[0]))
                    elif kind == "c_ng":
                        nc.vector.tensor_scalar(neg[:, :, :], mi[:, :, :], -1.0, NEG, ALU.add, ALU.mult)\
                            .then_inc(neg_ready, 1)
                    elif kind == "c_kv":
                        k, = a
                        if k and not feed:
                            dve.wait_ge(kbd_ready, CT)
                            dve.wait_ge(v_ready, 1)
                        fc.wait_full(dve, s)
                        ps = fc.bank(s)
                        for c in range(CT):
                            nc.vector.tensor_scalar(kf[:, c, :], ps[:, c * LC:(c + 1) * LC],
                                                    cst[:, K_XKB + c:K_XKB + c + 1], None, ALU.add)
                        fc.drained(nc.vector.tensor_tensor(vf[0:LC, :], ps[0:LC, CT * LC:CT * LC + C],
                                                           cst[0:LC, K_XVB:K_XVB + C], ALU.add), s)
                        fc.wait_drained(dve, s)
                        dve.sem_inc(kf_ready, 1)
                    elif kind == "c_q":
                        k, f = a
                        dve.wait_ge(q_hi, CT * (nth(feed, k) - 1) + f + 1)
                        nc.vector.tensor_tensor(qx["l"][:, f, :], qf[:, f, :], qx["h"][:, f, :].bitcast(F), ALU.subtract)\
                            .then_inc(qx_ready, 1)
                    elif kind == "c_l":
                        i, t = a
                        if i == 0 and t == 0:
                            dve.wait_ge(neg_ready, 1)
                        fc.wait_full(dve, s)
                        for j in range(HC):
                            h = i * HC + j
                            ins = nc.vector.tensor_tensor_reduce(
                                out=lm[:, t, h, :], in0=fc.bank(s)[:, j * LC:(j + 1) * LC], in1=neg[:, t, :],
                                scale=1.0, scalar=LOWEST, op0=ALU.add, op1=ALU.max, accum_out=mx[:, t, h:h + 1])
                        fc.drained(ins, s)
                    elif kind == "c_lx":
                        i, t = a
                        fc.wait_drained(dve, ("c_l", i, t))
                        heads = slice(i * HC, (i + 1) * HC)
                        nc.vector.tensor_scalar(nmx[:, t, heads], mx[:, t, heads], -1.0, None, ALU.mult).then_inc(nmx_ready, 1)
                    elif kind == "c_r":
                        i, t = a
                        dve.wait_ge(exp_done, i * T + t + 1)
                        heads = slice(i * HC, (i + 1) * HC)
                        nc.vector.reciprocal(rs[:, t, heads], sm[:, t, heads]).then_inc(rs_ready, 1)
                    elif kind == "c_m":
                        finish(dve, nc.vector, link, *a)
                    elif kind == "c_ol":
                        f, = a
                        s = ("c_o", f)
                        dve.wait_ge(ox_hi, f + 1)
                        fc.drained(nc.vector.tensor_tensor(ox["l"][:, f, :], fc.bank(s)[:, 0:L],
                                                           ox["h"][:, f, :].bitcast(F), ALU.subtract), s)
                    elif kind == "c_w":
                        fc.wait_full(dve, s)
                        dve.wait_ge(xb_ready, 1)
                        if feed:
                            dve.wait_ge(x2c_ready, 1)
                        fc.drained(nc.vector.tensor_tensor(x2n[:, :, :], fc.bank(s)[:, :].rearrange("p (t n) -> p t n", t=T),
                                                           xb[:, :, :], ALU.add), s)
                    elif kind == "c_n2":
                        fc.wait_drained(dve, ("c_w",))
                        link(norm_guess(x2n, stats2, mv2, var2, nt2, rstd2))
                        for n in range(3):
                            link(nc.vector.scalar_tensor_tensor(nt2[:, :], rstd2[:, :], -0.5, rstd2[:, :], ALU.mult, ALU.mult))
                            link(nc.vector.tensor_tensor(nt2[:, :], nt2[:, :], var2[:, :], ALU.mult))
                            link(nc.vector.scalar_tensor_tensor(rstd2[:, :], nt2[:, :], 1.5, rstd2[:, :], ALU.add, ALU.mult))
                    elif kind == "c_x2":
                        if fetch:
                            fc.wait_full(dve, ("c_xt", 1))
                        normalise(x2n, mv2, rstd2).then_inc(xn_ready, 1)
                    elif kind == "c_x3":
                        halves_lo(fc, s, x2t, L, x2t_hi)
                    elif kind == "f_rt":
                        n, = a
                        if n == 0:
                            ff.wait_drained(dve, ("f_g2",))
                        else:
                            dve.wait_ge(rt_step, n)
                        routing[n]().then_inc(rt_step, 1)
                    elif kind == "f_gu":
                        e, = a
                        dve.wait_ge(sg_ready, e + 1)
                        if e >= 2:
                            ff.wait_drained(dve, ("f_gu", e - 2))
                        nc.vector.scalar_tensor_tensor(gs2[:, e % 2, :], sg[:, e % 2, :], 1.0, ff.bank(s)[:, 0:L],
                                                       ALU.add, ALU.mult).then_inc(gs_ready, 1)
                    elif kind == "f_gv":
                        e, = a
                        gu = ("f_gu", e)
                        dve.wait_ge(gs_ready, e + 1)
                        ff.drained(nc.vector.tensor_tensor(hu[:, e, :], ff.bank(gu)[:, L:2 * L],
                                                           gs2[:, e % 2, :], ALU.mult), gu)
                    elif kind == "f_h":
                        e, = a
                        cb = ("f_cb", e // 2)
                        ff.wait_full(dve, cb)
                        ff.wait_drained(dve, ("f_gu", e))
                        if e >= 4:
                            dve.wait_ge(hr_ready, e - 3)
                        ins = nc.vector.tensor_tensor(hf[:, e % 4, :], ff.bank(cb)[:, (e % 2) * L:(e % 2 + 1) * L],
                                                      hu[:, e, :], ALU.mult)
                        if e % 2:
                            ff.drained(ins, cb)
                        else:
                            ins.then_inc(hf_ready, 1)
                    elif kind == "f_dn":
                        t, = a
                        ff.wait_full(dve, s)
                        if t == 0:
                            dve.wait_ge(last_add, 1)
                            dve.wait_ge(x2c_ready, 1)
                        ff.drained(nc.vector.tensor_tensor(ob[:, t, :], ff.bank(s)[:, 0:C], x2c[:, t, :], ALU.add), s)
            iterations(dve, body)

        @block.tensor
        def _(pe):
            pe.wait_ge(split, 2)
            pe.wait_ge(const_in, 32)
            pe.wait_ge(zeroed, 1)
            pe.wait_ge(ctx_in, 16)

            def project(out, lhs, rhs, tiles):
                n, last = 0, len(PRODUCTS) * tiles - 1
                for c in range(tiles):
                    for a, b in PRODUCTS:
                        ins = nc.tensor.matmul(out, lhs(a, c), rhs(b, c), start=(n == 0), stop=(n == last))
                        n += 1
                return ins

            def weight(o, width, at, n):
                return lambda k, c: w[k][:, o + c * width + at:o + c * width + at + n]

            def turn(fl, s):
                fl.wait_free(pe, s)
                for c in range(CT):
                    for t in range(T):
                        o = c * L + t * P
                        ins = nc.tensor.transpose(fl.bank(s)[:, o:o + P], xn[:, t, c * P:(c + 1) * P], idn[:, :])
                fl.filled(ins, s)

            def body(b, feed, prepare, fetch):
                ff, fc = fills(feed, prepare, fetch)
                for s in cross_stages(feed, prepare, fetch):
                    kind, a = s[0], s[1:]
                    if kind == "c_ct":
                        if a[0]:
                            pe.wait_ge(ctx_here, 1)
                        fc.wait_free(pe, s)
                        for c in range(CT):
                            ins = nc.tensor.transpose(fc.bank(s)[:, c * LC:(c + 1) * LC], cin[0:LC, c * P:(c + 1) * P],
                                                      idn[0:LC, 0:LC])
                        fc.filled(ins, s)
                    elif kind == "c_kv":
                        fc.wait_drained(pe, ("c_ct", a[0]))
                        fc.wait_free(pe, s)
                        for f in range(CT):
                            project(fc.bank(s)[:, f * LC:(f + 1) * LC], weight(O_XK, C, f * P, P),
                                    lambda k, c: ctt[k][:, c, :], CT)
                        fc.filled(project(fc.bank(s)[0:LC, CT * LC:CT * LC + C], lambda k, c: ctt[k][:, c, :],
                                          weight(O_XV, C, 0, C), CT), s)
                    elif kind == "c_xt":
                        pe.wait_ge(xin_read, nth(feed, a[0]))
                        turn(fc, s)
                    elif kind == "c_q":
                        k, f = a
                        fc.wait_drained(pe, ("c_xt", k))
                        fc.wait_free(pe, s)
                        fc.filled(project(fc.bank(s)[:, 0:L], weight(O_XQ, C, f * P, P), lambda k, c: xnt[k][:, c, :], CT), s)
                    elif kind == "c_l":
                        i, t = a
                        f, o = i // 2, (i % 2) * HC
                        if not feed:
                            pe.wait_ge(kbd_ready, CT)
                            pe.wait_ge(qx_ready, CT)
                        fc.wait_free(pe, s)
                        fc.filled(project(fc.bank(s)[:, 0:HC * LC], lambda k, c: qx[k][:, f, t * P:(t + 1) * P],
                                          lambda k, c: kbd[k][:, f, o:o + HC, :].rearrange("p j n -> p (j n)"), 1), s)
                    elif kind == "c_p":
                        i, t = a
                        mine, count = finisher(i, t)
                        pe.wait_ge(pc_ready[mine], count)
                        fc.wait_free(pe, s)
                        for j in range(HC):
                            ins = nc.tensor.transpose(fc.bank(s)[0:LC, j * P:(j + 1) * P], lm[:, t, i * HC + j, :], idn[:, :])
                        fc.filled(ins, s)
                    elif kind == "c_o":
                        f, = a
                        if not feed:
                            pe.wait_ge(v_ready, 1)
                        fc.wait_free(pe, s)
                        for j in range(HPT):
                            if j % HC == 0:
                                for t in range(T):
                                    fc.wait_drained(pe, ("c_p", (f * HPT + j) // HC, t))
                            ins = nc.tensor.matmul(fc.bank(s)[:, 0:L], vpad[0:LC, f, j, :], ptc[0:LC, f * HPT + j, :],
                                                   start=(j == 0), stop=(j == HPT - 1))
                        fc.filled(ins, s)
                    elif kind == "c_w":
                        for f in range(CT):
                            fc.wait_drained(pe, ("c_o", f))
                        fc.wait_free(pe, s)
                        for t in range(T):
                            ins = project(fc.bank(s)[:, t * C:(t + 1) * C], lambda k, c: ox[k][:, c, t * P:(t + 1) * P],
                                          weight(O_XO, C, 0, C), CT)
                        fc.filled(ins, s)
                    elif kind == "c_x3":
                        pe.wait_ge(xn_ready, 1)
                        turn(fc, s)
                    elif kind == "f_gt":
                        ff.filled(project(ff.bank(s)[0:E, 0:L], weight(O_GT, E, 0, E), lambda k, c: x2t[k][:, c, :], CT), s)
                    elif kind == "f_g2":
                        ff.wait_drained(pe, ("f_gt",))
                        for t in range(T):
                            ins = nc.tensor.transpose(ff.bank(s)[:, t * E:(t + 1) * E], gl[:, t * P:(t + 1) * P],
                                                      idn[0:E, 0:E])
                        ff.filled(ins, s)
                    elif kind == "f_gu":
                        e, = a
                        ff.wait_free(pe, s)
                        for n, o in enumerate((O_G, O_U)):
                            ins = project(ff.bank(s)[:, n * L:(n + 1) * L], weight(o, E * I, e * I, I),
                                          lambda k, c: x2t[k][:, c, :], CT)
                        ff.filled(ins, s)
                    elif kind == "f_cb":
                        i, = a
                        pe.wait_ge(rt_step, RT)
                        ff.wait_free(pe, s)
                        for j in range(2):
                            for t in range(T):
                                o, e = j * L + t * P, 2 * i + j
                                ins = nc.tensor.transpose(ff.bank(s)[:, o:o + P], cw[:, t, e:e + 1].broadcast_to([P, P]),
                                                          idn[:, :])
                        ff.filled(ins, s)
                    elif kind == "f_dn":
                        t, = a
                        pe.wait_ge(hr_ready, E)
                        ff.wait_free(pe, s)
                        ff.filled(project(ff.bank(s)[:, 0:C], lambda k, c: hr[k][:, c, t * P:(t + 1) * P],
                                          weight(O_DN, C, 0, C), E), s)
            iterations(pe, body)


def decoder(nc, x, ctxt, gp, mask, w1, k1, rope, w2, k2, ident, out, batches=B):
    x1 = nc.dram_tensor("x1_dram", [batches, L, C], F, kind="Internal").ap()
    with ExitStack() as keep:
        self_attention(nc, keep, x, x1, w1, k1, rope, ident, batches)
        cross_and_feed(nc, keep, x1, ctxt, gp, mask, out, w2, k2, ident, batches)


def tiles(w):
    return w.reshape(-1, P, w.shape[1]).transpose(1, 0, 2).reshape(P, -1)


def everywhere(v):
    return np.broadcast_to(v.reshape(1, -1), (P, v.size))


def packed(i):
    a = {n[8:]: np.asarray(v) for n, v in i.items() if n.startswith("L0_attn_")}
    c = {n[9:]: np.asarray(v) for n, v in i.items() if n.startswith("L0_xattn_")}
    f = {n[7:]: np.asarray(v) for n, v in i.items() if n.startswith("L0_ffn_")}
    groups = []
    for g in range(G):
        q, kv = slice(g * RG * D, (g + 1) * RG * D), slice(g * D, (g + 1) * D)
        groups += [a["Wq"][:, q], a["Wk"][:, kv], a["Wv"][:, kv]]
    w1 = [tiles(np.concatenate([a["Wqi"], a["Wki"], a["Wwi"]], 1)), tiles(np.concatenate(groups, 1)),
          tiles(a["Wvg"]), tiles(a["Wog"]), tiles(a["Wo"])]
    k1 = [everywhere(a["bvg"]), everywhere(a["bi"]), a["bog"].reshape(HT, P).T]
    half = np.arange(0, D, 2, dtype=np.float32) / np.float32(D)
    angle = np.outer(np.arange(L, dtype=np.float32), np.float32(1) / np.float32(10000) ** half).astype(np.float32)
    cos, sin = np.cos(angle), np.sin(angle)
    rope = np.stack([np.concatenate([cos, cos], 1), np.concatenate([-sin, sin], 1)], 1)
    rope = rope.reshape(T, P, 2, D).transpose(1, 0, 2, 3)
    experts = [w.reshape(E * I, C).T for w in (f["gate_proj"], f["up_proj"])]
    w2 = [tiles(c["wq_k"]), tiles(c["wk_k"]), tiles(c["wv_k"]), tiles(c["wo_k"]), tiles(f["gate_weight"].T),
          tiles(experts[0]), tiles(experts[1]), f["down_proj"].transpose(2, 0, 1).reshape(I, E * C)]
    own = (np.arange(P)[:, None] // DX == np.arange(HPT)[None, :]).astype(np.float32)
    k2 = [c["wq_b"].reshape(CT, P).T, c["wk_b"].reshape(CT, P).T, everywhere(c["wv_b"]), everywhere(c["wo_b"]),
          everywhere(f["e_score_correction_bias"]), own, everywhere(np.tril(np.ones((E, E), np.float32), -1)),
          everywhere(np.tril(np.ones((NGRP, NGRP), np.float32), -1))]
    return {"w1": np.concatenate(w1, 1), "k1": np.concatenate(k1, 1), "rope": rope, "w2": np.concatenate(w2, 1),
            "k2": np.concatenate(k2, 1), "ident": np.eye(P, dtype=np.float32)}


def kernel(**inputs):
    import concourse.bacc as bacc
    from concourse.bass_utils import run_bass_kernel_spmd

    arrays = {"x": inputs["x"], "ctx": inputs["ctx_1024"], "gp": inputs["fside_BxSxS2_0"],
              "mask": inputs["mask_BxSxS2_ik1"], **packed(inputs)}
    arrays = {"in_" + n: np.ascontiguousarray(a) for n, a in arrays.items()}
    nc = bacc.Bacc("TRN2", target_bir_lowering=False, num_devices=1)
    t = {n[3:]: nc.dram_tensor(n, list(a.shape), mybir.dt.from_np(a.dtype), kind="ExternalInput").ap()
         for n, a in arrays.items()}
    out = nc.dram_tensor("out_dram", [B, L, C], F, kind="ExternalOutput").ap()
    decoder(nc, t["x"], t["ctx"], t["gp"], t["mask"], t["w1"], t["k1"], t["rope"], t["w2"], t["k2"], t["ident"], out)
    return run_bass_kernel_spmd(nc, [arrays], core_ids=[0]).results[0]["out_dram"]
```
